# Optimizing a Trainium2 kernel written in Bass

```python
import numpy as np
import jax
import jax.numpy as jnp

def _softmax(x, axis=-1):
    return jax.nn.softmax(x, axis=axis)

def _gelu(x):
    return jax.nn.gelu(x, approximate=True)

def _silu(x):
    return jax.nn.silu(x)

def _sigmoid(x):
    return jax.nn.sigmoid(x)

def _layernorm(x, axis=-1, eps=1e-05):
    m = jnp.mean(x, axis=axis, keepdims=True)
    v = jnp.var(x, axis=axis, keepdims=True)
    return (x - m) / jnp.sqrt(v + eps)

def _scatter_add(tgt, idx, src, axis=0):
    return tgt.at[idx].add(src)

def _segment_sum(src, seg, n):
    return jax.ops.segment_sum(src, seg, n)
kernel_name = 'mk_gps_d1_gnn_r8_b340ec'

def setup_inputs(seed: int=0):
    np.random.seed(seed)
    _w = jnp.asarray

    def _rec_inputs():
        import jax
        import jax.numpy as jnp
        _gk = jax.random.key(seed)
        x = -0.0003713 + 1 * jax.random.normal(jax.random.fold_in(_gk, 1), (6250, 256), jnp.float32)
        _s = jax.random.randint(jax.random.fold_in(_gk, 2), (100000,), 0, 6250, jnp.int32)
        _d = jax.random.randint(jax.random.fold_in(_gk, 3), (100000,), 0, 6250, jnp.int32)
        _loop = jnp.arange(6250, dtype=jnp.int32)
        src = jnp.concatenate([_s, _d, _loop])
        dst = jnp.concatenate([_d, _s, _loop])
        _o = jnp.argsort(dst, stable=True)
        src = src[_o]
        dst = dst[_o]
        edge_attr_3 = -1.09012e-05 + 0.99985 * jax.random.normal(jax.random.fold_in(_gk, 11), (206250, 3), jnp.float32)
        return (x, src, dst, edge_attr_3)
    x, src, dst, edge_attr_3 = _rec_inputs()

    def _L0_gnn_setup():
        import jax, jax.numpy as jnp
        import numpy as np
        N = 6250
        E = 50000
        IN = 256
        H = 8
        D = 32
        EF = 3
        key = jax.random.key(seed)
        ks = jax.random.split(key, 8)
        x = jax.random.normal(ks[0], (N, IN), dtype=jnp.float32)
        edge_index = jax.random.randint(ks[1], (2, E), 0, N, dtype=jnp.int64)
        edge_attr = jax.random.normal(ks[2], (E, EF), dtype=jnp.float32)
        W = jax.random.normal(ks[3], (H * D, IN), dtype=jnp.float32) * np.float32(np.sqrt(2.0 / (IN + H * D)))
        a_src = jax.random.normal(ks[4], (H, D), dtype=jnp.float32) * np.float32(np.sqrt(2.0 / (H + D)))
        a_dst = jax.random.normal(ks[5], (H, D), dtype=jnp.float32) * np.float32(np.sqrt(2.0 / (H + D)))
        edge_W = jax.random.normal(ks[6], (H * D, EF), dtype=jnp.float32) * np.float32(np.sqrt(2.0 / (EF + H * D)))
        edge_b = jnp.zeros((H * D,), dtype=jnp.float32)
        bias = jnp.zeros((H * D,), dtype=jnp.float32)
        return {'x': x, 'W': W, 'a_src': a_src, 'a_dst': a_dst, 'edge_W': edge_W, 'edge_b': edge_b, 'bias': bias, 'edge_attr': edge_attr, 'edge_index': edge_index}
    _L0_gnn_all = _L0_gnn_setup()
    _L0_gnn_in = {k: v for k, v in _L0_gnn_all.items() if k in ('W', 'a_src', 'a_dst', 'edge_W', 'edge_b', 'bias')}
    del _L0_gnn_all

    def _L0_mix_setup():
        import jax, jax.numpy as jnp
        import numpy as np
        HEADS = 4
        DIM_HEAD = 32
        key = jax.random.key(seed)
        k1, k2, k3 = jax.random.split(key, 3)
        B, L, D = (16, 1024, 256)
        hidden = HEADS * DIM_HEAD
        x = jax.random.normal(k1, (B, L, D), dtype=jnp.float32)
        W_qkv = jax.random.normal(k2, (D, 3 * hidden), dtype=jnp.float32) * D ** (-0.5)
        W_out = jax.random.normal(k3, (hidden, D), dtype=jnp.float32) * hidden ** (-0.5)
        b_out = jnp.zeros((D,), dtype=jnp.float32)
        return {'x': x, 'W_qkv': W_qkv, 'W_out': W_out, 'b_out': b_out}
    _L0_mix_all = _L0_mix_setup()
    _L0_mix_in = {k: v for k, v in _L0_mix_all.items() if k in ('W_qkv', 'W_out', 'b_out')}
    del _L0_mix_all

    def _L0_ffn_setup():
        import math
        import jax, jax.numpy as jnp
        import numpy as np
        CAPACITY_FACTOR = 1.25
        TOP_K = 2
        LN_EPS = 1e-05

        def _layer_norm(x, gamma, beta):
            mu = jnp.mean(x, axis=-1, keepdims=True)
            var = jnp.var(x, axis=-1, keepdims=True)
            return (x - mu) * jax.lax.rsqrt(var + LN_EPS) * gamma + beta
        key = jax.random.key(seed)
        ks = jax.random.split(key, 4)
        B, S, D, F, E = (8, 512, 256, 512, 8)
        x = jax.random.normal(ks[0], (B, S, D), dtype=jnp.float32)
        Wr = jax.random.normal(ks[1], (D, E), dtype=jnp.float32) / np.sqrt(D)
        br = jnp.zeros((E,), jnp.float32)
        W1 = jax.random.normal(ks[2], (E, D, F), dtype=jnp.float32) / np.sqrt(D)
        b1 = jnp.zeros((E, F), jnp.float32)
        W2 = jax.random.normal(ks[3], (E, F, D), dtype=jnp.float32) / np.sqrt(F)
        b2 = jnp.zeros((E, D), jnp.float32)
        gamma = jnp.ones((D,), jnp.float32)
        beta = jnp.zeros((D,), jnp.float32)
        return {'x': x, 'Wr': Wr, 'br': br, 'W1': W1, 'b1': b1, 'W2': W2, 'b2': b2, 'gamma': gamma, 'beta': beta}
    _L0_ffn_all = _L0_ffn_setup()
    _L0_ffn_in = {k: v for k, v in _L0_ffn_all.items() if k in ('Wr', 'br', 'W1', 'b1', 'W2', 'b2', 'gamma', 'beta')}
    del _L0_ffn_all
    return {'x': x, 'src': src, 'dst': dst, 'edge_attr_3': edge_attr_3, 'L0_gnn_W': _L0_gnn_in['W'], 'L0_gnn_a_src': _L0_gnn_in['a_src'], 'L0_gnn_a_dst': _L0_gnn_in['a_dst'], 'L0_gnn_edge_W': _L0_gnn_in['edge_W'], 'L0_gnn_edge_b': _L0_gnn_in['edge_b'], 'L0_gnn_bias': _L0_gnn_in['bias'], 'L0_mix_W_qkv': _L0_mix_in['W_qkv'], 'L0_mix_W_out': _L0_mix_in['W_out'], 'L0_mix_b_out': _L0_mix_in['b_out'], 'L0_ffn_Wr': _L0_ffn_in['Wr'], 'L0_ffn_br': _L0_ffn_in['br'], 'L0_ffn_W1': _L0_ffn_in['W1'], 'L0_ffn_b1': _L0_ffn_in['b1'], 'L0_ffn_W2': _L0_ffn_in['W2'], 'L0_ffn_b2': _L0_ffn_in['b2'], 'L0_ffn_gamma': _L0_ffn_in['gamma'], 'L0_ffn_beta': _L0_ffn_in['beta']}

def reference(x, src, dst, edge_attr_3, L0_gnn_W, L0_gnn_a_src, L0_gnn_a_dst, L0_gnn_edge_W, L0_gnn_edge_b, L0_gnn_bias, L0_mix_W_qkv, L0_mix_W_out, L0_mix_b_out, L0_ffn_Wr, L0_ffn_br, L0_ffn_W1, L0_ffn_b1, L0_ffn_W2, L0_ffn_b2, L0_ffn_gamma, L0_ffn_beta):
    import jax
    import jax.numpy as jnp

    def _L0_gnn_ref(x, W, a_src, a_dst, edge_W, edge_b, bias, edge_attr, edge_index):
        import jax, jax.numpy as jnp
        import numpy as np
        N = 6250
        E = 50000
        IN = 256
        H = 8
        D = 32
        EF = 3
        n = x.shape[0]
        h = (x @ W.T).reshape(n, H, D)
        src, dst = (edge_index[0], edge_index[1])
        h_src = h[src]
        h_dst = h[dst]
        alpha = jnp.einsum('ehd,hd->eh', h_src, a_src) + jnp.einsum('ehd,hd->eh', h_dst, a_dst)
        enc = jax.nn.relu(edge_attr @ edge_W.T + edge_b).reshape(-1, H, D)
        alpha = alpha + jnp.sum(enc * h_dst, axis=-1)
        alpha = jnp.where(alpha >= 0, alpha, 0.2 * alpha)
        amax = jax.ops.segment_max(alpha, dst, num_segments=n)
        ex = jnp.exp(alpha - amax[dst])
        denom = jax.ops.segment_sum(ex, dst, num_segments=n)
        attn = ex / jnp.maximum(denom[dst], 1e-10)
        out = jax.ops.segment_sum(h_src * attn[..., None], dst, num_segments=n)
        return out.reshape(n, H * D) + bias

    def _L0_mix_ref(x, W_qkv, W_out, b_out):
        import jax, jax.numpy as jnp
        import numpy as np
        HEADS = 4
        DIM_HEAD = 32
        B, L, D = x.shape
        scale = DIM_HEAD ** (-0.5)
        qkv = jnp.einsum('bld,df->blf', x, W_qkv)
        qkv = qkv.reshape(B, L, 3, HEADS, DIM_HEAD)
        q = jnp.transpose(qkv[:, :, 0], (0, 2, 1, 3)) * scale
        k = jax.nn.softmax(jnp.transpose(qkv[:, :, 1], (0, 2, 1, 3)), axis=2)
        v = jnp.transpose(qkv[:, :, 2], (0, 2, 1, 3))
        context = jnp.einsum('bhld,bhle->bhde', k, v)
        out = jnp.einsum('bhde,bhld->bhle', context, q)
        out = jnp.transpose(out, (0, 2, 1, 3)).reshape(B, L, HEADS * DIM_HEAD)
        return jnp.einsum('blf,fd->bld', out, W_out) + b_out

    def _L0_ffn_ref(x, Wr, br, W1, b1, W2, b2, gamma, beta):
        import math
        import jax, jax.numpy as jnp
        import numpy as np
        CAPACITY_FACTOR = 1.25
        TOP_K = 2
        LN_EPS = 1e-05

        def _layer_norm(x, gamma, beta):
            mu = jnp.mean(x, axis=-1, keepdims=True)
            var = jnp.var(x, axis=-1, keepdims=True)
            return (x - mu) * jax.lax.rsqrt(var + LN_EPS) * gamma + beta
        B, S, D = x.shape
        E = Wr.shape[1]
        N = B * S
        K = TOP_K
        logits = jnp.mean(x, axis=1) @ Wr + br
        routing_weights = jax.nn.softmax(logits, axis=-1)
        capacity = float(math.ceil(N * CAPACITY_FACTOR / E))
        expected_loads = routing_weights.sum(axis=0) * (N / B)
        scale = jnp.where(expected_loads > capacity, capacity / expected_loads, 1.0)
        routing_weights = jax.nn.softmax(routing_weights * scale, axis=-1)
        rw_tok = jnp.broadcast_to(routing_weights[:, None, :], (B, S, E)).reshape(N, E)
        top_w, top_i = jax.lax.top_k(rw_tok, K)
        top_w = jax.nn.softmax(top_w, axis=-1)
        xf = x.reshape(N, D)
        h = jax.nn.gelu(jnp.einsum('nd,edf->enf', xf, W1) + b1[:, None, :], approximate=False)
        y = jnp.einsum('enf,efd->end', h, W2) + b2[:, None, :]
        w_dense = jnp.zeros((N, E), x.dtype).at[jnp.arange(N)[:, None], top_i].add(top_w)
        out = jnp.einsum('ne,end->nd', w_dense, y).reshape(B, S, D)
        out = _layer_norm(out + x, gamma, beta)
        return out
    edge_index = jnp.stack([src, dst])
    xn = _layernorm(x, axis=-1)
    x = x + _L0_gnn_ref(xn, L0_gnn_W, L0_gnn_a_src, L0_gnn_a_dst, L0_gnn_edge_W, L0_gnn_edge_b, L0_gnn_bias, edge_attr_3, edge_index) + _L0_mix_ref(xn[None], L0_mix_W_qkv, L0_mix_W_out, L0_mix_b_out)[0]
    x = x + _L0_ffn_ref(_layernorm(x, axis=-1)[None], L0_ffn_Wr, L0_ffn_br, L0_ffn_W1, L0_ffn_b1, L0_ffn_W2, L0_ffn_b2, L0_ffn_gamma, L0_ffn_beta)[0]
    return x

_drawn_inputs = setup_inputs


def setup_inputs(seed=0):
    import zlib

    import numpy as np

    out = dict(_drawn_inputs(seed))
    spreads = {'L0_gnn_edge_b': (0.0, 0.1),
     'L0_gnn_bias': (0.0, 0.1),
     'L0_mix_b_out': (0.0, 0.1),
     'L0_ffn_br': (0.0, 0.8),
     'L0_ffn_b1': (0.0, 0.382),
     'L0_ffn_b2': (0.0, 0.1),
     'L0_ffn_gamma': (1.0, 0.2),
     'L0_ffn_beta': (0.0, 0.1)}
    factors = {'L0_ffn_Wr': 64.0}
    for name, (base, spread) in spreads.items():
        noise = np.random.default_rng([zlib.crc32(name.encode()), seed]).standard_normal(out[name].shape)
        drawn = base * np.exp(spread * noise) if base else spread * noise
        out[name] = jnp.asarray(drawn.astype(out[name].dtype))
    for name, factor in factors.items():
        out[name] = (out[name] * factor).astype(out[name].dtype)
    return out
```

```python
from contextlib import ExitStack
import math

import concourse.bass as bass
from concourse import mybir

F32 = mybir.dt.float32
BF16 = mybir.dt.bfloat16
I32 = mybir.dt.int32
ALU = mybir.AluOpType
ACT = mybir.ActivationFunctionType
AX = mybir.AxisListType

N, D = 6250, 256
E = 206250
H, DH = 8, 32
T = 125
NT = N // T
ET = E // T
K = 128
KC = D // K
HR = D + 2 * H
SR = D + 2 * H
QK = 128
MD = 32
X8 = 8
FF = 512
FC = FF // K
TOP = 2
CH = 2 * T
NCH = N // CH
LOADS = 10
PER_LOAD = NT // LOADS
EPS = 1e-5
LOW = -3.0e38
CAPACITY = float(math.ceil(N * 1.25 / X8))


def gps_block(nc, x, src, dst, edge_attr_3, L0_gnn_W, L0_gnn_a_src, L0_gnn_a_dst, L0_gnn_edge_W,
              L0_gnn_edge_b, L0_gnn_bias, L0_mix_W_qkv, L0_mix_W_out, L0_mix_b_out, L0_ffn_Wr,
              L0_ffn_br, L0_ffn_W1, L0_ffn_b1, L0_ffn_W2, L0_ffn_b2, L0_ffn_gamma, L0_ffn_beta, out):
    assert N % T == 0 and E % T == 0 and NT % 2 == 0 and NCH % 2 == 1

    node_table = nc.dram_tensor("node_table", (N, HR), F32, kind="Internal").ap()
    state_table = nc.dram_tensor("state_table", (N + T, SR), F32, kind="Internal").ap()

    with ExitStack() as ctx:
        ctx.enter_context(nc.allow_non_contiguous_dma(reason="weights of a few hundred elements"))

        def sb(name, shape, dt=F32):
            return ctx.enter_context(nc.sbuf_tensor(name, shape, dt))

        def sem(name):
            return ctx.enter_context(nc.semaphore(name))

        X = sb("X", [T, NT, D])
        xnT = sb("xnT", [K, KC, N])
        shared = sb("shared", [K, NT * 2 * QK])
        KV = shared[0:T, :].rearrange("p (t f) -> p t f", t=NT)
        taken = 0

        def later(rows, shape, pattern, **sizes):
            nonlocal taken
            size = int(math.prod(shape))
            taken += size
            assert taken <= NT * 2 * QK
            return shared[0:rows, taken - size:taken].rearrange(pattern, **sizes)


        ident = sb("ident", [K, K])
        ones = sb("ones", [K, K])
        Wg = sb("Wg", [K, KC, D])
        a_cols = sb("a_cols", [K, 2, KC])
        a_blocks = sb("a_blocks", [K, KC, 2 * H])
        Wnode = sb("Wnode", [K, KC, HR])
        Wenc = sb("Wenc", [4, D])
        Wqkv = sb("Wqkv", [K, KC, 3 * QK])
        WqT = sb("WqT", [QK, D])
        Wo = sb("Wo", [QK, D])
        Wmix = sb("Wmix", [K, KC, D])
        bias_rows = sb("bias_rows", [1, 2, D])
        bias_row = sb("bias_row", [1, D])
        Wr = sb("Wr", [K, KC, X8])
        br = sb("br", [1, X8])
        gamma = sb("gamma", [T, D])
        beta = sb("beta", [T, D])
        W1 = later(K, [TOP, KC, FF], "p (n k f) -> p n k f", n=TOP, k=KC)
        b1 = sb("b1", [K, TOP, FC])
        W2 = later(K, [TOP, FC, D], "p (n c f) -> p n c f", n=TOP, c=FC)
        b2 = sb("b2", [1, TOP, D])

        stats = sb("stats", [T, PER_LOAD, 6])
        mvs = sb("mvs", [T, PER_LOAD, 2])
        mv = sb("mv", [T, NT, 2])
        rstd = sb("rstd", [T, NT])

        xn = sb("xn", [T, 2, D])
        xnTs = sb("xnTs", [K, 2, KC, T])
        hrow = sb("hrow", [T, 2, HR])
        kmax = sb("kmax", [T, QK])
        kmaxT = sb("kmaxT", [QK, 1])
        nkmax = sb("nkmax", [1, QK])
        nkmaxB = sb("nkmaxB", [T, QK])
        kexp = sb("kexp", [T, 2, QK])
        ksum = sb("ksum", [QK, 1])
        ctxn = sb("ctxn", [QK, QK])
        ctxT = sb("ctxT", [QK, QK])
        ctxWo = sb("ctxWo", [QK, D])
        onescol = sb("onescol", [T, 1])
        zrow = sb("zrow", [1, K])

        init_row = sb("init_row", [T, SR])
        lower = sb("lower", [T, T])
        spare = sb("spare", [T, 1])
        src_i = sb("src_i", [T, 1], I32)
        dst_i = sb("dst_i", [T, 1], I32)
        dst_f = sb("dst_f", [T, 1])
        ea = sb("ea", [T, 4])
        eaT = sb("eaT", [4, T])
        Gs = sb("Gs", [T, HR])
        Gd = sb("Gd", [T, HR])
        S0 = sb("S0", [T, SR])
        same = sb("same", [T, T])
        apart = sb("apart", [T, T])
        prod = sb("prod", [T, D])
        score = sb("score", [T, H])
        score2 = sb("score2", [T, H])
        spread = later(T, [H, T], "p (h e) -> p h e", h=H)
        masked = later(T, [H, T], "p (h e) -> p h e", h=H)
        tmax = sb("tmax", [T, H])
        newmax = sb("newmax", [T, H])
        shifted = sb("shifted", [T, 2 * H])
        ew = sb("ew", [T, 2 * H])
        msg = sb("msg", [T, D + H])
        S1 = sb("S1", [T, SR])
        before = sb("before", [T, T])
        nbefore = sb("nbefore", [T, 1])
        to_f = sb("to_f", [T, 1])
        to_i = sb("to_i", [T, 1], I32)

        st = sb("st", [T, 2, SR])
        den = sb("den", [T, 2, H])
        rden = sb("rden", [T, 2, H])
        agg = later(T, [2, D], "p (b f) -> p b f", b=2)
        ysum = sb("ysum", [K, KC])
        r = {n: sb("r_" + n, [1, X8]) for n in
             ("logits", "exp", "w", "cap", "load", "exp2", "w2", "rank", "first", "second", "num", "tmp")}
        rs = {n: sb("rs_" + n, [1, 1]) for n in
              ("max", "sum", "rsum", "max2", "sum2", "rsum2", "diff", "e", "e1")}
        top = sb("top", [1, TOP])
        topi = sb("topi", [1, TOP])
        topi_i = sb("topi_i", [1, TOP], I32)
        topw = sb("topw", [1, TOP])
        topwB = sb("topwB", [K, TOP])
        pair = sb("pair", [1, X8, X8])
        pair2 = sb("pair2", [1, X8, X8])
        tri8 = sb("tri8", [1, X8, X8])
        hid = later(K, [2, TOP * FC, CH], "p (b j e) -> p b j e", b=2, j=TOP * FC)
        yrow = later(T, [2, D], "p (b f) -> p b f", b=2)
        z = sb("z", [T, 2, D])
        zmv = sb("zmv", [T, 2, 2])
        zsd = sb("zsd", [T, 2])
        zr = sb("zr", [T, 2])
        res = sb("res", [T, 2, D])

        bank = [ctx.enter_context(nc.psum_tensor(f"bank{i}", [K, 512], F32)) for i in range(8)]

        s_xload = [sem(f"s_xload{i}") for i in range(LOADS)]
        s_wload = sem("s_wload")
        s_const = sem("s_const")
        s_setup_pe = sem("s_setup_pe")
        s_setup_ve = sem("s_setup_ve")
        s_stats = sem("s_stats")
        s_mvs = sem("s_mvs")
        s_mv = sem("s_mv")
        s_var = sem("s_var")
        s_sd = sem("s_sd")
        s_rstd = sem("s_rstd")
        s_xn = sem("s_xn")
        s_xnT = sem("s_xnT")
        s_xnTs = sem("s_xnTs")
        s_xnTr = sem("s_xnTr")
        s_rows = sem("s_rows")
        s_hrow = sem("s_hrow")
        s_kv = sem("s_kv")
        s_kmax = sem("s_kmax")
        s_hst = [sem(f"s_hst{i}") for i in range(2)]
        s_km = sem("s_km")
        s_kmp = sem("s_kmp")
        s_kshift = sem("s_kshift")
        s_kexp = sem("s_kexp")
        s_ctx = sem("s_ctx")
        s_fold_v = sem("s_fold_v")
        s_fold_p = sem("s_fold_p")
        s_stage = sem("s_stage")
        s_mix = sem("s_mix")
        s_mixed = sem("s_mixed")
        s_passed = sem("s_passed")
        s_init = sem("s_init")
        s_initst = sem("s_initst")
        g_src, g_dst, g_ea = sem("g_src"), sem("g_dst"), sem("g_ea")
        g_Gs, g_Gd, g_S0 = sem("g_Gs"), sem("g_Gd"), sem("g_S0")
        g = {n: sem("g_" + n) for n in
             ("dstf", "dstT", "eaTp", "same", "eaT", "enc", "prod", "a1", "a2", "a3", "score", "spread",
              "apart", "spreadB", "masked", "tmax", "newmax", "shift", "ew", "msg", "sum", "keep",
              "new", "before", "nbefore", "gap", "sel", "tof", "toi")}
        g_scatter = sem("g_scatter")
        g_done = sem("g_done")
        s_st = [sem(f"s_st{i}") for i in range(2)]
        s_den, s_rden, s_agg = sem("s_den"), sem("s_rden"), sem("s_agg")
        s_x1 = sem("s_x1")
        s_yr = sem("s_yr")
        s_yT = sem("s_yT")
        s_yTr = sem("s_yTr")
        s_ysum = sem("s_ysum")
        s_r, s_rp, s_ra = sem("s_r"), sem("s_rp"), sem("s_ra")
        s_topi = sem("s_topi")
        s_wx = sem("s_wx")
        s_w2s = sem("s_w2s")
        s_l1 = sem("s_l1")
        s_hid = sem("s_hid")
        s_l2 = sem("s_l2")
        s_yrow, s_z = sem("s_yrow"), sem("s_z")
        s_zst, s_zmv, s_zvar, s_zsd, s_zr = (sem(n) for n in ("s_zst", "s_zmv", "s_zvar", "s_zsd", "s_zr"))
        s_n1, s_n2, s_n3, s_res = (sem(n) for n in ("s_n1", "s_n2", "s_n3", "s_res"))
        s_out = [sem(f"s_out{i}") for i in range(2)]

        block = ctx.enter_context(nc.Block())
        WEIGHT_LOADS = 13
        CONSTS = 21

        @block.sync
        def _(sp):
            x_tiles = x.rearrange("(t p) f -> p t f", p=T)
            weight_loads = [
                (Wg[:, :, :], L0_gnn_W.rearrange("(k p) i -> p k i", p=K)),
                (a_cols[:, 0, :], L0_gnn_a_src.rearrange("h d -> (h d)").rearrange("(k p) -> p k", p=K)),
                (a_cols[:, 1, :], L0_gnn_a_dst.rearrange("h d -> (h d)").rearrange("(k p) -> p k", p=K)),
                (Wenc[0:3, :], L0_gnn_edge_W.rearrange("f c -> c f")),
                (Wenc[3:4, :], L0_gnn_edge_b.unsqueeze(0)),
                (Wqkv[:, :, :], L0_mix_W_qkv.rearrange("(k p) f -> p k f", p=K)),
                (Wo[:, :], L0_mix_W_out),
                (bias_rows[:, 0, :], L0_gnn_bias.unsqueeze(0)),
                (bias_rows[:, 1, :], L0_mix_b_out.unsqueeze(0)),
                (Wr[:, :, :], L0_ffn_Wr.rearrange("(k p) e -> p k e", p=K)),
                (br[:, :], L0_ffn_br.unsqueeze(0)),
                (gamma[:, :], L0_ffn_gamma.partition_broadcast(T)),
                (beta[:, :], L0_ffn_beta.partition_broadcast(T)),
            ]
            assert len(weight_loads) == WEIGHT_LOADS
            for i in range(LOADS):
                part = slice(i * PER_LOAD, (i + 1) * PER_LOAD)
                sp.dma_start(X[:, part, :], x_tiles[:, part, :]).then_inc(s_xload[i], 16)
                if i == 0:
                    for dest, source in weight_loads:
                        sp.dma_start(dest, source).then_inc(s_wload, 16)
            sp.wait_ge(s_init, 2)
            sp.dma_start(state_table.rearrange("(t p) c -> p t c", p=T),
                         init_row[:, :].unsqueeze(1).broadcast_to([T, NT + 1, SR])).then_inc(s_initst, 16)
            with sp.Fori(0, NT // 2) as i:
                for par in range(2):
                    t = 2 * i + par
                    sp.wait_ge(s_hrow, t + 3)
                    sp.dma_start(node_table[bass.ds(t * T, T), :], hrow[:, par, :]).then_inc(s_hst[par], 16)
            with sp.Fori(0, ET) as t:
                sp.wait_ge(g_done, t + 1)
                sp.dma_start(src_i[:, :], src[bass.ds(t * T, T)].unsqueeze(1)).then_inc(g_src, 16)
                sp.dma_start(dst_i[:, :], dst[bass.ds(t * T, T)].unsqueeze(1)).then_inc(g_dst, 16)
                sp.dma_start(ea[:, 0:3], edge_attr_3[bass.ds(t * T, T), :]).then_inc(g_ea, 16)
            sp.wait_ge(g_done, ET + 1)
            with sp.Fori(0, NT // 2) as i:
                for par in range(2):
                    t = 2 * i + par
                    sp.wait_ge(s_x1, t + 1)
                    sp.dma_start(st[:, par, :], state_table[bass.ds(t * T, T), :]).then_inc(s_st[par], 16)
            sp.wait_ge(s_topi, 1)
            for n in range(TOP):
                e = sp.value_load(topi_i[0:1, n:n + 1], min_val=0, max_val=X8 - 1)
                sp.dma_start(W1[:, n, :, :], L0_ffn_W1[bass.ds(e, 1), :, :]
                             .rearrange("a (k p) f -> p (a k) f", p=K)).then_inc(s_wx, 16)
                sp.dma_start(b1[:, n, :], L0_ffn_b1[bass.ds(e, 1), :]
                             .rearrange("a (c p) -> p (a c)", p=K)).then_inc(s_wx, 16)
                sp.dma_start(W2[:, n, :, :], L0_ffn_W2[bass.ds(e, 1), :, :]
                             .rearrange("a (c p) f -> p (a c) f", p=K)).then_inc(s_wx, 16)
                sp.dma_start(b2[:, n, :], L0_ffn_b2[bass.ds(e, 1), :]).then_inc(s_wx, 16)
            with sp.Fori(0, NCH) as c:
                for par in range(2):
                    t = 2 * c + par
                    sp.wait_ge(s_res, t + 1)
                    sp.dma_start(out[bass.ds(t * T, T), :], res[:, par, :]).then_inc(s_out[par], 16)
            for par in range(2):
                sp.wait_ge(s_out[par], NCH * 16)

        @block.gpsimd
        def _(po):
            po.sem_inc(s_xnTr, 2)
            po.memset(init_row[:, :], 0.0).then_inc(s_init, 1)
            po.memset(ones[:, :], 1.0).then_inc(s_const, 1)
            po.memset(ident[:, :], 0.0).then_inc(s_const, 1)
            po.memset(lower[:, :], 1.0).then_inc(s_const, 1)
            po.memset(tri8[:, :, :], 1.0).then_inc(s_const, 1)
            po.memset(ea[:, :], 1.0).then_inc(s_const, 1)
            po.memset(onescol[:, :], 1.0).then_inc(s_const, 1)
            po.memset(ctxn[:, :], 0.0).then_inc(s_const, 1)
            po.memset(zrow[:, :], 0.0).then_inc(s_const, 1)
            po.iota(spare[:, :], pattern=[[0, 1]], base=N, channel_multiplier=1,
                    allow_small_or_imprecise_dtypes=True).then_inc(s_const, 1)
            po.iota(r["num"][:, :], pattern=[[1, X8]], base=0, channel_multiplier=0,
                    allow_small_or_imprecise_dtypes=True).then_inc(s_const, 1)
            n = 10
            po.wait_ge(s_init, 1)
            po.memset(init_row[:, D + H:SR], LOW).then_inc(s_init, 1)
            po.wait_ge(s_const, n)
            po.affine_select(out=ident[:, :], in_=ident[:, :], compare_op=ALU.not_equal, fill=1.0,
                             base=0, pattern=[[-1, K]], channel_multiplier=1).then_inc(s_const, 1)
            po.affine_select(out=lower[:, :], in_=lower[:, :], compare_op=ALU.is_gt, fill=0.0,
                             base=0, pattern=[[-1, T]], channel_multiplier=1).then_inc(s_const, 1)
            po.affine_select(out=tri8[:, :, :], in_=tri8[:, :, :], compare_op=ALU.is_gt, fill=0.0,
                             base=0, pattern=[[1, X8], [-1, X8]], channel_multiplier=0).then_inc(s_const, 1)
            po.wait_ge(s_wload, WEIGHT_LOADS * 16)
            for k in range(KC):
                for s in range(2):
                    po.tensor_copy(a_blocks[:, k, s * H:(s + 1) * H],
                                   a_cols[:, s, k:k + 1].broadcast_to([K, H])).then_inc(s_const, 1)
            n += 3 + 4
            po.wait_ge(s_const, n)
            for k in range(KC):
                blk = a_blocks[:, k, :].rearrange("p (s h) -> p s h", s=2)
                po.affine_select(out=blk, in_=blk, compare_op=ALU.is_ge, fill=0.0,
                                 base=K * k, pattern=[[0, 2], [-DH, H]], channel_multiplier=1).then_inc(s_const, 1)
                n += 1
                po.wait_ge(s_const, n)
                po.affine_select(out=blk, in_=blk, compare_op=ALU.is_ge, fill=0.0,
                                 base=DH - 1 - K * k, pattern=[[0, 2], [DH, H]],
                                 channel_multiplier=-1).then_inc(s_const, 1)
                n += 1
            assert n == CONSTS
            with po.Fori(0, NT // 2) as i:
                for par in range(2):
                    t = 2 * i + par
                    po.wait_ge(s_xnTs, t + 3)
                    po.tensor_copy(xnT[:, :, bass.ds(t * T, T)], xnTs[:, par, :, :]).then_inc(s_xnTr, 1)
            po.wait_ge(s_xnTr, NT + 2)
            po.wait_ge(s_rows, NT + 2)
            with po.Fori(0, NT // 2) as i:
                for par in range(2):
                    t = 2 * i + par
                    po.wait_ge(s_mix, t + 1)
                    po.tensor_copy(xnTs[:, par, :, :], xnT[:, :, bass.ds(t * T, T)]).then_inc(s_stage, 1)
            for par in range(2):
                po.wait_ge(s_hst[par], NT // 2 * 16)
            po.wait_ge(s_initst, 16)
            with po.Fori(0, ET) as t:
                po.wait_ge(g_src, 16 * t + 16)
                po.wait_ge(g_dst, 16 * t + 16)
                po.sem_inc(s_passed, 1)
                for rows, table, index, landed in ((Gs, node_table, src_i, g_Gs), (Gd, node_table, dst_i, g_Gd),
                                                   (S0, state_table, dst_i, g_S0)):
                    po.indirect_dma_start(out=rows[:, :], out_offset=None, in_=table,
                                          in_offset=bass.IndirectOffsetOnAxis(ap=index[:, :], axis=0)
                                          ).then_inc(landed, 16)
                po.wait_ge(g["new"], t + 1)
                po.wait_ge(g["newmax"], t + 1)
                po.wait_ge(g["toi"], t + 1)
                po.wait_ge(g_S0, 16 * t + 16)
                po.sem_inc(s_passed, 1)
                po.indirect_dma_start(out=state_table, out_offset=bass.IndirectOffsetOnAxis(ap=to_i[:, :], axis=0),
                                      in_=S1[:, :], in_offset=None).then_inc(g_scatter, 16)

        @block.tensor
        def _(pe):
            for s, credit in ((s_xnT, 2), (s_rows, 2), (s_ctx, 2), (s_mix, 2), (s_yT, 2), (s_l2, 4)):
                pe.sem_inc(s, credit)
            pe.wait_ge(s_const, CONSTS)
            pe.wait_ge(s_wload, WEIGHT_LOADS * 16)
            for ki in range(KC):
                for kh in range(KC):
                    mm = pe.transpose(bank[ki][:, kh * K:(kh + 1) * K], Wg[:, kh, ki * K:(ki + 1) * K], ident[:, :])
                mm.then_inc(s_setup_pe, 1)
            for ki in range(KC):
                for kh in range(KC):
                    mm = pe.matmul(bank[2 + ki][:, 0:2 * H], Wg[:, kh, ki * K:(ki + 1) * K], a_blocks[:, kh, :],
                                   start=(kh == 0), stop=(kh == KC - 1))
                mm.then_inc(s_setup_pe, 1)
            for ki in range(KC):
                mm = pe.transpose(bank[4][:, ki * K:(ki + 1) * K], Wqkv[:, ki, 0:QK], ident[:, :])
            mm.then_inc(s_setup_pe, 1)
            pe.wait_ge(s_setup_ve, 5)

            def turn(t, par):
                pe.wait_ge(s_xn, t + 1)
                pe.wait_ge(s_xnTs, t + 1)
                for k in range(KC):
                    mm = pe.transpose(bank[par][:, k * T:(k + 1) * T], xn[:, par, k * K:(k + 1) * K], ident[0:T, 0:T])
                mm.then_inc(s_xnT, 1)

            def node_rows(t, par):
                pe.wait_ge(s_xnTs, t + 3)
                pe.wait_ge(s_hrow, t + 1)
                pe.wait_ge(s_kmax, t + 1)
                for k in range(KC):
                    pe.matmul(bank[2 + par][0:T, 0:HR], xnTs[:, par, k, :], Wnode[:, k, :],
                              start=(k == 0), stop=(k == KC - 1))
                for k in range(KC):
                    mm = pe.matmul(bank[4 + par][0:T, 0:2 * QK], xnTs[:, par, k, :], Wqkv[:, k, QK:3 * QK],
                                   start=(k == 0), stop=(k == KC - 1))
                mm.then_inc(s_rows, 1)

            turn(0, 0)
            with pe.Fori(0, NT // 2 - 1) as i:
                for par in range(2):
                    turn(2 * i + par + 1, 1 - par)
                    node_rows(2 * i + par, par)
            turn(NT - 1, 1)
            node_rows(NT - 2, 0)
            node_rows(NT - 1, 1)

            pe.wait_ge(s_kmax, NT + 2)
            pe.wait_ge(s_xnTs, NT + 2)
            pe.wait_ge(s_hrow, NT + 2)
            pe.transpose(bank[0][:, 0:T], kmax[:, :], ident[0:T, 0:T]).then_inc(s_kmp, 1)
            pe.wait_ge(s_km, 1)
            pe.transpose(bank[1][0:1, 0:K], kmaxT[:, :], ident[:, :]).then_inc(s_kmp, 1)
            pe.wait_ge(s_km, 2)
            pe.matmul(bank[2][0:T, 0:QK], ones[0:1, 0:T], nkmax[:, :], start=True, stop=True).then_inc(s_kmp, 1)
            pe.matmul(bank[6][:, 0:QK], zrow[:, :], zrow[:, :], start=True, stop=False)
            pe.matmul(bank[7][:, 0:1], zrow[:, :], zrow[:, 0:1], start=True, stop=False)
            with pe.Fori(0, NT // 2) as i:
                for par in range(2):
                    t = 2 * i + par
                    pe.wait_ge(s_kexp, t + 1)
                    pe.matmul(bank[6][:, 0:QK], kexp[:, par, :],
                              KV[:, bass.ds(t, 1), QK:2 * QK].rearrange("p a f -> p (a f)"),
                              start=False, stop=False)
                    pe.matmul(bank[7][:, 0:1], kexp[:, par, :], onescol[:, :],
                              start=False, stop=False).then_inc(s_ctx, 1)
            pe.matmul(bank[6][:, 0:QK], zrow[:, :], zrow[:, :], start=False, stop=True)
            pe.matmul(bank[7][:, 0:1], zrow[:, :], zrow[:, 0:1], start=False, stop=True).then_inc(s_fold_p, 1)
            pe.wait_ge(s_fold_v, 5)
            pe.transpose(bank[4][:, 0:QK], ctxn[:, :], ident[:, :]).then_inc(s_fold_p, 1)
            pe.wait_ge(s_fold_v, 6)
            pe.matmul(bank[5][:, 0:D], ctxT[:, :], Wo[:, :], start=True, stop=True).then_inc(s_fold_p, 1)
            pe.wait_ge(s_fold_v, 7)
            for k in range(KC):
                mm = pe.matmul(bank[2 + k][:, 0:D], WqT[:, k * K:(k + 1) * K], ctxWo[:, :], start=True, stop=True)
            mm.then_inc(s_fold_p, 1)
            pe.wait_ge(s_fold_v, 10)
            with pe.Fori(0, NT // 2) as i:
                for par in range(2):
                    t = 2 * i + par
                    pe.wait_ge(s_stage, t + 1)
                    pe.wait_ge(s_mixed, t + 1)
                    for k in range(KC):
                        pe.matmul(bank[par][0:T, 0:D], xnTs[:, par, k, :], Wmix[:, k, :], start=(k == 0), stop=False)
                    pe.matmul(bank[par][0:T, 0:D], ones[0:1, 0:T], bias_row[:, :],
                              start=False, stop=True).then_inc(s_mix, 1)

            pe.wait_ge(s_mixed, NT + 2)
            with pe.Fori(0, ET) as t:
                pe.wait_ge(g_done, t + 1)
                pe.wait_ge(g["dstf"], t + 1)
                pe.transpose(bank[0][0:T, 0:T], dst_f[:, :].broadcast_to([T, T]), ident[0:T, 0:T]).then_inc(g["dstT"], 1)
                pe.wait_ge(g_ea, 16 * t + 16)
                pe.transpose(bank[1][0:4, 0:T], ea[:, :], ident[0:T, 0:T]).then_inc(g["eaTp"], 1)
                pe.wait_ge(g["eaT"], t + 1)
                pe.matmul(bank[2][0:T, 0:D], eaT[:, :], Wenc[:, :], start=True, stop=True).then_inc(g["enc"], 1)
                pe.wait_ge(g["spread"], t + 1)
                for b in range(2):
                    mm = pe.matmul(bank[3 + b][0:T, 0:4 * T], ones[0:T, 0:T],
                                   spread[:, 4 * b:4 * b + 4, :].rearrange("p h e -> p (h e)"), start=True, stop=True)
                mm.then_inc(g["spreadB"], 1)
                pe.wait_ge(g["msg"], 2 * t + 2)
                pe.wait_ge(g["same"], t + 1)
                pe.matmul(bank[5][0:T, 0:D + H], same[:, :], msg[:, :], start=True, stop=True).then_inc(g["sum"], 1)

            with pe.Fori(0, NT // 2) as i:
                for par in range(2):
                    t = 2 * i + par
                    pe.wait_ge(s_yr, t + 1)
                    pe.wait_ge(s_yTr, t + 1)
                    for k in range(KC):
                        mm = pe.transpose(bank[par][:, k * T:(k + 1) * T], xn[:, par, k * K:(k + 1) * K], ident[0:T, 0:T])
                    mm.then_inc(s_yT, 1)
            pe.wait_ge(s_ysum, 1)
            for k in range(KC):
                mm = pe.matmul(bank[2][0:1, 0:X8], ysum[:, k:k + 1], Wr[:, k, :], start=(k == 0), stop=(k == KC - 1))
            mm.then_inc(s_rp, 1)
            pe.wait_ge(s_w2s, 1)
            pe.matmul(bank[3][:, 0:TOP], ones[0:1, :], topw[:, :], start=True, stop=True).then_inc(s_rp, 1)
            pe.wait_ge(s_w2s, 2)
            pe.wait_ge(s_wx, 8 * 16)
            pe.wait_ge(s_yTr, NT + 2)

            def hidden(c, cp):
                for j in range(TOP * FC):
                    n, f = j // FC, j % FC
                    pe.wait_ge(s_hid, TOP * FC * c + j + 1)
                    for k in range(KC):
                        mm = pe.matmul(bank[j % 4][:, 0:CH], W1[:, n, k, f * K:(f + 1) * K],
                                       xnT[:, k:k + 1, bass.ds(c * CH, CH)].rearrange("p a e -> p (a e)"),
                                       start=(k == 0), stop=(k == KC - 1))
                    mm.then_inc(s_l1, 1)

            def experts(c, cp):
                pe.wait_ge(s_hid, TOP * FC * c + TOP * FC + 4)
                for half in range(2):
                    pe.wait_ge(s_z, 2 * c + half + 1)
                    ps = bank[4 + 2 * cp + half][0:T, 0:D]
                    for j in range(TOP * FC):
                        pe.matmul(ps, hid[:, cp, j, half * T:(half + 1) * T], W2[:, j // FC, j % FC, :],
                                  start=(j == 0), stop=False)
                    pe.matmul(ps, ones[0:1, 0:T], bias_row[:, :], start=False, stop=True).then_inc(s_l2, 1)

            hidden(0, 0)
            pe.wait_ge(s_w2s, 7)
            with pe.Fori(0, NCH // 2) as i:
                for cp in range(2):
                    hidden(2 * i + cp + 1, 1 - cp)
                    experts(2 * i + cp, cp)
            experts(NCH - 1, 0)

        @block.scalar
        def _(ac):
            for s, credit in ((s_xnTs, 2), (s_hrow, 2), (s_yTr, 2), (s_hid, 4)):
                ac.sem_inc(s, credit)
            ac.wait_ge(s_var, 1)
            ac.activation(rstd[:, :], rstd[:, :], ACT.Sqrt).then_inc(s_sd, 1)

            def stage(t, par):
                ac.wait_ge(s_xnT, t + 3)
                ac.wait_ge(s_rows, t + 1)
                ac.wait_ge(s_xnTr, t + 1)
                ac.activation(xnTs[:, par, :, :], bank[par][:, 0:KC * T].rearrange("p (k e) -> p k e", k=KC),
                              ACT.Copy).then_inc(s_xnTs, 1)

            def h_row(t, par, i):
                ac.wait_ge(s_rows, t + 3)
                if i is not None:
                    ac.wait_ge(s_hst[par], 16 * i)
                ac.activation(hrow[:, par, :], bank[2 + par][0:T, 0:HR], ACT.Copy).then_inc(s_hrow, 1)

            stage(0, 0)
            for par in range(2):
                stage(par + 1, 1 - par)
                h_row(par, par, None)
            with ac.Fori(1, NT // 2 - 1) as i:
                for par in range(2):
                    stage(2 * i + par + 1, 1 - par)
                    h_row(2 * i + par, par, i)
            stage(NT - 1, 1)
            h_row(NT - 2, 0, NT // 2 - 1)
            h_row(NT - 1, 1, NT // 2 - 1)
            with ac.Fori(0, NT // 10) as i:
                ac.wait_ge(s_kshift, i + 1)
                for j in range(10):
                    t = 10 * i + j
                    ac.wait_ge(s_ctx, t + 1)
                    ac.activation(kexp[:, j % 2, :], KV[:, bass.ds(t, 1), 0:QK].rearrange("p a f -> p (a f)"),
                                  ACT.Exp).then_inc(s_kexp, 1)
            with ac.Fori(0, ET) as t:
                ac.wait_ge(g["shift"], 2 * t + 2)
                ac.activation(ew[:, :], shifted[:, :], ACT.Exp).then_inc(g["ew"], 1)
            ac.wait_ge(s_var, 2)
            ac.activation(rstd[:, :], rstd[:, :], ACT.Sqrt).then_inc(s_sd, 1)
            with ac.Fori(0, NT // 2) as i:
                for par in range(2):
                    t = 2 * i + par
                    ac.wait_ge(s_yT, t + 3)
                    ac.activation(xnT[:, :, bass.ds(t * T, T)],
                                  bank[par][:, 0:KC * T].rearrange("p (k e) -> p k e", k=KC),
                                  ACT.Copy).then_inc(s_yTr, 1)
            for n, (a, b) in enumerate((("logits", "exp"), ("tmp", "exp2"))):
                ac.wait_ge(s_ra, 2 * n + 1)
                ac.activation(r[b][:, :], r[a][:, :], ACT.Exp).then_inc(s_ra, 1)
            ac.wait_ge(s_ra, 5)
            ac.activation(rs["e"][:, :], rs["diff"][:, :], ACT.Exp).then_inc(s_ra, 1)
            ac.wait_ge(s_wx, 8 * 16)

            def gelus(c, cp):
                ac.wait_ge(s_l2, 2 * c + 2)
                for j in range(TOP * FC):
                    ac.wait_ge(s_l1, TOP * FC * c + j + 1)
                    ac.activation(hid[:, cp, j, :], bank[j % 4][:, 0:CH], ACT.Gelu,
                                  bias=b1[:, j // FC, j % FC:j % FC + 1]).then_inc(s_hid, 1)

            def roots(c):
                ac.wait_ge(s_zvar, c + 1)
                ac.activation(zsd[:, :], zsd[:, :], ACT.Sqrt).then_inc(s_zsd, 1)

            gelus(0, 0)
            with ac.Fori(0, NCH // 2) as i:
                for cp in range(2):
                    gelus(2 * i + cp + 1, 1 - cp)
                    roots(2 * i + cp)
            roots(NCH - 1)

        @block.vector
        def _(ve):
            ve.memset(kmax[:, :], LOW).then_inc(s_kmax, 2)
            for s, credit in ((s_mixed, 2), (s_x1, 2), (s_z, 4), (g_done, 1)):
                ve.sem_inc(s, credit)

            def part_stats(part, n):
                ve.wait_ge(s_mv, n)
                ve.sem_inc(s_passed, 1)
                for j in range(PER_LOAD):
                    ve.bn_stats(stats[:, j, :], X[:, bass.ds(PER_LOAD * part + j, 1), :]
                                .rearrange("p a f -> p (a f)")).then_inc(s_stats, 1)
                ve.wait_ge(s_stats, PER_LOAD * (n + 1))
                ve.sem_inc(s_passed, 1)
                for j in range(PER_LOAD):
                    ve.bn_aggr(mvs[:, j, :], stats[:, j, :]).then_inc(s_mvs, 1)
                ve.wait_ge(s_mvs, PER_LOAD * (n + 1))
                ve.tensor_copy(mv[:, bass.ds(PER_LOAD * part, PER_LOAD), :], mvs[:, :, :]).then_inc(s_mv, 1)

            def rsqrt_all(n):
                ve.wait_ge(s_mv, LOADS * (n + 1))
                ve.tensor_scalar(rstd[:, :], mv[:, :, 1:2].rearrange("p t a -> p (t a)"), EPS, None,
                                 ALU.add).then_inc(s_var, 1)
                ve.wait_ge(s_sd, n + 1)
                ve.reciprocal(rstd[:, :], rstd[:, :]).then_inc(s_rstd, 1)
                ve.wait_ge(s_rstd, n + 1)

            def normalise(out, t):
                return ve.tensor_scalar(out, X[:, bass.ds(t, 1), :].rearrange("p a f -> p (a f)"),
                                        mv[:, bass.ds(t, 1), 0:1].rearrange("p a f -> p (a f)"),
                                        rstd[:, bass.ds(t, 1)], ALU.subtract, ALU.mult)

            for part in range(LOADS):
                ve.wait_ge(s_xload[part], 16)
                part_stats(part, part)
            rsqrt_all(0)
            for ki in range(KC):
                ve.wait_ge(s_setup_pe, ki + 1)
                ve.tensor_copy(Wnode[:, ki, 0:D], bank[ki][:, 0:D]).then_inc(s_setup_ve, 1)
            for ki in range(KC):
                ve.wait_ge(s_setup_pe, KC + ki + 1)
                ve.tensor_copy(Wnode[:, ki, D:HR], bank[2 + ki][:, 0:2 * H]).then_inc(s_setup_ve, 1)
            ve.wait_ge(s_setup_pe, 2 * KC + 1)
            ve.tensor_copy(WqT[:, :], bank[4][:, 0:D]).then_inc(s_setup_ve, 1)

            def normal_tile(t, par):
                ve.wait_ge(s_xnT, t + 1)
                normalise(xn[:, par, :], t).then_inc(s_xn, 1)

            def kv_rows(t, par):
                ve.wait_ge(s_rows, t + 3)
                ve.tensor_copy(KV[:, bass.ds(t, 1), :].rearrange("p a f -> p (a f)"),
                               bank[4 + par][0:T, 0:2 * QK]).then_inc(s_kv, 1)
                ve.wait_ge(s_kmax, t + 2)
                ve.tensor_tensor(kmax[:, :], kmax[:, :], bank[4 + par][0:T, 0:QK], ALU.max).then_inc(s_kmax, 1)

            normal_tile(0, 0)
            with ve.Fori(0, NT // 2 - 1) as i:
                for par in range(2):
                    normal_tile(2 * i + par + 1, 1 - par)
                    kv_rows(2 * i + par, par)
            normal_tile(NT - 1, 1)
            kv_rows(NT - 2, 0)
            kv_rows(NT - 1, 1)

            ve.wait_ge(s_kmp, 1)
            ve.tensor_reduce(kmaxT[:, :], bank[0][:, 0:T], AX.X, ALU.max).then_inc(s_km, 1)
            ve.wait_ge(s_kmp, 2)
            ve.tensor_scalar(nkmax[:, :], bank[1][0:1, 0:K], -1.0, None, ALU.mult).then_inc(s_km, 1)
            ve.wait_ge(s_kmp, 3)
            ve.tensor_copy(nkmaxB[:, :], bank[2][0:T, 0:QK]).then_inc(s_km, 1)
            ve.wait_ge(s_km, 3)
            ve.wait_ge(s_kv, NT)
            with ve.Fori(0, NT // 10) as i:
                part = KV[:, bass.ds(10 * i, 10), 0:QK]
                ve.tensor_tensor(part, part, nkmaxB[:, :].unsqueeze(1).broadcast_to([T, 10, QK]),
                                 ALU.add).then_inc(s_kshift, 1)
            ve.wait_ge(s_fold_p, 1)
            ve.reciprocal(ksum[:, :], bank[7][:, 0:1]).then_inc(s_fold_v, 1)
            ve.wait_ge(s_fold_v, 1)
            for a in range(QK // MD):
                q = slice(a * MD, (a + 1) * MD)
                ve.tensor_scalar(ctxn[q, q], bank[6][q, q], ksum[q, :], MD ** -0.5,
                                 ALU.mult, ALU.mult).then_inc(s_fold_v, 1)
            ve.wait_ge(s_fold_p, 2)
            ve.tensor_copy(ctxT[:, :], bank[4][:, 0:QK]).then_inc(s_fold_v, 1)
            ve.wait_ge(s_fold_p, 3)
            ve.tensor_copy(ctxWo[:, :], bank[5][:, 0:D]).then_inc(s_fold_v, 1)
            ve.wait_ge(s_fold_p, 4)
            for k in range(KC):
                ve.tensor_copy(Wmix[:, k, :], bank[2 + k][:, 0:D]).then_inc(s_fold_v, 1)
            ve.tensor_tensor(bias_row[:, :], bias_rows[:, 0, :], bias_rows[:, 1, :], ALU.add).then_inc(s_fold_v, 1)
            with ve.Fori(0, NT // 2) as i:
                for par in range(2):
                    t = 2 * i + par
                    ve.wait_ge(s_mix, t + 3)
                    tile = X[:, bass.ds(t, 1), :].rearrange("p a f -> p (a f)")
                    ve.tensor_tensor(tile, tile, bank[par][0:T, 0:D], ALU.add).then_inc(s_mixed, 1)

            with ve.Fori(0, ET) as t:
                ve.wait_ge(g_dst, 16 * t + 16)
                ve.tensor_copy(dst_f[:, :], dst_i[:, :]).then_inc(g["dstf"], 1)
                ve.wait_ge(g["dstT"], t + 1)
                ve.wait_ge(g["dstf"], t + 1)
                ve.tensor_scalar(same[:, :], bank[0][0:T, 0:T], dst_f[:, :], None, ALU.is_equal).then_inc(g["same"], 1)
                ve.wait_ge(g["eaTp"], t + 1)
                ve.tensor_copy(eaT[:, :], bank[1][0:4, 0:T]).then_inc(g["eaT"], 1)
                ve.wait_ge(g["same"], t + 1)
                ve.tensor_scalar(apart[:, :], same[:, :], 1.0, -LOW, ALU.subtract, ALU.mult).then_inc(g["apart"], 1)
                ve.tensor_tensor(before[:, :], same[:, :], lower[:, :], ALU.mult).then_inc(g["before"], 1)
                ve.wait_ge(g["before"], t + 1)
                ve.tensor_reduce(nbefore[:, :], before[:, :], AX.X, ALU.max).then_inc(g["nbefore"], 1)
                ve.tensor_tensor(to_f[:, :], spare[:, :], dst_f[:, :], ALU.subtract).then_inc(g["gap"], 1)
                ve.wait_ge(g["gap"], t + 1)
                ve.wait_ge(g["nbefore"], t + 1)
                ve.tensor_tensor(to_f[:, :], to_f[:, :], nbefore[:, :], ALU.mult).then_inc(g["sel"], 1)
                ve.wait_ge(g["sel"], t + 1)
                ve.tensor_tensor(to_f[:, :], to_f[:, :], dst_f[:, :], ALU.add).then_inc(g["tof"], 1)
                ve.wait_ge(g["tof"], t + 1)
                ve.tensor_copy(to_i[:, :], to_f[:, :]).then_inc(g["toi"], 1)
                ve.wait_ge(g["enc"], t + 1)
                ve.wait_ge(g_Gs, 16 * t + 16)
                ve.wait_ge(g_Gd, 16 * t + 16)
                ve.wait_ge(g_S0, 16 * t + 16)
                ve.scalar_tensor_tensor(out=prod[:, :], in0=bank[2][0:T, 0:D], scalar=0.0, in1=Gd[:, 0:D],
                                        op0=ALU.max, op1=ALU.mult).then_inc(g["prod"], 1)
                ve.wait_ge(g["prod"], t + 1)
                ve.tensor_reduce(score[:, :], prod[:, :].rearrange("p (h d) -> p h d", h=H), AX.X,
                                 ALU.add).then_inc(g["a1"], 1)
                ve.wait_ge(g["a1"], t + 1)
                ve.tensor_tensor(score[:, :], score[:, :], Gs[:, D:D + H], ALU.add).then_inc(g["a2"], 1)
                ve.wait_ge(g["a2"], t + 1)
                ve.tensor_tensor(score[:, :], score[:, :], Gd[:, D + H:HR], ALU.add).then_inc(g["a3"], 1)
                ve.wait_ge(g["a3"], t + 1)
                ve.scalar_tensor_tensor(out=score2[:, :], in0=score[:, :], scalar=0.2, in1=score[:, :],
                                        op0=ALU.mult, op1=ALU.max).then_inc(g["score"], 1)
                ve.wait_ge(g["score"], t + 1)
                ve.tensor_tensor(spread[:, :, :], score2[:, :].unsqueeze(2).broadcast_to([T, H, T]),
                                 ident[0:T, 0:T].unsqueeze(1).broadcast_to([T, H, T]), ALU.mult).then_inc(g["spread"], 1)
                ve.wait_ge(g["spreadB"], t + 1)
                ve.wait_ge(g["apart"], t + 1)
                for b in range(2):
                    ve.tensor_tensor(masked[:, 4 * b:4 * b + 4, :],
                                     bank[3 + b][0:T, 0:4 * T].rearrange("p (h e) -> p h e", h=4),
                                     apart[:, :].unsqueeze(1).broadcast_to([T, 4, T]), ALU.add).then_inc(g["masked"], 1)
                ve.wait_ge(g["masked"], 2 * t + 2)
                ve.tensor_reduce(tmax[:, :], masked[:, :, :], AX.X, ALU.max).then_inc(g["tmax"], 1)
                ve.wait_ge(g["tmax"], t + 1)
                ve.tensor_tensor(S1[:, D + H:SR], tmax[:, :], S0[:, D + H:SR], ALU.max).then_inc(g["newmax"], 1)
                ve.wait_ge(g["newmax"], t + 1)
                ve.tensor_tensor(shifted[:, 0:H], score2[:, :], S1[:, D + H:SR], ALU.subtract).then_inc(g["shift"], 1)
                ve.tensor_tensor(shifted[:, H:2 * H], S0[:, D + H:SR], S1[:, D + H:SR], ALU.subtract).then_inc(g["shift"], 1)
                ve.wait_ge(g["ew"], t + 1)
                ve.tensor_tensor(msg[:, 0:D].rearrange("p (h d) -> p h d", h=H),
                                 Gs[:, 0:D].rearrange("p (h d) -> p h d", h=H),
                                 ew[:, 0:H].unsqueeze(2).broadcast_to([T, H, DH]), ALU.mult).then_inc(g["msg"], 1)
                ve.tensor_copy(msg[:, D:D + H], ew[:, 0:H]).then_inc(g["msg"], 1)
                ve.tensor_tensor(S1[:, 0:D].rearrange("p (h d) -> p h d", h=H),
                                 S0[:, 0:D].rearrange("p (h d) -> p h d", h=H),
                                 ew[:, H:2 * H].unsqueeze(2).broadcast_to([T, H, DH]), ALU.mult).then_inc(g["keep"], 1)
                ve.tensor_tensor(S1[:, D:D + H], S0[:, D:D + H], ew[:, H:2 * H], ALU.mult).then_inc(g["keep"], 1)
                ve.wait_ge(g["keep"], 2 * t + 2)
                ve.wait_ge(g["sum"], t + 1)
                ve.tensor_tensor(S1[:, 0:D + H], S1[:, 0:D + H], bank[5][0:T, 0:D + H], ALU.add).then_inc(g["new"], 1)
                ve.wait_ge(g_scatter, 16 * t + 16)
                ve.sem_inc(g_done, 1)

            with ve.Fori(0, NT // 2) as i:
                for par in range(2):
                    t = 2 * i + par
                    ve.wait_ge(s_st[par], 16 * i + 16)
                    ve.tensor_scalar(den[:, par, :], st[:, par, D:D + H], 1e-10, None, ALU.max).then_inc(s_den, 1)
                    ve.wait_ge(s_den, t + 1)
                    ve.reciprocal(rden[:, par, :], den[:, par, :]).then_inc(s_rden, 1)
                    ve.wait_ge(s_rden, t + 1)
                    ve.tensor_tensor(agg[:, par, :].rearrange("p (h d) -> p h d", h=H),
                                     st[:, par, 0:D].rearrange("p (h d) -> p h d", h=H),
                                     rden[:, par, :].unsqueeze(2).broadcast_to([T, H, DH]), ALU.mult).then_inc(s_agg, 1)
                    ve.wait_ge(s_agg, t + 1)
                    tile = X[:, bass.ds(t, 1), :].rearrange("p a f -> p (a f)")
                    ve.tensor_tensor(tile, tile, agg[:, par, :], ALU.add).then_inc(s_x1, 1)
            ve.wait_ge(s_x1, NT + 2)
            with ve.Fori(0, LOADS) as i:
                part_stats(i, LOADS + i)
            rsqrt_all(1)
            with ve.Fori(0, NT // 2) as i:
                for par in range(2):
                    t = 2 * i + par
                    ve.wait_ge(s_yT, t + 1)
                    normalise(xn[:, par, :], t).then_inc(s_yr, 1)
            ve.wait_ge(s_yTr, NT + 2)
            ve.tensor_reduce(ysum[:, :], xnT[:, :, :], AX.X, ALU.add).then_inc(s_ysum, 1)

            steps = 0

            def done(ins):
                nonlocal steps
                ins.then_inc(s_r, 1)
                steps += 1
                ve.wait_ge(s_r, steps)

            def softmax(a, top_, shifted_, e, total, rtotal, w, turn_):
                done(ve.tensor_reduce(top_[:, :], a[:, :], AX.X, ALU.max))
                ve.tensor_scalar(shifted_[:, :], a[:, :], top_[:, :], None, ALU.subtract).then_inc(s_ra, 1)
                ve.wait_ge(s_ra, turn_)
                done(ve.tensor_reduce(total[:, :], e[:, :], AX.X, ALU.add))
                done(ve.reciprocal(rtotal[:, :], total[:, :]))
                done(ve.tensor_scalar(w[:, :], e[:, :], rtotal[:, :], None, ALU.mult))

            ve.wait_ge(s_rp, 1)
            done(ve.scalar_tensor_tensor(out=r["tmp"][:, :], in0=bank[2][0:1, 0:X8], scalar=1.0 / N, in1=br[:, :],
                                         op0=ALU.mult, op1=ALU.add))
            softmax(r["tmp"], rs["max"], r["logits"], r["exp"], rs["sum"], rs["rsum"], r["w"], 2)
            done(ve.tensor_scalar(r["load"][:, :], r["w"][:, :], float(N), None, ALU.mult))
            done(ve.reciprocal(r["cap"][:, :], r["load"][:, :]))
            done(ve.tensor_scalar(r["cap"][:, :], r["cap"][:, :], CAPACITY, 1.0, ALU.mult, ALU.min))
            done(ve.tensor_tensor(r["load"][:, :], r["w"][:, :], r["cap"][:, :], ALU.mult))
            softmax(r["load"], rs["max2"], r["tmp"], r["exp2"], rs["sum2"], rs["rsum2"], r["w2"], 4)
            w_i = r["w2"][:, :].unsqueeze(2).broadcast_to([1, X8, X8])
            w_j = r["w2"][:, :].unsqueeze(1).broadcast_to([1, X8, X8])
            done(ve.tensor_tensor(pair[:, :, :], w_j, w_i, ALU.is_equal))
            done(ve.tensor_tensor(pair[:, :, :], pair[:, :, :], tri8[:, :, :], ALU.mult))
            done(ve.tensor_tensor(pair2[:, :, :], w_j, w_i, ALU.is_gt))
            done(ve.tensor_tensor(pair[:, :, :], pair[:, :, :], pair2[:, :, :], ALU.add))
            done(ve.tensor_reduce(r["rank"][:, :], pair[:, :, :], AX.X, ALU.add))
            for n in range(TOP):
                done(ve.tensor_scalar(r["first"][:, :], r["rank"][:, :], float(n), None, ALU.is_equal))
                done(ve.tensor_tensor(r["second"][:, :], r["first"][:, :], r["num"][:, :], ALU.mult))
                done(ve.tensor_reduce(topi[:, n:n + 1], r["second"][:, :], AX.X, ALU.add))
                done(ve.tensor_tensor(r["second"][:, :], r["first"][:, :], r["w2"][:, :], ALU.mult))
                done(ve.tensor_reduce(top[:, n:n + 1], r["second"][:, :], AX.X, ALU.add))
            ve.tensor_copy(topi_i[:, :], topi[:, :]).then_inc(s_topi, 1)
            ve.tensor_tensor(rs["diff"][:, :], top[:, 1:2], top[:, 0:1], ALU.subtract).then_inc(s_ra, 1)
            ve.wait_ge(s_ra, 6)
            done(ve.tensor_scalar(rs["e1"][:, :], rs["e"][:, :], 1.0, None, ALU.add))
            done(ve.reciprocal(topw[:, 0:1], rs["e1"][:, :]))
            ve.tensor_tensor(topw[:, 1:2], topw[:, 0:1], rs["e"][:, :], ALU.mult).then_inc(s_w2s, 1)
            ve.wait_ge(s_rp, 2)
            ve.tensor_copy(topwB[:, :], bank[3][:, 0:TOP]).then_inc(s_w2s, 1)
            ve.wait_ge(s_w2s, 2)
            ve.wait_ge(s_wx, 8 * 16)
            for n in range(TOP):
                ve.tensor_scalar(W2[:, n, :, :], W2[:, n, :, :], topwB[:, n:n + 1], None, ALU.mult).then_inc(s_w2s, 1)
                ve.tensor_scalar(b2[:, n, :], b2[:, n, :], topw[:, n:n + 1], None, ALU.mult).then_inc(s_w2s, 1)
            ve.wait_ge(s_w2s, 6)
            ve.tensor_tensor(bias_row[:, :], b2[:, 0, :], b2[:, 1, :], ALU.add).then_inc(s_w2s, 1)

            def outputs(c, cp, first=False):
                for half in range(2):
                    t = 2 * c + half
                    ve.wait_ge(s_l2, t + 5)
                    normalise(yrow[:, half, :], t).then_inc(s_yrow, 1)
                    ve.wait_ge(s_yrow, t + 1)
                    ve.tensor_tensor(z[:, half, :], yrow[:, half, :], bank[4 + 2 * cp + half][0:T, 0:D],
                                     ALU.add).then_inc(s_z, 1)
                    ve.wait_ge(s_z, t + 5)
                    ve.sem_inc(s_passed, 1)
                    ve.bn_stats(stats[:, half, :], z[:, half, :]).then_inc(s_zst, 1)
                    ve.wait_ge(s_zst, t + 1)
                    ve.sem_inc(s_passed, 1)
                    ve.bn_aggr(zmv[:, half, :], stats[:, half, :]).then_inc(s_zmv, 1)
                ve.wait_ge(s_zmv, 2 * c + 2)
                ve.tensor_scalar(zsd[:, :], zmv[:, :, 1:2].rearrange("p t a -> p (t a)"), EPS, None,
                                 ALU.add).then_inc(s_zvar, 1)
                ve.wait_ge(s_zsd, c + 1)
                ve.reciprocal(zr[:, :], zsd[:, :]).then_inc(s_zr, 1)
                ve.wait_ge(s_zr, c + 1)
                for half in range(2):
                    t = 2 * c + half
                    if not first:
                        ve.wait_ge(s_out[half], 16 * c)
                    ve.tensor_scalar(res[:, half, :], z[:, half, :], zmv[:, half, 0:1], zr[:, half:half + 1],
                                     ALU.subtract, ALU.mult).then_inc(s_n1, 1)
                    ve.wait_ge(s_n1, t + 1)
                    ve.tensor_tensor(res[:, half, :], res[:, half, :], gamma[:, :], ALU.mult).then_inc(s_n2, 1)
                    ve.wait_ge(s_n2, t + 1)
                    ve.tensor_tensor(res[:, half, :], res[:, half, :], beta[:, :], ALU.add).then_inc(s_n3, 1)
                    ve.wait_ge(s_n3, t + 1)
                    ve.tensor_tensor(res[:, half, :], res[:, half, :],
                                     X[:, bass.ds(t, 1), :].rearrange("p a f -> p (a f)"), ALU.add).then_inc(s_res, 1)

            outputs(0, 0, first=True)
            with ve.Fori(0, NCH // 2) as i:
                for cp in range(2):
                    outputs(2 * i + cp + 1, 1 - cp)


_INS = ["x", "src", "dst", "edge_attr_3", "L0_gnn_W", "L0_gnn_a_src", "L0_gnn_a_dst", "L0_gnn_edge_W",
        "L0_gnn_edge_b", "L0_gnn_bias", "L0_mix_W_qkv", "L0_mix_W_out", "L0_mix_b_out", "L0_ffn_Wr",
        "L0_ffn_br", "L0_ffn_W1", "L0_ffn_b1", "L0_ffn_W2", "L0_ffn_b2", "L0_ffn_gamma", "L0_ffn_beta"]


def kernel(**inputs):
    import numpy as _np
    import concourse.bacc as _bacc
    from concourse.bass_utils import run_bass_kernel_spmd as _run

    nc = _bacc.Bacc("TRN2", target_bir_lowering=False, num_devices=1)
    arrays, args = {}, []
    for name in _INS:
        a = _np.ascontiguousarray(inputs[name])
        arrays[f"in_{name}"] = a
        args.append(nc.dram_tensor(f"in_{name}", a.shape, mybir.dt.from_np(a.dtype), kind="ExternalInput").ap())
    out = nc.dram_tensor("out_0", (N, D), F32, kind="ExternalOutput").ap()
    gps_block(nc, *args, out)
    r = _run(nc, [arrays], core_ids=[0])
    return r.results[0]["out_0"]
```

```python
from contextlib import ExitStack
import math

import concourse.bass as bass
from concourse import mybir

F32 = mybir.dt.float32
BF16 = mybir.dt.bfloat16
I32 = mybir.dt.int32
ALU = mybir.AluOpType
ACT = mybir.ActivationFunctionType
AX = mybir.AxisListType

N, D = 6250, 256
E = 206250
H, DH = 8, 32
T = 125
NT = N // T
ET = E // T
K = 128
KC = D // K
HB = DH + 1
HD = H * HB
HR = HD + H
SR = HD + H
J = 15
GE = J * T
G = E // GE
W = 128
BT = 3
BN = J // BT
VT = 5
VN = J // VT
EQ = 4
EB = (J + EQ - 1) // EQ
EK = 32
NP = 3
QK = 128
MD = 32
X8 = 8
FF = 512
FC = FF // K
TOP = 2
CH = 2 * T
NCH = N // CH
LOADS = 10
PER_LOAD = NT // LOADS
EPS = 1e-5
LOW = -3.0e38
CAPACITY = float(math.ceil(N * 1.25 / X8))


def gps_block(nc, x, src, dst, edge_attr_3, L0_gnn_W, L0_gnn_a_src, L0_gnn_a_dst, L0_gnn_edge_W,
              L0_gnn_edge_b, L0_gnn_bias, L0_mix_W_qkv, L0_mix_W_out, L0_mix_b_out, L0_ffn_Wr,
              L0_ffn_br, L0_ffn_W1, L0_ffn_b1, L0_ffn_W2, L0_ffn_b2, L0_ffn_gamma, L0_ffn_beta, out):
    assert N % T == 0 and E % GE == 0 and NT % 2 == 0 and NCH % 2 == 1 and G % 2 == 0 and W <= 2 * T

    node_table = nc.dram_tensor("node_table", (N, HR), F32, kind="Internal").ap()
    state_table = nc.dram_tensor("state_table", (N + 2 * T, SR), F32, kind="Internal").ap()
    window_table = nc.dram_tensor("window_table", (N + 2 * T, NP * HD), BF16, kind="Internal").ap()

    with ExitStack() as ctx:
        ctx.enter_context(nc.allow_non_contiguous_dma(reason="weights of a few hundred elements"))

        def sb(name, shape, dt=F32):
            return ctx.enter_context(nc.sbuf_tensor(name, shape, dt))

        def sem(name):
            return ctx.enter_context(nc.semaphore(name))

        X = sb("X", [T, NT, D])
        xnT = sb("xnT", [K, KC, N])
        lent = xnT[:, :, :].rearrange("p k n -> p (k n)")
        shared = sb("shared", [K, NT * 2 * QK])
        KV = shared[0:T, :].rearrange("p (t f) -> p t f", t=NT)
        taken = 0

        def later(rows, shape, pattern, **sizes):
            nonlocal taken
            size = int(math.prod(shape))
            taken += size
            assert taken <= NT * 2 * QK
            return shared[0:rows, taken - size:taken].rearrange(pattern, **sizes)


        early = sb("early", [K, 4168])
        early_taken = 0

        def place(rows, shape, dt=F32, pattern=None, **sizes):
            nonlocal early_taken
            words = -(-int(math.prod(shape)) * (2 if dt == BF16 else 4) // 4)
            early_taken += words
            assert early_taken <= 4168
            view = early[0:rows, early_taken - words:early_taken]
            view = view if dt == F32 else view.bitcast(dt)
            return view.rearrange(pattern, **sizes) if pattern else view

        ident = sb("ident", [K, K])
        ones = sb("ones", [K, K])
        Wg = place(K, [KC, D], F32, "p (k f) -> p k f", k=KC)
        a_cols = sb("a_cols", [K, 2, KC])
        a_blocks = sb("a_blocks", [K, KC, 2 * H])
        Wnode = sb("Wnode", [K, KC, HR])
        Wenc = sb("Wenc", [4, HD])
        Wenc0 = place(4, [D])
        WencP = sb("WencP", [K, HD], BF16)
        ew_cols = sb("ew_cols", [K, KC, 4])
        ew_res = sb("ew_res", [K, KC, 4])
        ew_p = sb("ew_p", [K, NP, KC, 4], BF16)
        ew_parts = sb("ew_parts", [K, KC, EQ, EK], BF16)
        identb = sb("identb", [K, K], BF16)
        wrow = place(T, [2, NP, HD], BF16, "p (b n f) -> p b n f", b=2, n=NP)
        wres = place(T, [2, HD], F32, "p (b f) -> p b f", b=2)
        Wqkv = sb("Wqkv", [K, KC, 3 * QK])
        WqT = place(QK, [D])
        Wo = place(QK, [D])
        Wmix = place(K, [KC, D], F32, "p (k f) -> p k f", k=KC)
        bias_rows = sb("bias_rows", [1, 2, D])
        bias_row = sb("bias_row", [1, D])
        Wr = sb("Wr", [K, KC, X8])
        br = sb("br", [1, X8])
        gamma = sb("gamma", [T, D])
        beta = sb("beta", [T, D])
        b1 = sb("b1", [K, TOP, FC])

        stats = sb("stats", [T, PER_LOAD, 6])
        mvs = sb("mvs", [T, PER_LOAD, 2])
        mv = sb("mv", [T, NT, 2])
        rstd = sb("rstd", [T, NT])

        xn = sb("xn", [T, 2, D])
        xnTs = sb("xnTs", [K, 2, KC, T])
        hrow = place(T, [2, HR], F32, "p (b f) -> p b f", b=2)
        kmax = sb("kmax", [T, QK])
        kmaxT = sb("kmaxT", [QK, 1])
        nkmax = sb("nkmax", [1, QK])
        nkmaxB = sb("nkmaxB", [T, QK])
        kexp = place(T, [2, QK], F32, "p (b f) -> p b f", b=2)
        ksum = sb("ksum", [QK, 1])
        ctxn = sb("ctxn", [QK, QK])
        ctxT = sb("ctxT", [QK, QK])
        ctxWo = place(QK, [D])
        onescol = sb("onescol", [T, 1])
        zrow = sb("zrow", [1, K])

        lower = sb("lower", [T, T])
        spare = sb("spare", [T, 1])
        src_i = sb("src_i", [T, 1], I32)
        dst_i = sb("dst_i", [T, 1], I32)
        dst_f = sb("dst_f", [T, 1])
        ea = sb("ea", [T, 4])
        eaT = sb("eaT", [4, T])
        Gs, Gd, S0, S1 = (later(T, [HR], "p f -> p f") for _ in range(4))
        same, apart, before = (later(T, [T], "p f -> p f") for _ in range(3))
        prod, msg = (later(T, [HD], "p f -> p f") for _ in range(2))
        score = sb("score", [T, H])
        score2 = sb("score2", [T, H])
        spread = later(T, [H, T], "p (h e) -> p h e", h=H)
        masked = later(T, [H, T], "p (h e) -> p h e", h=H)
        tmax = sb("tmax", [T, H])
        newmax = sb("newmax", [T, H])
        shifted = sb("shifted", [T, 2 * H])
        ew = sb("ew", [T, 2 * H])
        nbefore = sb("nbefore", [T, 1])
        to_f = sb("to_f", [T, 1])
        to_i = sb("to_i", [T, 1], I32)

        taken = 0
        nat_src = later(G, [GE], "p f -> p f")
        nat_dst = later(G, [GE], "p f -> p f")
        nat_ea = later(G, [3 * GE], "p f -> p f")
        nat_new = later(G, [GE + 1], "p f -> p f")
        nat_next = sb("nat_next", [G, 1], I32)
        nat_nextf = sb("nat_nextf", [G, 1])
        nat_gap = sb("nat_gap", [G, 4])
        nat_ok = sb("nat_ok", [G, 1])
        nat_loc = sb("nat_loc", [G, 1])
        nat_str = sb("nat_str", [G, 1])
        base_i = sb("base_i", [1, G], I32)
        straddle = sb("straddle", [1, G + 1])
        ok = sb("ok", [1, 2])
        ok_i = sb("ok_i", [1, 1], I32)
        last_hot = sb("last_hot", [W, G])
        iota_p = sb("iota_p", [W, 1])
        C = G * J
        col_src = lent[0:T, 0:C].bitcast(I32)
        col_loc = lent[0:T, C:2 * C]
        col_new = lent[0:T, 2 * C:3 * C]
        col_last = lent[0:T, 3 * C:4 * C]
        col_ea = lent[0:T, 4 * C:7 * C]
        taken = 0
        early_taken = 0
        Gr = later(T, [2, J, HR], "p (b j f) -> p b j f", b=2, j=J)
        M = later(T, [2, J, W], "p (b j w) -> p b j w", b=2, j=J)
        MT_mem = sb("MT_mem", [W, 2 * J * T + 10], BF16)
        zpad = MT_mem[0:T, 0:NP * HD]
        init_row = MT_mem[0:T, NP * HD:NP * HD + 2 * SR].bitcast(F32)
        MT = MT_mem[:, 0:2 * J * T].rearrange("p (b j e) -> p b j e", b=2, j=J)
        nat_f = MT_mem[0:G, 0:2 * (GE + 2)].bitcast(F32)
        iota_w = sb("iota_w", [T, W])
        e0 = sb("e0", [1, W])
        src_g = sb("src_g", [T, 2, J], I32)
        win = place(W, [2, NP, HD], BF16, "p (b n f) -> p b n f", b=2, n=NP)
        es = sb("es", [T, EB * EQ, EK], BF16)
        es_res = sb("es_res", [T, J, 3])
        penB = sb("penB", [T, J, H])
        eaTg = place(K, [2, EB, T], BF16, "p (b q e) -> p b q e", b=2, q=EB)
        penT = place(J * H, [2, T], F32, "p (b e) -> p b e", b=2)
        er = place(T, [2, HD], F32, "p (b f) -> p b f", b=2)
        pr = place(T, [2, HD], F32, "p (b f) -> p b f", b=2)
        al = place(T, [2, J, H], F32, "p (b j h) -> p b j h", b=2, j=J)
        alx = place(T, [J, H], F32, "p (j h) -> p j h", j=J)
        alL = place(T, [J, H], F32, "p (j h) -> p j h", j=J)
        Fs = place(J * H, [T])
        Fm = sb("Fm", [T, 2, J, H + 1])
        cmr = sb("cmr", [1, H + 1])
        pres = sb("pres", [W, J + 1])
        wmx = place(W, [J + 1, H], F32, "p (j h) -> p j h", h=H)
        mW = sb("mW", [W, H])
        mWr = sb("mWr", [W, H])
        mWp = sb("mWp", [W, H, NP], BF16)
        mE = place(T, [J * H])
        dsh = place(T, [J * H])
        hot = sb("hot", [W, 2])
        Ps = place(W, [2, HD], F32, "p (b f) -> p b f", b=2)
        c_raw = sb("c_raw", [1, SR])
        c_dif = sb("c_dif", [1, H])
        c_fac = sb("c_fac", [1, H])
        c_fs = sb("c_fs", [1, H])
        crow = sb("crow", [1, HD])
        taken = 0
        W1 = later(K, [TOP, KC, FF], "p (n k f) -> p n k f", n=TOP, k=KC)
        W2 = later(K, [TOP, FC, D], "p (n c f) -> p n c f", n=TOP, c=FC)
        hid = later(K, [2, TOP * FC, CH], "p (b j e) -> p b j e", b=2, j=TOP * FC)
        agg = later(T, [2, D], "p (b f) -> p b f", b=2)
        b2 = later(1, [TOP, D], "p (b f) -> p b f", b=TOP)
        yrow = later(T, [2, D], "p (b f) -> p b f", b=2)

        st = later(T, [2, SR], "p (b f) -> p b f", b=2)
        den = sb("den", [T, 2, H])
        rden = sb("rden", [T, 2, H])
        ysum = sb("ysum", [K, KC])
        r = {n: sb("r_" + n, [1, X8]) for n in
             ("logits", "exp", "w", "cap", "load", "exp2", "w2", "rank", "first", "second", "num", "tmp")}
        rs = {n: sb("rs_" + n, [1, 1]) for n in
              ("max", "sum", "rsum", "max2", "sum2", "rsum2", "diff", "e", "e1")}
        top = sb("top", [1, TOP])
        topi = sb("topi", [1, TOP])
        topi_i = sb("topi_i", [1, TOP], I32)
        topw = sb("topw", [1, TOP])
        topwB = sb("topwB", [K, TOP])
        pair = sb("pair", [1, X8, X8])
        pair2 = sb("pair2", [1, X8, X8])
        tri8 = sb("tri8", [1, X8, X8])
        z = later(T, [2, D], "p (b f) -> p b f", b=2)
        zmv = sb("zmv", [T, 2, 2])
        zsd = sb("zsd", [T, 2])
        zr = sb("zr", [T, 2])
        res = later(T, [2, D], "p (b f) -> p b f", b=2)

        bank = [ctx.enter_context(nc.psum_tensor(f"bank{i}", [K, 512], F32)) for i in range(8)]

        s_xload = [sem(f"s_xload{i}") for i in range(LOADS)]
        s_wload = sem("s_wload")
        s_wenc = sem("s_wenc")
        s_wencp = sem("s_wencp")
        s_ewp = sem("s_ewp")
        s_const = sem("s_const")
        s_setup_pe = sem("s_setup_pe")
        s_setup_ve = sem("s_setup_ve")
        s_stats = sem("s_stats")
        s_mvs = sem("s_mvs")
        s_mv = sem("s_mv")
        s_var = sem("s_var")
        s_sd = sem("s_sd")
        s_rstd = sem("s_rstd")
        s_xn = sem("s_xn")
        s_xnT = sem("s_xnT")
        s_xnTs = sem("s_xnTs")
        s_xnTr = sem("s_xnTr")
        s_rows = sem("s_rows")
        s_hrow = sem("s_hrow")
        s_kv = sem("s_kv")
        s_kmax = sem("s_kmax")
        s_hst = [sem(f"s_hst{i}") for i in range(2)]
        s_km = sem("s_km")
        s_kmp = sem("s_kmp")
        s_kshift = sem("s_kshift")
        s_kexp = sem("s_kexp")
        s_ctx = sem("s_ctx")
        s_fold_v = sem("s_fold_v")
        s_fold_p = sem("s_fold_p")
        s_stage = sem("s_stage")
        s_mix = sem("s_mix")
        s_mixed = sem("s_mixed")
        s_passed = sem("s_passed")
        s_init = sem("s_init")
        s_initst = sem("s_initst")
        g_src, g_dst, g_ea = sem("g_src"), sem("g_dst"), sem("g_ea")
        g_Gs, g_Gd, g_S0 = sem("g_Gs"), sem("g_Gd"), sem("g_S0")
        V_STEPS = ("dstf same eaT apart before nbefore gap sel tof toi prod a1 a2 score spread masked masked "
                   "tmax newmax shift shift msg msg keep new").split()
        P_STEPS = "dstT eaTp enc spreadB sum".split()
        g_v, g_p, g_ew = sem("g_v"), sem("g_p"), sem("g_ew")

        def v_done(name, t):
            return len(V_STEPS) * t + len(V_STEPS) - V_STEPS[::-1].index(name)

        def p_done(name, t):
            return len(P_STEPS) * t + P_STEPS.index(name) + 1

        g_scatter = sem("g_scatter")
        g_done = sem("g_done")
        f_nat = [sem(f"f_nat{i}") for i in range(4)]
        f_natd = sem("f_natd")
        f_turn = sem("f_turn")
        f_colv, f_cola = sem("f_colv"), sem("f_cola")
        f_rows = sem("f_rows")
        f_ok = sem("f_ok")
        f_pad = sem("f_pad")
        f_wst = [sem(f"f_wst{i}") for i in range(2)]
        s_wp = sem("s_wp")
        s_wv = sem("s_wv")
        f_es = sem("f_es")
        f_esp = sem("f_esp")
        f_src = sem("f_src")
        f_last = sem("f_last")
        f_hot = sem("f_hot")
        f_G = [sem(f"f_G{i}") for i in range(2)]
        f_win = [sem(f"f_win{i}") for i in range(2)]
        f_ET = sem("f_ET")
        f_eaT = sem("f_eaT")
        f_M = sem("f_M")
        f_MTp = sem("f_MTp")
        f_MT = sem("f_MT")
        f_enc = sem("f_enc")
        f_hd = sem("f_hd")
        f_relu = sem("f_relu")
        f_prod = sem("f_prod")
        f_red = sem("f_red")
        f_al0, f_al = sem("f_al0"), sem("f_al")
        f_C1, f_scan, f_C2, f_Fm = sem("f_C1"), sem("f_scan"), sem("f_C2"), sem("f_Fm")
        f_cm = sem("f_cm")
        f_C3 = sem("f_C3")
        f_w = sem("f_w")
        f_C4 = sem("f_C4")
        f_mE, f_dsh, f_exp = sem("f_mE"), sem("f_dsh"), sem("f_exp")
        f_dif, f_fac, f_fs, f_crow = sem("f_dif"), sem("f_fac"), sem("f_fs"), sem("f_crow")
        f_v = sem("f_v")
        f_agg = sem("f_agg")
        f_P = sem("f_P")
        f_C5 = sem("f_C5")
        f_craw = sem("f_craw")
        f_store = sem("f_store")
        f_stored = sem("f_stored")
        s_st = [sem(f"s_st{i}") for i in range(2)]
        s_den, s_rden, s_agg = sem("s_den"), sem("s_rden"), sem("s_agg")
        s_x1 = sem("s_x1")
        s_yr = sem("s_yr")
        s_yT = sem("s_yT")
        s_yTr = sem("s_yTr")
        s_ysum = sem("s_ysum")
        s_r, s_rp, s_ra = sem("s_r"), sem("s_rp"), sem("s_ra")
        s_topi = sem("s_topi")
        s_wx = sem("s_wx")
        s_w2s = sem("s_w2s")
        s_l1 = sem("s_l1")
        s_hid = sem("s_hid")
        s_l2 = sem("s_l2")
        s_yrow, s_z = sem("s_yrow"), sem("s_z")
        s_zst, s_zmv, s_zvar, s_zsd, s_zr = (sem(n) for n in ("s_zst", "s_zmv", "s_zvar", "s_zsd", "s_zr"))
        s_n1, s_n2, s_n3, s_res = (sem(n) for n in ("s_n1", "s_n2", "s_n3", "s_res"))
        s_out = [sem(f"s_out{i}") for i in range(2)]

        f_eaTb = sem("f_eaTb")
        NAT_STEPS = 15
        column_batches = []

        def batches(kind, dest, sources, scale=1.0):
            for a in range(0, len(sources), 4):
                part = sources[a:a + 4]
                column_batches.append((kind, dest[:, a:a + len(part), :], part, scale))

        def tiles_of(nat, at=0):
            return [nat[:, j * T + at:(j + 1) * T + at] for j in range(J)]

        batches("src", col_src.rearrange("p (g j) -> p j g", j=J), tiles_of(nat_src))
        batches("loc", col_loc.rearrange("p (g j) -> p j g", j=J), tiles_of(nat_dst))
        batches("new", col_new.rearrange("p (g j) -> p j g", j=J), tiles_of(nat_new), LOW)
        batches("last", col_last.rearrange("p (g j) -> p j g", j=J), tiles_of(nat_new, 1))
        batches("ea", col_ea.rearrange("p (g m) -> p m g", m=3 * J),
                [nat_ea[:, 3 * T * j + c:3 * T * (j + 1):3] for j in range(J) for c in range(3)])
        COLUMNS_VEC = [n for n, b in enumerate(column_batches) if b[0] == "src" or n % 2]
        COLUMNS_ACT = [n for n in range(len(column_batches)) if n not in COLUMNS_VEC]
        COLV, COLA = len(COLUMNS_VEC), len(COLUMNS_ACT)
        column_read = [(f_colv, COLUMNS_VEC.index(n) + 1) if n in COLUMNS_VEC else (f_cola, COLUMNS_ACT.index(n) + 1)
                       for n in range(len(column_batches))]

        block = ctx.enter_context(nc.Block())
        WEIGHT_LOADS = 15
        CONSTS = 35

        @block.sync
        def _(sp):
            x_tiles = x.rearrange("(t p) f -> p t f", p=T)
            weight_loads = [
                (Wg[:, :, :], L0_gnn_W.rearrange("(k p) i -> p k i", p=K)),
                (a_cols[:, 0, :], L0_gnn_a_src.rearrange("h d -> (h d)").rearrange("(k p) -> p k", p=K)),
                (a_cols[:, 1, :], L0_gnn_a_dst.rearrange("h d -> (h d)").rearrange("(k p) -> p k", p=K)),
                (Wenc0[0:3, :], L0_gnn_edge_W.rearrange("f c -> c f")),
                (Wenc0[3:4, :], L0_gnn_edge_b.unsqueeze(0)),
                (ew_cols[:, :, 0:3], L0_gnn_edge_W.rearrange("(k p) c -> p k c", p=K)),
                (ew_cols[:, :, 3:4], L0_gnn_edge_b.rearrange("(k p) -> p k", p=K).unsqueeze(2)),
                (Wqkv[:, :, :], L0_mix_W_qkv.rearrange("(k p) f -> p k f", p=K)),
                (Wo[:, :], L0_mix_W_out),
                (bias_rows[:, 0, :], L0_gnn_bias.unsqueeze(0)),
                (bias_rows[:, 1, :], L0_mix_b_out.unsqueeze(0)),
                (Wr[:, :, :], L0_ffn_Wr.rearrange("(k p) e -> p k e", p=K)),
                (br[:, :], L0_ffn_br.unsqueeze(0)),
                (gamma[:, :], L0_ffn_gamma.partition_broadcast(T)),
                (beta[:, :], L0_ffn_beta.partition_broadcast(T)),
            ]
            assert len(weight_loads) == WEIGHT_LOADS
            for i in range(LOADS):
                part = slice(i * PER_LOAD, (i + 1) * PER_LOAD)
                sp.dma_start(X[:, part, :], x_tiles[:, part, :]).then_inc(s_xload[i], 16)
                if i == 0:
                    for dest, source in weight_loads:
                        sp.dma_start(dest, source).then_inc(s_wload, 16)
            sp.wait_ge(s_init, 2)
            sp.dma_start(state_table.rearrange("(t p) c -> p t c", p=T),
                         init_row[:, :].unsqueeze(1).broadcast_to([T, NT + 2, SR])).then_inc(s_initst, 16)
            sp.wait_ge(s_const, CONSTS)
            sp.dma_start(window_table[N:N + 2 * T, :].rearrange("(t p) c -> p t c", p=T),
                         zpad[:, :].unsqueeze(1).broadcast_to([T, 2, NP * HD])).then_inc(f_pad, 16)
            with sp.Fori(0, NT // 2) as i:
                for par in range(2):
                    t = 2 * i + par
                    sp.wait_ge(s_hrow, t + 3)
                    sp.dma_start(node_table[bass.ds(t * T, T), :], hrow[:, par, :]).then_inc(s_hst[par], 16)
                    sp.wait_ge(s_wv, 4 * t + 12)
                    sp.dma_start(window_table[bass.ds(t * T, T), :],
                                 wrow[:, par, :, :].rearrange("p n f -> p (n f)")).then_inc(f_wst[par], 16)
            def any_order():
                with sp.Fori(0, ET) as t:
                    sp.wait_ge(g_done, t + 1)
                    sp.dma_start(src_i[:, :], src[bass.ds(t * T, T)].unsqueeze(1)).then_inc(g_src, 16)
                    sp.dma_start(dst_i[:, :], dst[bass.ds(t * T, T)].unsqueeze(1)).then_inc(g_dst, 16)
                    sp.dma_start(ea[:, 0:3], edge_attr_3[bass.ds(t * T, T), :]).then_inc(g_ea, 16)

                sp.wait_ge(g_done, ET + 1)

            def in_groups():
                def load(g, par):
                    sp.wait_ge(f_hd, J * g + J)
                    first = sp.value_load(base_i[0:1, bass.ds(g, 1)], min_val=0, max_val=N - 1)
                    sp.dma_start(win[:, par, :, :].rearrange("p n f -> p (n f)"),
                                 window_table[bass.ds(first, W), :]).then_inc(f_win[par], 16)

                def store(g, par):
                    sp.wait_ge(f_P, g + 2)
                    first = sp.value_load(base_i[0:1, bass.ds(g, 1)], min_val=0, max_val=N - 1)
                    sp.dma_start(state_table[bass.ds(first, W), 0:HD], Ps[:, par, :]).then_inc(f_store, 16)
                    sp.wait_ge(f_store, 16 * g + 16)
                    sp.sem_inc(f_stored, 1)

                for par in range(2):
                    sp.wait_ge(f_wst[par], NT // 2 * 16)
                sp.wait_ge(f_pad, 16)
                sp.wait_ge(s_initst, 16)
                load(0, 0)
                load(1, 1)
                with sp.Fori(0, G // 2 - 1) as i:
                    for par in range(2):
                        load(2 * i + par + 2, par)
                        store(2 * i + par, par)
                store(G - 2, 0)
                store(G - 1, 1)

            sp.sem_inc(f_stored, 2)
            sp.wait_ge(s_ctx, NT + 2)
            sp.dma_start(nat_dst[:, :].bitcast(I32), dst.rearrange("(g e) -> g e", e=GE)).then_inc(f_nat[0], 16)
            sp.dma_start(nat_next[0:G - 1, :], dst.rearrange("(g e) -> g e", e=GE)[1:G, 0:1]).then_inc(f_nat[1], 16)
            sp.dma_start(nat_src[:, :].bitcast(I32), src.rearrange("(g e) -> g e", e=GE)).then_inc(f_nat[2], 16)
            sp.dma_start(nat_ea[:, :], edge_attr_3.rearrange("(g e) c -> g (e c)", e=GE)).then_inc(f_nat[3], 16)

            sp.wait_ge(f_ok, 4)
            grouped = sp.value_load(ok_i[0:1, 0:1], min_val=0, max_val=1)
            with sp.If(grouped == 1):
                in_groups()
            with sp.Else():
                any_order()
            with sp.Fori(0, NT // 2) as i:
                for par in range(2):
                    t = 2 * i + par
                    sp.wait_ge(s_x1, t + 1)
                    sp.dma_start(st[:, par, :], state_table[bass.ds(t * T, T), :]).then_inc(s_st[par], 16)
            sp.wait_ge(s_topi, 1)
            for n in range(TOP):
                e = sp.value_load(topi_i[0:1, n:n + 1], min_val=0, max_val=X8 - 1)
                sp.dma_start(W1[:, n, :, :], L0_ffn_W1[bass.ds(e, 1), :, :]
                             .rearrange("a (k p) f -> p (a k) f", p=K)).then_inc(s_wx, 16)
                sp.dma_start(b1[:, n, :], L0_ffn_b1[bass.ds(e, 1), :]
                             .rearrange("a (c p) -> p (a c)", p=K)).then_inc(s_wx, 16)
                sp.dma_start(W2[:, n, :, :], L0_ffn_W2[bass.ds(e, 1), :, :]
                             .rearrange("a (c p) f -> p (a c) f", p=K)).then_inc(s_wx, 16)
                sp.dma_start(b2[:, n, :], L0_ffn_b2[bass.ds(e, 1), :]).then_inc(s_wx, 16)
            with sp.Fori(0, NCH) as c:
                for par in range(2):
                    t = 2 * c + par
                    sp.wait_ge(s_res, t + 1)
                    sp.dma_start(out[bass.ds(t * T, T), :], res[:, par, :]).then_inc(s_out[par], 16)
            for par in range(2):
                sp.wait_ge(s_out[par], NCH * 16)

        @block.gpsimd
        def _(po):
            po.sem_inc(s_xnTr, 2)
            po.memset(Wenc[:, :], 0.0).then_inc(s_wenc, 1)
            po.wait_ge(s_wenc, 1)
            po.affine_select(out=Wenc[:, :], in_=Wenc[:, :], compare_op=ALU.not_equal, fill=1.0,
                             base=-3, pattern=[[0, HD]], channel_multiplier=1).then_inc(s_wenc, 1)
            po.memset(init_row[:, :], 0.0).then_inc(s_init, 1)
            po.memset(ones[:, :], 1.0).then_inc(s_const, 1)
            po.memset(ident[:, :], 0.0).then_inc(s_const, 1)
            po.memset(lower[:, :], 1.0).then_inc(s_const, 1)
            po.memset(tri8[:, :, :], 1.0).then_inc(s_const, 1)
            po.memset(ea[:, :], 1.0).then_inc(s_const, 1)
            po.memset(onescol[:, :], 1.0).then_inc(s_const, 1)
            po.memset(ctxn[:, :], 0.0).then_inc(s_const, 1)
            po.memset(zrow[:, :], 0.0).then_inc(s_const, 1)
            po.iota(spare[:, :], pattern=[[0, 1]], base=N, channel_multiplier=1,
                    allow_small_or_imprecise_dtypes=True).then_inc(s_const, 1)
            po.iota(iota_p[:, :], pattern=[[0, 1]], base=0, channel_multiplier=1,
                    allow_small_or_imprecise_dtypes=True).then_inc(s_const, 1)
            po.iota(iota_w[:, :], pattern=[[1, W]], base=0, channel_multiplier=0,
                    allow_small_or_imprecise_dtypes=True).then_inc(s_const, 1)
            po.memset(identb[:, :], 0.0).then_inc(s_const, 1)
            po.memset(WencP[:, :], 0.0).then_inc(s_const, 1)
            po.memset(ew_parts[:, :, :, :], 0.0).then_inc(s_const, 1)
            po.memset(zpad[:, :], 0.0).then_inc(s_const, 1)
            po.memset(e0[:, :], 0.0).then_inc(s_const, 1)
            po.memset(es[:, :, :], 0.0).then_inc(s_const, 1)
            po.memset(c_raw[:, :], 0.0).then_inc(s_const, 1)
            po.memset(straddle[:, :], 0.0).then_inc(s_const, 1)
            po.memset(nat_next[:, :], N).then_inc(s_const, 1)
            po.iota(r["num"][:, :], pattern=[[1, X8]], base=0, channel_multiplier=0,
                    allow_small_or_imprecise_dtypes=True).then_inc(s_const, 1)
            n = 21
            po.wait_ge(s_init, 1)
            po.memset(init_row[:, HD:SR], LOW).then_inc(s_init, 1)
            po.wait_ge(s_const, n)
            po.affine_select(out=ident[:, :], in_=ident[:, :], compare_op=ALU.not_equal, fill=1.0,
                             base=0, pattern=[[-1, K]], channel_multiplier=1).then_inc(s_const, 1)
            po.affine_select(out=identb[:, :], in_=identb[:, :], compare_op=ALU.not_equal, fill=1.0,
                             base=0, pattern=[[-1, K]], channel_multiplier=1).then_inc(s_const, 1)
            po.memset(e0[:, 0:1], 1.0).then_inc(s_const, 1)
            po.memset(es[:, 0:J, 18:21], 1.0).then_inc(s_const, 1)
            po.affine_select(out=lower[:, :], in_=lower[:, :], compare_op=ALU.is_gt, fill=0.0,
                             base=0, pattern=[[-1, T]], channel_multiplier=1).then_inc(s_const, 1)
            po.affine_select(out=tri8[:, :, :], in_=tri8[:, :, :], compare_op=ALU.is_gt, fill=0.0,
                             base=0, pattern=[[1, X8], [-1, X8]], channel_multiplier=0).then_inc(s_const, 1)
            po.wait_ge(s_wload, WEIGHT_LOADS * 16)
            for k in range(KC):
                for s in range(2):
                    po.tensor_copy(a_blocks[:, k, s * H:(s + 1) * H],
                                   a_cols[:, s, k:k + 1].broadcast_to([K, H])).then_inc(s_const, 1)
            n += 6 + 4
            po.wait_ge(s_const, n)
            for k in range(KC):
                blk = a_blocks[:, k, :].rearrange("p (s h) -> p s h", s=2)
                po.affine_select(out=blk, in_=blk, compare_op=ALU.is_ge, fill=0.0,
                                 base=K * k, pattern=[[0, 2], [-DH, H]], channel_multiplier=1).then_inc(s_const, 1)
                n += 1
                po.wait_ge(s_const, n)
                po.affine_select(out=blk, in_=blk, compare_op=ALU.is_ge, fill=0.0,
                                 base=DH - 1 - K * k, pattern=[[0, 2], [DH, H]],
                                 channel_multiplier=-1).then_inc(s_const, 1)
                n += 1
            assert n == CONSTS
            po.wait_ge(s_setup_ve, 8)
            ones_at = WencP[:, :].rearrange("p (h b) -> p h b", h=H)[:, :, DH:HB]
            for q in range(EQ):
                po.affine_select(out=ones_at, in_=ones_at, compare_op=ALU.not_equal, fill=1.0,
                                 base=-(EK * q + 18), pattern=[[0, H], [0, 1]], channel_multiplier=1
                                 ).then_inc(s_wencp, 1)
                po.wait_ge(s_wencp, q + 1)
            with po.Fori(0, NT // 2) as i:
                for par in range(2):
                    t = 2 * i + par
                    po.wait_ge(s_xnTs, t + 3)
                    po.tensor_copy(xnT[:, :, bass.ds(t * T, T)], xnTs[:, par, :, :]).then_inc(s_xnTr, 1)
            po.wait_ge(s_xnTr, NT + 2)
            po.wait_ge(s_rows, NT + 2)
            with po.Fori(0, NT // 2) as i:
                for par in range(2):
                    t = 2 * i + par
                    po.wait_ge(s_mix, t + 1)
                    po.tensor_copy(xnTs[:, par, :, :], xnT[:, :, bass.ds(t * T, T)]).then_inc(s_stage, 1)
            for par in range(2):
                po.wait_ge(s_hst[par], NT // 2 * 16)
            po.wait_ge(s_initst, 16)
            def any_order():
                with po.Fori(0, ET) as t:
                    po.wait_ge(g_src, 16 * t + 16)
                    po.wait_ge(g_dst, 16 * t + 16)
                    po.sem_inc(s_passed, 1)
                    for rows, table, index, landed in ((Gs, node_table, src_i, g_Gs), (Gd, node_table, dst_i, g_Gd),
                                                       (S0, state_table, dst_i, g_S0)):
                        po.indirect_dma_start(out=rows[:, :], out_offset=None, in_=table,
                                              in_offset=bass.IndirectOffsetOnAxis(ap=index[:, :], axis=0)
                                              ).then_inc(landed, 16)
                    po.wait_ge(g_v, v_done("new", t))
                    po.wait_ge(g_v, v_done("newmax", t))
                    po.wait_ge(g_v, v_done("toi", t))
                    po.wait_ge(g_S0, 16 * t + 16)
                    po.sem_inc(s_passed, 1)
                    po.indirect_dma_start(out=state_table, out_offset=bass.IndirectOffsetOnAxis(ap=to_i[:, :], axis=0),
                                          in_=S1[:, :], in_offset=None).then_inc(g_scatter, 16)


            def in_groups():
                def gathers(g, par, piece):
                    po.wait_ge(f_agg, VN * g + piece + 1)
                    po.sem_inc(s_passed, 1)
                    for j in range(VT * piece, VT * piece + VT):
                        po.indirect_dma_start(out=Gr[:, par, j, :], out_offset=None, in_=node_table,
                                              in_offset=bass.IndirectOffsetOnAxis(ap=src_g[:, par, j:j + 1], axis=0)
                                              ).then_inc(f_G[par], 16)

                def attributes(g):
                    if g is not zero:
                        po.wait_ge(f_ET, g)
                        po.sem_inc(s_passed, 1)
                    ea_g = col_ea[:, bass.ds(3 * J * g, 3 * J)].rearrange("p (j c) -> p j c", c=3)
                    po.tensor_copy(es[:, 0:J, 0:3], ea_g).then_inc(f_esp, 1)
                    po.wait_ge(f_esp, 5 * g + 1)
                    po.sem_inc(s_passed, 1)
                    po.tensor_tensor(es_res[:, :, :], ea_g, es[:, 0:J, 0:3], ALU.subtract).then_inc(f_esp, 1)
                    po.wait_ge(f_esp, 5 * g + 2)
                    po.sem_inc(s_passed, 1)
                    po.tensor_copy(es[:, 0:J, 6:9], es_res[:, :, :]).then_inc(f_esp, 1)
                    po.wait_ge(f_esp, 5 * g + 3)
                    po.sem_inc(s_passed, 1)
                    po.tensor_tensor(es_res[:, :, :], es_res[:, :, :], es[:, 0:J, 6:9], ALU.subtract).then_inc(f_esp, 1)
                    po.wait_ge(f_esp, 5 * g + 4)
                    po.sem_inc(s_passed, 1)
                    po.tensor_copy(es[:, 0:J, 12:15], es_res[:, :, :]).then_inc(f_esp, 1)
                    for at, of in ((3, 0), (9, 0), (15, 6)):
                        po.tensor_copy(es[:, 0:J, at:at + 3], es[:, 0:J, of:of + 3]).then_inc(f_es, 1)
                    po.tensor_copy(penB[:, :, :], col_new[:, bass.ds(J * g, J)].unsqueeze(2)
                                   .broadcast_to([T, J, H])).then_inc(f_es, 1)

                zero = 0

                def group(g, par, last=False):
                    po.wait_ge(f_agg, VN * g + 1)
                    po.sem_inc(s_passed, 1)
                    po.tensor_copy(src_g[:, par, :], col_src[:, bass.ds(J * g, J)]).then_inc(f_src, 1)
                    po.tensor_copy(Fm[:, par, :, H:H + 1], col_last[:, bass.ds(J * g, J)].unsqueeze(2)
                                   ).then_inc(f_last, 1)
                    po.wait_ge(f_src, g + 1)
                    gathers(g, par, 0)
                    if not last:
                        attributes(g + 1)
                    gathers(g, par, 1)
                    gathers(g, par, 2)
                    po.wait_ge(f_craw, g + 2)
                    po.sem_inc(s_passed, 1)
                    po.tensor_copy(hot[:, par:par + 1], last_hot[:, bass.ds(g, 1)]).then_inc(f_hot, 1)

                attributes(zero)
                with po.Fori(0, G // 2 - 1) as i:
                    group(2 * i, 0)
                    group(2 * i + 1, 1)
                group(G - 2, 0)
                group(G - 1, 1, last=True)

            po.wait_ge(f_colv, COLV)
            po.wait_ge(f_cola, COLA)

            po.wait_ge(f_ok, 4)
            grouped = po.value_load(ok_i[0:1, 0:1], min_val=0, max_val=1)
            with po.If(grouped == 1):
                in_groups()
            with po.Else():
                any_order()

        @block.tensor
        def _(pe):
            for s, credit in ((s_xnT, 2), (s_rows, 2), (s_ctx, 2), (s_mix, 2), (s_yT, 2), (s_l2, 4), (f_hd, 2 * J), (f_agg, 6)):
                pe.sem_inc(s, credit)
            pe.wait_ge(s_const, CONSTS)
            pe.wait_ge(s_wload, WEIGHT_LOADS * 16)
            for ki in range(KC):
                for kh in range(KC):
                    mm = pe.transpose(bank[ki][:, kh * K:(kh + 1) * K], Wg[:, kh, ki * K:(ki + 1) * K], ident[:, :])
                mm.then_inc(s_setup_pe, 1)
            for ki in range(KC):
                for kh in range(KC):
                    mm = pe.matmul(bank[2 + ki][:, 0:2 * H], Wg[:, kh, ki * K:(ki + 1) * K], a_blocks[:, kh, :],
                                   start=(kh == 0), stop=(kh == KC - 1))
                mm.then_inc(s_setup_pe, 1)
            for ki in range(KC):
                mm = pe.transpose(bank[4][:, ki * K:(ki + 1) * K], Wqkv[:, ki, 0:QK], ident[:, :])
            mm.then_inc(s_setup_pe, 1)
            pe.wait_ge(s_ewp, 15)
            for k in range(KC):
                mm = pe.transpose(bank[5][:, k * K // 2:(k + 1) * K // 2].bitcast(BF16),
                                  ew_parts[:, k, :, :].rearrange("p q r -> p (q r)"), identb[:, :])
            mm.then_inc(s_setup_pe, 1)
            pe.wait_ge(s_setup_ve, 8)

            def turn(t, par):
                pe.wait_ge(s_xn, t + 1)
                pe.wait_ge(s_xnTs, t + 1)
                for k in range(KC):
                    mm = pe.transpose(bank[par][:, k * T:(k + 1) * T], xn[:, par, k * K:(k + 1) * K], ident[0:T, 0:T])
                mm.then_inc(s_xnT, 1)

            def node_rows(t, par):
                pe.wait_ge(s_xnTs, t + 3)
                pe.wait_ge(s_hrow, t + 1)
                pe.wait_ge(s_kmax, t + 1)
                for k in range(KC):
                    pe.matmul(bank[2 + par][0:T, 0:HR], xnTs[:, par, k, :], Wnode[:, k, :],
                              start=(k == 0), stop=(k == KC - 1))
                for k in range(KC):
                    mm = pe.matmul(bank[4 + par][0:T, 0:2 * QK], xnTs[:, par, k, :], Wqkv[:, k, QK:3 * QK],
                                   start=(k == 0), stop=(k == KC - 1))
                mm.then_inc(s_rows, 1)

            turn(0, 0)
            with pe.Fori(0, NT // 2 - 1) as i:
                for par in range(2):
                    turn(2 * i + par + 1, 1 - par)
                    node_rows(2 * i + par, par)
            turn(NT - 1, 1)
            node_rows(NT - 2, 0)
            node_rows(NT - 1, 1)

            pe.wait_ge(s_kmax, NT + 2)
            pe.wait_ge(s_xnTs, NT + 2)
            pe.wait_ge(s_hrow, NT + 2)
            pe.transpose(bank[0][:, 0:T], kmax[:, :], ident[0:T, 0:T]).then_inc(s_kmp, 1)
            pe.wait_ge(s_km, 1)
            pe.transpose(bank[1][0:1, 0:K], kmaxT[:, :], ident[:, :]).then_inc(s_kmp, 1)
            pe.wait_ge(s_km, 2)
            pe.matmul(bank[2][0:T, 0:QK], ones[0:1, 0:T], nkmax[:, :], start=True, stop=True).then_inc(s_kmp, 1)
            pe.matmul(bank[6][:, 0:QK], zrow[:, :], zrow[:, :], start=True, stop=False)
            pe.matmul(bank[7][:, 0:1], zrow[:, :], zrow[:, 0:1], start=True, stop=False)
            with pe.Fori(0, NT // 2) as i:
                for par in range(2):
                    t = 2 * i + par
                    pe.wait_ge(s_kexp, t + 1)
                    pe.matmul(bank[6][:, 0:QK], kexp[:, par, :],
                              KV[:, bass.ds(t, 1), QK:2 * QK].rearrange("p a f -> p (a f)"),
                              start=False, stop=False)
                    pe.matmul(bank[7][:, 0:1], kexp[:, par, :], onescol[:, :],
                              start=False, stop=False).then_inc(s_ctx, 1)
            pe.matmul(bank[6][:, 0:QK], zrow[:, :], zrow[:, :], start=False, stop=True)
            pe.matmul(bank[7][:, 0:1], zrow[:, :], zrow[:, 0:1], start=False, stop=True).then_inc(s_fold_p, 1)
            pe.wait_ge(s_fold_v, 5)
            pe.transpose(bank[4][:, 0:QK], ctxn[:, :], ident[:, :]).then_inc(s_fold_p, 1)
            pe.wait_ge(s_fold_v, 6)
            pe.matmul(bank[5][:, 0:D], ctxT[:, :], Wo[:, :], start=True, stop=True).then_inc(s_fold_p, 1)
            pe.wait_ge(s_fold_v, 7)
            for k in range(KC):
                mm = pe.matmul(bank[2 + k][:, 0:D], WqT[:, k * K:(k + 1) * K], ctxWo[:, :], start=True, stop=True)
            mm.then_inc(s_fold_p, 1)
            pe.wait_ge(s_fold_v, 10)
            with pe.Fori(0, NT // 2) as i:
                for par in range(2):
                    t = 2 * i + par
                    pe.wait_ge(s_stage, t + 1)
                    pe.wait_ge(s_mixed, t + 1)
                    for k in range(KC):
                        pe.matmul(bank[par][0:T, 0:D], xnTs[:, par, k, :], Wmix[:, k, :], start=(k == 0), stop=False)
                    pe.matmul(bank[par][0:T, 0:D], ones[0:1, 0:T], bias_row[:, :],
                              start=False, stop=True).then_inc(s_mix, 1)

            pe.wait_ge(s_mixed, NT + 2)
            for par in range(2):
                pe.wait_ge(f_wst[par], NT // 2 * 16)
                pe.wait_ge(s_hst[par], NT // 2 * 16)
            pe.wait_ge(f_natd, NAT_STEPS)
            pe.wait_ge(f_nat[3], 16)
            idg = ident[0:G, 0:G]
            pe.transpose(bank[6][0:1, 0:G], nat_ok[:, :], idg)
            pe.transpose(bank[6][0:1, 128:128 + G], nat_f[:, 1:2], idg)
            pe.transpose(bank[6][0:1, 256:256 + G], nat_str[:, :], idg)
            pe.transpose(bank[6][:, 384:384 + G], nat_loc[:, :].broadcast_to([G, W]), idg).then_inc(f_rows, 1)
            for n, (kind, dest, sources, scale) in enumerate(column_batches):
                if n >= 4:
                    done, count = column_read[n - 4]
                    pe.wait_ge(done, count)
                for k, source in enumerate(sources):
                    mm = pe.transpose(bank[n % 4][0:T, k * G:(k + 1) * G], source, idg)
                mm.then_inc(f_turn, 1)
            pe.wait_ge(f_colv, COLV)
            pe.wait_ge(f_cola, COLA)
            def any_order():
                with pe.Fori(0, ET) as t:
                    pe.wait_ge(g_done, t + 1)
                    pe.wait_ge(g_v, v_done("dstf", t))
                    pe.transpose(bank[0][0:T, 0:T], dst_f[:, :].broadcast_to([T, T]), ident[0:T, 0:T]).then_inc(g_p, 1)
                    pe.wait_ge(g_ea, 16 * t + 16)
                    pe.transpose(bank[1][0:4, 0:T], ea[:, :], ident[0:T, 0:T]).then_inc(g_p, 1)
                    pe.wait_ge(g_v, v_done("eaT", t))
                    pe.matmul(bank[2][0:T, 0:HD], eaT[:, :], Wenc[:, :], start=True, stop=True).then_inc(g_p, 1)
                    pe.wait_ge(g_v, v_done("spread", t))
                    for b in range(2):
                        mm = pe.matmul(bank[3 + b][0:T, 0:4 * T], ones[0:T, 0:T],
                                       spread[:, 4 * b:4 * b + 4, :].rearrange("p h e -> p (h e)"), start=True, stop=True)
                    mm.then_inc(g_p, 1)
                    pe.wait_ge(g_v, v_done("msg", t))
                    pe.wait_ge(g_v, v_done("same", t))
                    pe.matmul(bank[5][0:T, 0:HD], same[:, :], msg[:, :], start=True, stop=True).then_inc(g_p, 1)


            def in_groups():
                enc, spread_h, mt, sums, small, turned = bank[0:2], bank[2:4], bank[4], bank[5], bank[6], bank[7]

                def turn_attributes(g, n):
                    pe.wait_ge(f_es, 4 * g + 4)
                    pe.wait_ge(f_eaT, g + 1)
                    pe.wait_ge(f_craw, g + 1)
                    for b in range(EB):
                        pe.transpose(turned[:, 64 * b:64 * b + 64].bitcast(BF16)[:, 0:T],
                                     es[:, EQ * b:EQ * b + EQ, :].rearrange("p j r -> p (j r)"), identb[0:T, 0:T])
                    pe.transpose(turned[0:J * H, 256:256 + T], penB[:, :, :].rearrange("p j h -> p (j h)"),
                                 ident[0:T, 0:T]).then_inc(f_ET, 1)

                def turn_onehot(gx, px, b):
                    pe.wait_ge(f_M, BN * gx + b + 1)
                    pe.wait_ge(f_MT, BN * gx + b + 1)
                    for k in range(BT):
                        mm = pe.transpose(mt[:, k * T:(k + 1) * T], M[:, px, BT * b + k, :], ident[0:T, 0:T])
                    mm.then_inc(f_MTp, 1)

                def tile(gx, px, kx, j):
                    if j == 0:
                        pe.wait_ge(f_eaT, gx + 2)
                        pe.wait_ge(f_win[px], 16 * kx + 16)
                    if j % BT == 0:
                        pe.wait_ge(f_MT, BN * gx + j // BT + 2)
                    q, n = j % EQ, (px + j) % 2
                    pe.wait_ge(f_relu, J * gx + j + 1)
                    pe.matmul(enc[n][0:T, 0:HD], eaTg[EK * q:EK * (q + 1), px, j // EQ, :],
                              WencP[EK * q:EK * (q + 1), :], start=True, stop=True).then_inc(f_enc, 1)
                    pe.wait_ge(f_prod, J * gx + j + 1)
                    for part in range(NP):
                        mm = pe.matmul(spread_h[n][0:T, 0:HD], MT[:, px, j, :], win[:, px, part, :],
                                       start=(part == 0), stop=(part == NP - 1))
                    mm.then_inc(f_hd, 1)

                def scores_to_rows(gy):
                    pe.wait_ge(f_al, gy + 1)
                    pe.wait_ge(f_mE, gy + 1)
                    pe.transpose(small[0:J * H, 0:T], alL[:, :, :].rearrange("p j h -> p (j h)"),
                                 ident[0:T, 0:T]).then_inc(f_C1, 1)

                def maxima_to_columns(gy):
                    pe.wait_ge(f_scan, gy + 1)
                    pe.transpose(small[0:T, 0:J * H], Fs[:, :], ident[0:J * H, 0:J * H]).then_inc(f_C2, 1)

                def maxima_by_window_row(gy, py):
                    pe.wait_ge(f_Fm, gy + 1)
                    pe.wait_ge(f_last, gy + 1)
                    pe.wait_ge(f_cm, 2 * gy + 2)
                    for j in range(J):
                        pe.matmul(small[:, (H + 1) * j:(H + 1) * (j + 1)], M[:, py, j, :], Fm[:, py, j, :],
                                  start=True, stop=True)
                    pe.matmul(small[:, (H + 1) * J:(H + 1) * (J + 1)], e0[:, :], cmr[:, :],
                              start=True, stop=True).then_inc(f_C3, 1)

                def maxima_to_edges(gy, py):
                    pe.wait_ge(f_w, 8 * gy + 8)
                    for j in range(J):
                        mm = pe.matmul(small[0:T, H * NP * j:H * NP * (j + 1)], MT[:, py, j, :],
                                       mWp[:, :, :].rearrange("p h n -> p (h n)"), start=True, stop=True)
                    mm.then_inc(f_C4, 1)

                def add_messages(gy, py, piece):
                    pe.wait_ge(f_v, VN * gy + piece + 1)
                    if piece == 0:
                        pe.wait_ge(f_P, gy + 1)
                    for j in range(VT * piece, VT * piece + VT):
                        mm = pe.matmul(sums[:, 0:HD], M[:, py, j, :], Gr[:, py, j, 0:HD], start=(j == 0), stop=False)
                    if piece == VN - 1:
                        pe.wait_ge(f_crow, gy + 1)
                        mm = pe.matmul(sums[:, 0:HD], e0[:, :], crow[:, :], start=False, stop=True)
                    mm.then_inc(f_agg, 1)

                def last_node(gy, py, turned_read):
                    pe.wait_ge(f_P, gy + 2)
                    pe.wait_ge(f_hot, gy + 1)
                    pe.wait_ge(f_eaT, turned_read)
                    pe.matmul(turned[0:1, 0:HD], hot[:, py:py + 1], Ps[:, py, :], start=True, stop=True)
                    pe.matmul(turned[0:1, HD:SR], hot[:, py:py + 1], mW[:, :], start=True, stop=True).then_inc(f_C5, 1)

                def step(gx, px, kx, gy, py, ky, last=False):
                    if gx is not None:
                        turn_onehot(gx, px, 0)
                    if gy is not None:
                        scores_to_rows(gy)
                    if gx is not None:
                        turn_onehot(gx, px, 1)
                    for j in range(J):
                        if gx is not None:
                            tile(gx, px, kx, j)
                        if gy is not None and j == 2:
                            maxima_to_columns(gy)
                        if gx is not None and j in (2, 5, 8):
                            turn_onehot(gx, px, j // 3 + 2)
                        if gy is not None and j == 4:
                            maxima_by_window_row(gy, py)
                        if gy is not None and j == 6:
                            maxima_to_edges(gy, py)
                        if gx is not None and j == 10 and not last:
                            turn_attributes(gx + 1, gx + 2)
                        if gy is not None and j in (10, 12, 14):
                            add_messages(gy, py, (j - 10) // 2)
                    if gy is not None:
                        last_node(gy, py, G + 1 if last or gx is None else gy + 4)

                turn_attributes(0, 1)
                step(0, 0, 0, None, None, None)
                with pe.Fori(0, G // 2 - 1) as i:
                    step(2 * i + 1, 1, i, 2 * i, 0, i)
                    step(2 * i + 2, 0, i + 1, 2 * i + 1, 1, i)
                step(G - 1, 1, G // 2 - 1, G - 2, 0, G // 2 - 1, last=True)
                step(None, None, None, G - 1, 1, G // 2 - 1)

            pe.wait_ge(f_ok, 4)
            grouped = pe.value_load(ok_i[0:1, 0:1], min_val=0, max_val=1)
            with pe.If(grouped == 1):
                in_groups()
            with pe.Else():
                any_order()

            with pe.Fori(0, NT // 2) as i:
                for par in range(2):
                    t = 2 * i + par
                    pe.wait_ge(s_yr, t + 1)
                    pe.wait_ge(s_yTr, t + 1)
                    for k in range(KC):
                        mm = pe.transpose(bank[par][:, k * T:(k + 1) * T], xn[:, par, k * K:(k + 1) * K], ident[0:T, 0:T])
                    mm.then_inc(s_yT, 1)
            pe.wait_ge(s_ysum, 1)
            for k in range(KC):
                mm = pe.matmul(bank[2][0:1, 0:X8], ysum[:, k:k + 1], Wr[:, k, :], start=(k == 0), stop=(k == KC - 1))
            mm.then_inc(s_rp, 1)
            pe.wait_ge(s_w2s, 1)
            pe.matmul(bank[3][:, 0:TOP], ones[0:1, :], topw[:, :], start=True, stop=True).then_inc(s_rp, 1)
            pe.wait_ge(s_w2s, 2)
            pe.wait_ge(s_wx, 8 * 16)
            pe.wait_ge(s_yTr, NT + 2)

            def hidden(c, cp):
                for j in range(TOP * FC):
                    n, f = j // FC, j % FC
                    pe.wait_ge(s_hid, TOP * FC * c + j + 1)
                    for k in range(KC):
                        mm = pe.matmul(bank[j % 4][:, 0:CH], W1[:, n, k, f * K:(f + 1) * K],
                                       xnT[:, k:k + 1, bass.ds(c * CH, CH)].rearrange("p a e -> p (a e)"),
                                       start=(k == 0), stop=(k == KC - 1))
                    mm.then_inc(s_l1, 1)

            def experts(c, cp):
                pe.wait_ge(s_hid, TOP * FC * c + TOP * FC + 4)
                for half in range(2):
                    pe.wait_ge(s_z, 2 * c + half + 1)
                    ps = bank[4 + 2 * cp + half][0:T, 0:D]
                    for j in range(TOP * FC):
                        pe.matmul(ps, hid[:, cp, j, half * T:(half + 1) * T], W2[:, j // FC, j % FC, :],
                                  start=(j == 0), stop=False)
                    pe.matmul(ps, ones[0:1, 0:T], bias_row[:, :], start=False, stop=True).then_inc(s_l2, 1)

            hidden(0, 0)
            pe.wait_ge(s_w2s, 7)
            with pe.Fori(0, NCH // 2) as i:
                for cp in range(2):
                    hidden(2 * i + cp + 1, 1 - cp)
                    experts(2 * i + cp, cp)
            experts(NCH - 1, 0)

        @block.scalar
        def _(ac):
            for s, credit in ((s_xnTs, 2), (s_hrow, 2), (s_yTr, 2), (s_hid, 4), (f_eaT, 1), (f_MT, 1), (f_relu, 2), (f_P, 1)):
                ac.sem_inc(s, credit)
            ac.wait_ge(s_var, 1)
            ac.activation(rstd[:, :], rstd[:, :], ACT.Sqrt).then_inc(s_sd, 1)

            def stage(t, par):
                ac.wait_ge(s_xnT, t + 3)
                ac.wait_ge(s_rows, t + 1)
                ac.wait_ge(s_xnTr, t + 1)
                ac.activation(xnTs[:, par, :, :], bank[par][:, 0:KC * T].rearrange("p (k e) -> p k e", k=KC),
                              ACT.Copy).then_inc(s_xnTs, 1)

            def h_row(t, par, i):
                ac.wait_ge(s_rows, t + 3)
                ac.wait_ge(s_wv, 4 * t + 4)
                if i is not None:
                    ac.wait_ge(s_hst[par], 16 * i)
                    ac.wait_ge(f_wst[par], 16 * i)
                ac.activation(wrow[:, par, 0, :], bank[2 + par][0:T, 0:HD], ACT.Copy).then_inc(s_wp, 1)
                ac.activation(hrow[:, par, :], bank[2 + par][0:T, 0:HR], ACT.Copy).then_inc(s_hrow, 1)

            stage(0, 0)
            for par in range(2):
                stage(par + 1, 1 - par)
                h_row(par, par, None)
            with ac.Fori(1, NT // 2 - 1) as i:
                for par in range(2):
                    stage(2 * i + par + 1, 1 - par)
                    h_row(2 * i + par, par, i)
            stage(NT - 1, 1)
            h_row(NT - 2, 0, NT // 2 - 1)
            h_row(NT - 1, 1, NT // 2 - 1)
            with ac.Fori(0, NT // 10) as i:
                ac.wait_ge(s_kshift, i + 1)
                for j in range(10):
                    t = 10 * i + j
                    ac.wait_ge(s_ctx, t + 1)
                    ac.activation(kexp[:, j % 2, :], KV[:, bass.ds(t, 1), 0:QK].rearrange("p a f -> p (a f)"),
                                  ACT.Exp).then_inc(s_kexp, 1)
            def any_order():
                with ac.Fori(0, ET) as t:
                    ac.wait_ge(g_v, v_done("shift", t))
                    ac.activation(ew[:, :], shifted[:, :], ACT.Exp).then_inc(g_ew, 1)


            def in_groups():
                enc, mt, sums, turned = bank[0:2], bank[4], bank[5], bank[7]

                def attributes(g):
                    ac.wait_ge(f_ET, g + 1)
                    par = attributes.par
                    ac.activation(eaTg[:, par, :, :],
                                  turned[:, 0:64 * EB].bitcast(BF16).rearrange("p (b e) -> p b e", b=EB)[:, :, 0:T],
                                  ACT.Copy).then_inc(f_eaTb, 1)
                    ac.activation(penT[:, par, :], turned[0:J * H, 256:256 + T], ACT.Copy).then_inc(f_eaT, 1)

                def onehot(gx, px, b):
                    ac.wait_ge(f_MTp, BN * gx + b + 1)
                    ac.activation(MT[:, px, BT * b:BT * (b + 1), :],
                                  mt[:, 0:BT * T].rearrange("p (k e) -> p k e", k=BT), ACT.Copy).then_inc(f_MT, 1)

                def encode(gx, px, j):
                    n = (px + j) % 2
                    ac.wait_ge(f_enc, J * gx + j + 1)
                    ac.wait_ge(f_prod, J * gx + j + 1)
                    ac.activation(er[:, n, :], enc[n][0:T, 0:HD], ACT.Relu).then_inc(f_relu, 1)

                def step(gx, px, kx, gy, py, ky, last=False):
                    if gx is not None:
                        onehot(gx, px, 0)
                        onehot(gx, px, 1)
                    for j in range(J):
                        if gx is not None:
                            encode(gx, px, j)
                        if gx is not None and j in (2, 5, 8):
                            onehot(gx, px, j // 3 + 2)
                        if gy is not None and j == 6:
                            ac.wait_ge(f_dif, 2 * gy + 2)
                            ac.activation(c_fac[:, :], c_dif[:, :], ACT.Exp).then_inc(f_fac, 1)
                        if gy is not None and j == 8:
                            ac.wait_ge(f_dsh, gy + 1)
                            ac.activation(Gr[:, py, :, 0:HD].rearrange("p j (h b) -> p j h b", h=H)[:, :, :, DH:HB],
                                          dsh[:, :].rearrange("p (j h) -> p j h", h=H).unsqueeze(3),
                                          ACT.Exp).then_inc(f_exp, 1)
                        if gx is not None and j == 10 and not last:
                            attributes.par = 1 - px
                            attributes(gx + 1)
                    if gy is not None:
                        ac.wait_ge(f_agg, VN * gy + VN + 6)
                        ac.wait_ge(f_stored, gy + 1)
                        ac.activation(Ps[:, py, :], sums[:, 0:HD], ACT.Copy).then_inc(f_P, 1)

                attributes.par = 0
                attributes(0)
                step(0, 0, 0, None, None, None)
                with ac.Fori(0, G // 2 - 1) as i:
                    step(2 * i + 1, 1, i, 2 * i, 0, i)
                    step(2 * i + 2, 0, i + 1, 2 * i + 1, 1, i)
                step(G - 1, 1, G // 2 - 1, G - 2, 0, G // 2 - 1, last=True)
                step(None, None, None, G - 1, 1, G // 2 - 1)

            for n in COLUMNS_ACT:
                ac.wait_ge(f_turn, n + 1)
                kind, dest, _, scale = column_batches[n]
                ac.activation(dest, bank[n % 4][0:T, 0:G * dest.shape[1]].rearrange("p (j g) -> p j g", g=G),
                              ACT.Copy, scale=scale).then_inc(f_cola, 1)

            ac.wait_ge(f_ok, 4)
            grouped = ac.value_load(ok_i[0:1, 0:1], min_val=0, max_val=1)
            with ac.If(grouped == 1):
                in_groups()
            with ac.Else():
                any_order()

            ac.wait_ge(s_var, 2)
            ac.activation(rstd[:, :], rstd[:, :], ACT.Sqrt).then_inc(s_sd, 1)
            with ac.Fori(0, NT // 2) as i:
                for par in range(2):
                    t = 2 * i + par
                    ac.wait_ge(s_yT, t + 3)
                    ac.activation(xnT[:, :, bass.ds(t * T, T)],
                                  bank[par][:, 0:KC * T].rearrange("p (k e) -> p k e", k=KC),
                                  ACT.Copy).then_inc(s_yTr, 1)
            for n, (a, b) in enumerate((("logits", "exp"), ("tmp", "exp2"))):
                ac.wait_ge(s_ra, 2 * n + 1)
                ac.activation(r[b][:, :], r[a][:, :], ACT.Exp).then_inc(s_ra, 1)
            ac.wait_ge(s_ra, 5)
            ac.activation(rs["e"][:, :], rs["diff"][:, :], ACT.Exp).then_inc(s_ra, 1)
            ac.wait_ge(s_wx, 8 * 16)

            def gelus(c, cp):
                ac.wait_ge(s_l2, 2 * c + 2)
                for j in range(TOP * FC):
                    ac.wait_ge(s_l1, TOP * FC * c + j + 1)
                    ac.activation(hid[:, cp, j, :], bank[j % 4][:, 0:CH], ACT.Gelu,
                                  bias=b1[:, j // FC, j % FC:j % FC + 1]).then_inc(s_hid, 1)

            def roots(c):
                ac.wait_ge(s_zvar, c + 1)
                ac.activation(zsd[:, :], zsd[:, :], ACT.Sqrt).then_inc(s_zsd, 1)

            gelus(0, 0)
            with ac.Fori(0, NCH // 2) as i:
                for cp in range(2):
                    gelus(2 * i + cp + 1, 1 - cp)
                    roots(2 * i + cp)
            roots(NCH - 1)

        @block.vector
        def _(ve):
            ve.memset(kmax[:, :], LOW).then_inc(s_kmax, 2)
            for s, credit in ((s_mixed, 2), (s_x1, 2), (s_z, 4), (g_done, 1), (s_wv, 8), (f_prod, 2), (f_red, 2), (f_mE, 1), (f_craw, 3)):
                ve.sem_inc(s, credit)

            def part_stats(part, n):
                ve.wait_ge(s_mv, n)
                ve.sem_inc(s_passed, 1)
                for j in range(PER_LOAD):
                    ve.bn_stats(stats[:, j, :], X[:, bass.ds(PER_LOAD * part + j, 1), :]
                                .rearrange("p a f -> p (a f)")).then_inc(s_stats, 1)
                ve.wait_ge(s_stats, PER_LOAD * (n + 1))
                ve.sem_inc(s_passed, 1)
                for j in range(PER_LOAD):
                    ve.bn_aggr(mvs[:, j, :], stats[:, j, :]).then_inc(s_mvs, 1)
                ve.wait_ge(s_mvs, PER_LOAD * (n + 1))
                ve.tensor_copy(mv[:, bass.ds(PER_LOAD * part, PER_LOAD), :], mvs[:, :, :]).then_inc(s_mv, 1)

            def rsqrt_all(n):
                ve.wait_ge(s_mv, LOADS * (n + 1))
                ve.tensor_scalar(rstd[:, :], mv[:, :, 1:2].rearrange("p t a -> p (t a)"), EPS, None,
                                 ALU.add).then_inc(s_var, 1)
                ve.wait_ge(s_sd, n + 1)
                ve.reciprocal(rstd[:, :], rstd[:, :]).then_inc(s_rstd, 1)
                ve.wait_ge(s_rstd, n + 1)

            def normalise(out, t):
                return ve.tensor_scalar(out, X[:, bass.ds(t, 1), :].rearrange("p a f -> p (a f)"),
                                        mv[:, bass.ds(t, 1), 0:1].rearrange("p a f -> p (a f)"),
                                        rstd[:, bass.ds(t, 1)], ALU.subtract, ALU.mult)

            ve.wait_ge(s_wload, WEIGHT_LOADS * 16)
            ve.wait_ge(s_const, CONSTS)
            ve.tensor_copy(ew_p[:, 0, :, :], ew_cols[:, :, :]).then_inc(s_ewp, 1)
            for n in range(1, NP):
                ve.wait_ge(s_ewp, 2 * n - 1)
                ve.tensor_tensor(ew_res[:, :, :], ew_cols[:, :, :] if n == 1 else ew_res[:, :, :],
                                 ew_p[:, n - 1, :, :], ALU.subtract).then_inc(s_ewp, 1)
                ve.wait_ge(s_ewp, 2 * n)
                ve.tensor_copy(ew_p[:, n, :, :], ew_res[:, :, :]).then_inc(s_ewp, 1)
            ve.wait_ge(s_ewp, 5)
            ve.wait_ge(s_wenc, 2)
            ve.tensor_copy(Wenc[:, :].rearrange("c (h b) -> c h b", h=H)[:, :, 0:DH],
                           Wenc0[:, :].rearrange("c (h d) -> c h d", h=H)).then_inc(s_ewp, 1)
            for at, n in ((0, 0), (3, 1), (6, 0), (9, 2), (12, 0), (15, 1)):
                ve.tensor_copy(ew_parts[:, :, :, at:at + 3],
                               ew_p[:, n, :, 0:3].unsqueeze(2).broadcast_to([K, KC, EQ, 3])).then_inc(s_ewp, 1)
            for n in range(NP):
                ve.tensor_copy(ew_parts[:, :, :, 18 + n:19 + n],
                               ew_p[:, n, :, 3:4].unsqueeze(2).broadcast_to([K, KC, EQ, 1])).then_inc(s_ewp, 1)
            for part in range(LOADS):
                ve.wait_ge(s_xload[part], 16)
                part_stats(part, part)
            rsqrt_all(0)
            ve.wait_ge(s_setup_pe, 2 * KC + 1)
            for ki in range(KC):
                blocks = Wnode[:, ki, 0:HD].rearrange("p (h b) -> p h b", h=H)
                ve.tensor_copy(blocks[:, :, 0:DH], bank[ki][:, 0:D].rearrange("p (h d) -> p h d", h=H)
                               ).then_inc(s_setup_ve, 1)
                ve.tensor_copy(blocks[:, :, DH:HB], bank[2 + ki][:, H:2 * H].unsqueeze(2)).then_inc(s_setup_ve, 1)
                ve.tensor_copy(Wnode[:, ki, HD:HR], bank[2 + ki][:, 0:H]).then_inc(s_setup_ve, 1)
            ve.tensor_copy(WqT[:, :], bank[4][:, 0:D]).then_inc(s_setup_ve, 1)
            ve.wait_ge(s_setup_pe, 2 * KC + 2)
            ve.tensor_copy(WencP[:, :].rearrange("p (h b) -> p h b", h=H)[:, :, 0:DH],
                           bank[5][:, 0:K].bitcast(BF16).rearrange("p (h d) -> p h d", h=H)).then_inc(s_setup_ve, 1)

            def normal_tile(t, par):
                ve.wait_ge(s_xnT, t + 1)
                normalise(xn[:, par, :], t).then_inc(s_xn, 1)

            def kv_rows(t, par):
                ve.wait_ge(s_rows, t + 3)
                ve.tensor_copy(KV[:, bass.ds(t, 1), :].rearrange("p a f -> p (a f)"),
                               bank[4 + par][0:T, 0:2 * QK]).then_inc(s_kv, 1)
                ve.wait_ge(s_kmax, t + 2)
                ve.tensor_tensor(kmax[:, :], kmax[:, :], bank[4 + par][0:T, 0:QK], ALU.max).then_inc(s_kmax, 1)

            def split_rows(t, par):
                ve.wait_ge(s_hrow, t + 3)
                ve.wait_ge(s_wp, t + 1)
                ve.tensor_tensor(wres[:, par, :], hrow[:, par, 0:HD], wrow[:, par, 0, :], ALU.subtract).then_inc(s_wv, 1)
                ve.wait_ge(s_wv, 4 * t + 9)
                ve.tensor_copy(wrow[:, par, 1, :], wres[:, par, :]).then_inc(s_wv, 1)
                ve.wait_ge(s_wv, 4 * t + 10)
                ve.tensor_tensor(wres[:, par, :], wres[:, par, :], wrow[:, par, 1, :], ALU.subtract).then_inc(s_wv, 1)
                ve.wait_ge(s_wv, 4 * t + 11)
                ve.tensor_copy(wrow[:, par, 2, :], wres[:, par, :]).then_inc(s_wv, 1)

            normal_tile(0, 0)
            with ve.Fori(0, NT // 2 - 1) as i:
                for par in range(2):
                    normal_tile(2 * i + par + 1, 1 - par)
                    kv_rows(2 * i + par, par)
                    split_rows(2 * i + par, par)
            normal_tile(NT - 1, 1)
            for par in range(2):
                kv_rows(NT - 2 + par, par)
                split_rows(NT - 2 + par, par)

            ve.wait_ge(s_kmp, 1)
            ve.tensor_reduce(kmaxT[:, :], bank[0][:, 0:T], AX.X, ALU.max).then_inc(s_km, 1)
            ve.wait_ge(s_kmp, 2)
            ve.tensor_scalar(nkmax[:, :], bank[1][0:1, 0:K], -1.0, None, ALU.mult).then_inc(s_km, 1)
            ve.wait_ge(s_kmp, 3)
            ve.tensor_copy(nkmaxB[:, :], bank[2][0:T, 0:QK]).then_inc(s_km, 1)
            ve.wait_ge(s_km, 3)
            ve.wait_ge(s_kv, NT)
            with ve.Fori(0, NT // 10) as i:
                part = KV[:, bass.ds(10 * i, 10), 0:QK]
                ve.tensor_tensor(part, part, nkmaxB[:, :].unsqueeze(1).broadcast_to([T, 10, QK]),
                                 ALU.add).then_inc(s_kshift, 1)
            ve.wait_ge(s_fold_p, 1)
            ve.reciprocal(ksum[:, :], bank[7][:, 0:1]).then_inc(s_fold_v, 1)
            ve.wait_ge(s_fold_v, 1)
            for a in range(QK // MD):
                q = slice(a * MD, (a + 1) * MD)
                ve.tensor_scalar(ctxn[q, q], bank[6][q, q], ksum[q, :], MD ** -0.5,
                                 ALU.mult, ALU.mult).then_inc(s_fold_v, 1)
            ve.wait_ge(s_fold_p, 2)
            ve.tensor_copy(ctxT[:, :], bank[4][:, 0:QK]).then_inc(s_fold_v, 1)
            ve.wait_ge(s_fold_p, 3)
            ve.tensor_copy(ctxWo[:, :], bank[5][:, 0:D]).then_inc(s_fold_v, 1)
            ve.wait_ge(s_fold_p, 4)
            for k in range(KC):
                ve.tensor_copy(Wmix[:, k, :], bank[2 + k][:, 0:D]).then_inc(s_fold_v, 1)
            ve.tensor_tensor(bias_row[:, :], bias_rows[:, 0, :], bias_rows[:, 1, :], ALU.add).then_inc(s_fold_v, 1)
            with ve.Fori(0, NT // 2) as i:
                for par in range(2):
                    t = 2 * i + par
                    ve.wait_ge(s_mix, t + 3)
                    tile = X[:, bass.ds(t, 1), :].rearrange("p a f -> p (a f)")
                    ve.tensor_tensor(tile, tile, bank[par][0:T, 0:D], ALU.add).then_inc(s_mixed, 1)

            def any_order():
                with ve.Fori(0, ET) as t:
                    ve.wait_ge(g_dst, 16 * t + 16)
                    ve.tensor_copy(dst_f[:, :], dst_i[:, :]).then_inc(g_v, 1)
                    ve.wait_ge(g_p, p_done("dstT", t))
                    ve.wait_ge(g_v, v_done("dstf", t))
                    ve.tensor_scalar(same[:, :], bank[0][0:T, 0:T], dst_f[:, :], None, ALU.is_equal).then_inc(g_v, 1)
                    ve.wait_ge(g_p, p_done("eaTp", t))
                    ve.tensor_copy(eaT[:, :], bank[1][0:4, 0:T]).then_inc(g_v, 1)
                    ve.wait_ge(g_v, v_done("same", t))
                    ve.tensor_scalar(apart[:, :], same[:, :], 1.0, -LOW, ALU.subtract, ALU.mult).then_inc(g_v, 1)
                    ve.tensor_tensor(before[:, :], same[:, :], lower[:, :], ALU.mult).then_inc(g_v, 1)
                    ve.wait_ge(g_v, v_done("before", t))
                    ve.tensor_reduce(nbefore[:, :], before[:, :], AX.X, ALU.max).then_inc(g_v, 1)
                    ve.tensor_tensor(to_f[:, :], spare[:, :], dst_f[:, :], ALU.subtract).then_inc(g_v, 1)
                    ve.wait_ge(g_v, v_done("gap", t))
                    ve.wait_ge(g_v, v_done("nbefore", t))
                    ve.tensor_tensor(to_f[:, :], to_f[:, :], nbefore[:, :], ALU.mult).then_inc(g_v, 1)
                    ve.wait_ge(g_v, v_done("sel", t))
                    ve.tensor_tensor(to_f[:, :], to_f[:, :], dst_f[:, :], ALU.add).then_inc(g_v, 1)
                    ve.wait_ge(g_v, v_done("tof", t))
                    ve.tensor_copy(to_i[:, :], to_f[:, :]).then_inc(g_v, 1)
                    ve.wait_ge(g_p, p_done("enc", t))
                    ve.wait_ge(g_Gs, 16 * t + 16)
                    ve.wait_ge(g_Gd, 16 * t + 16)
                    ve.wait_ge(g_S0, 16 * t + 16)
                    ve.scalar_tensor_tensor(out=prod[:, :], in0=bank[2][0:T, 0:HD], scalar=0.0, in1=Gd[:, 0:HD],
                                            op0=ALU.max, op1=ALU.mult).then_inc(g_v, 1)
                    ve.wait_ge(g_v, v_done("prod", t))
                    ve.tensor_reduce(score[:, :], prod[:, :].rearrange("p (h b) -> p h b", h=H), AX.X,
                                     ALU.add).then_inc(g_v, 1)
                    ve.wait_ge(g_v, v_done("a1", t))
                    ve.tensor_tensor(score[:, :], score[:, :], Gs[:, HD:HR], ALU.add).then_inc(g_v, 1)
                    ve.wait_ge(g_v, v_done("a2", t))
                    ve.scalar_tensor_tensor(out=score2[:, :], in0=score[:, :], scalar=0.2, in1=score[:, :],
                                            op0=ALU.mult, op1=ALU.max).then_inc(g_v, 1)
                    ve.wait_ge(g_v, v_done("score", t))
                    ve.tensor_tensor(spread[:, :, :], score2[:, :].unsqueeze(2).broadcast_to([T, H, T]),
                                     ident[0:T, 0:T].unsqueeze(1).broadcast_to([T, H, T]), ALU.mult).then_inc(g_v, 1)
                    ve.wait_ge(g_p, p_done("spreadB", t))
                    ve.wait_ge(g_v, v_done("apart", t))
                    for b in range(2):
                        ve.tensor_tensor(masked[:, 4 * b:4 * b + 4, :],
                                         bank[3 + b][0:T, 0:4 * T].rearrange("p (h e) -> p h e", h=4),
                                         apart[:, :].unsqueeze(1).broadcast_to([T, 4, T]), ALU.add).then_inc(g_v, 1)
                    ve.wait_ge(g_v, v_done("masked", t))
                    ve.tensor_reduce(tmax[:, :], masked[:, :, :], AX.X, ALU.max).then_inc(g_v, 1)
                    ve.wait_ge(g_v, v_done("tmax", t))
                    ve.tensor_tensor(S1[:, HD:SR], tmax[:, :], S0[:, HD:SR], ALU.max).then_inc(g_v, 1)
                    ve.wait_ge(g_v, v_done("newmax", t))
                    ve.tensor_tensor(shifted[:, 0:H], score2[:, :], S1[:, HD:SR], ALU.subtract).then_inc(g_v, 1)
                    ve.tensor_tensor(shifted[:, H:2 * H], S0[:, HD:SR], S1[:, HD:SR], ALU.subtract).then_inc(g_v, 1)
                    ve.wait_ge(g_ew, t + 1)
                    msg_blocks = msg[:, :].rearrange("p (h b) -> p h b", h=H)
                    ve.tensor_tensor(msg_blocks[:, :, 0:DH], Gs[:, 0:HD].rearrange("p (h b) -> p h b", h=H)[:, :, 0:DH],
                                     ew[:, 0:H].unsqueeze(2).broadcast_to([T, H, DH]), ALU.mult).then_inc(g_v, 1)
                    ve.tensor_copy(msg_blocks[:, :, DH:HB], ew[:, 0:H].unsqueeze(2)).then_inc(g_v, 1)
                    ve.tensor_tensor(S1[:, 0:HD].rearrange("p (h b) -> p h b", h=H),
                                     S0[:, 0:HD].rearrange("p (h b) -> p h b", h=H),
                                     ew[:, H:2 * H].unsqueeze(2).broadcast_to([T, H, HB]), ALU.mult).then_inc(g_v, 1)
                    ve.wait_ge(g_v, v_done("keep", t))
                    ve.wait_ge(g_p, p_done("sum", t))
                    ve.tensor_tensor(S1[:, 0:HD], S1[:, 0:HD], bank[5][0:T, 0:HD], ALU.add).then_inc(g_v, 1)
                    ve.wait_ge(g_scatter, 16 * t + 16)
                    ve.sem_inc(g_done, 1)


            def in_groups():
                spread_h, small, turned = bank[2:4], bank[6], bank[7]

                def onehot(gx, px, b):
                    if b == 0:
                        ve.wait_ge(f_agg, VN * gx + VN)
                    loc = col_loc[:, bass.ds(J * gx + BT * b, BT)]
                    ve.tensor_tensor(M[:, px, BT * b:BT * (b + 1), :], iota_w[:, :].unsqueeze(1).broadcast_to([T, BT, W]),
                                     loc.unsqueeze(2).broadcast_to([T, BT, W]), ALU.is_equal).then_inc(f_M, 1)

                def product(gx, px, j):
                    n = (px + j) % 2
                    ve.wait_ge(f_relu, J * gx + j + 3)
                    ve.wait_ge(f_hd, J * gx + j + 1 + 2 * J)
                    ve.wait_ge(f_red, J * gx + j + 1)
                    ve.tensor_tensor(pr[:, n, :], er[:, n, :], spread_h[n][0:T, 0:HD], ALU.mult).then_inc(f_prod, 1)

                def add_up(gx, px, j):
                    n = (px + j) % 2
                    ve.wait_ge(f_prod, J * gx + j + 3)
                    ve.tensor_reduce(al[:, px, j, :], pr[:, n, :].rearrange("p (h b) -> p h b", h=H), AX.X,
                                     ALU.add).then_inc(f_red, 1)

                def scores(gy, py, ky):
                    ve.wait_ge(f_red, J * gy + J + 2)
                    ve.wait_ge(f_G[py], 16 * J * ky + 16 * J)
                    ve.tensor_tensor(alx[:, :, :], al[:, py, :, :], Gr[:, py, :, HD:HR], ALU.add).then_inc(f_al0, 1)
                    ve.wait_ge(f_al0, gy + 1)
                    ve.scalar_tensor_tensor(out=alL[:, :, :], in0=alx[:, :, :], scalar=0.2, in1=alx[:, :, :],
                                            op0=ALU.mult, op1=ALU.max).then_inc(f_al, 1)

                def running_maxima(gy, py):
                    ve.wait_ge(f_C1, gy + 1)
                    ve.tensor_tensor_scan(Fs[:, :], penT[:, py, :], small[0:J * H, 0:T], LOW, ALU.add,
                                          ALU.max).then_inc(f_scan, 1)

                def keep_last(gy, py):
                    ve.wait_ge(f_C2, gy + 1)
                    ve.wait_ge(f_last, gy + 1)
                    ve.tensor_tensor(Fm[:, py, :, 0:H], small[0:T, 0:J * H].rearrange("p (j h) -> p j h", h=H),
                                     Fm[:, py, :, H:H + 1].broadcast_to([T, J, H]), ALU.mult).then_inc(f_Fm, 1)
                    went_on = straddle[0:1, bass.ds(gy, 1)]
                    ve.wait_ge(f_craw, gy + 3)
                    ve.tensor_scalar(cmr[:, 0:H], c_raw[:, HD:SR], went_on, None, ALU.mult).then_inc(f_cm, 1)
                    ve.tensor_copy(cmr[:, H:H + 1], went_on).then_inc(f_cm, 1)

                def window_maxima(gy):
                    by_tile = small[:, 0:(H + 1) * (J + 1)].rearrange("p (j c) -> p j c", c=H + 1)
                    ve.wait_ge(f_C3, gy + 1)
                    ve.tensor_scalar(pres[:, :].unsqueeze(2), by_tile[:, :, H:H + 1], 1.0, -LOW, ALU.subtract,
                                     ALU.mult).then_inc(f_w, 1)
                    ve.wait_ge(f_w, 8 * gy + 1)
                    ve.tensor_tensor(wmx[:, :, :], by_tile[:, :, 0:H], pres[:, :].unsqueeze(2)
                                     .broadcast_to([W, J + 1, H]), ALU.add).then_inc(f_w, 1)
                    ve.wait_ge(f_w, 8 * gy + 2)
                    ve.tensor_reduce(mW[:, :], wmx[:, :, :].rearrange("p j h -> p h j"), AX.X, ALU.max).then_inc(f_w, 1)
                    ve.wait_ge(f_w, 8 * gy + 3)
                    ve.tensor_copy(mWp[:, :, 0:1], mW[:, :].unsqueeze(2)).then_inc(f_w, 1)
                    ve.tensor_tensor(c_dif[:, :], c_raw[:, HD:SR], mW[0:1, :], ALU.subtract).then_inc(f_dif, 1)
                    ve.wait_ge(f_w, 8 * gy + 4)
                    ve.tensor_tensor(mWr[:, :].unsqueeze(2), mW[:, :].unsqueeze(2), mWp[:, :, 0:1],
                                     ALU.subtract).then_inc(f_w, 1)
                    ve.wait_ge(f_w, 8 * gy + 5)
                    ve.tensor_copy(mWp[:, :, 1:2], mWr[:, :].unsqueeze(2)).then_inc(f_w, 1)
                    ve.wait_ge(f_dif, 2 * gy + 1)
                    ve.tensor_scalar(c_dif[:, :], c_dif[:, :], 0.0, None, ALU.min).then_inc(f_dif, 1)
                    ve.wait_ge(f_w, 8 * gy + 6)
                    ve.tensor_tensor(mWr[:, :].unsqueeze(2), mWr[:, :].unsqueeze(2), mWp[:, :, 1:2],
                                     ALU.subtract).then_inc(f_w, 1)
                    ve.wait_ge(f_w, 8 * gy + 7)
                    ve.tensor_copy(mWp[:, :, 2:3], mWr[:, :].unsqueeze(2)).then_inc(f_w, 1)

                def shift(gy):
                    ve.wait_ge(f_C4, gy + 1)
                    ve.tensor_reduce(mE[:, :], small[0:T, 0:J * H * NP].rearrange("p (m n) -> p m n", n=NP), AX.X,
                                     ALU.add).then_inc(f_mE, 1)
                    ve.wait_ge(f_mE, gy + 2)
                    ve.tensor_tensor(dsh[:, :], alL[:, :, :].rearrange("p j h -> p (j h)"), mE[:, :],
                                     ALU.subtract).then_inc(f_dsh, 1)

                def messages(gy, py, piece):
                    ve.wait_ge(f_exp, gy + 1)
                    rows = Gr[:, py, VT * piece:VT * (piece + 1), 0:HD].rearrange("p j (h b) -> p j h b", h=H)
                    ve.tensor_tensor(rows[:, :, :, 0:DH], rows[:, :, :, 0:DH],
                                     rows[:, :, :, DH:HB].broadcast_to([T, VT, H, DH]), ALU.mult).then_inc(f_v, 1)

                def carried(gy):
                    ve.wait_ge(f_fac, gy + 1)
                    ve.tensor_scalar(c_fs[:, :], c_fac[:, :], straddle[0:1, bass.ds(gy, 1)], None,
                                     ALU.mult).then_inc(f_fs, 1)
                    ve.wait_ge(f_fs, gy + 1)
                    ve.wait_ge(f_agg, VN * gy + 6)
                    ve.tensor_tensor(crow[:, :].rearrange("p (h b) -> p h b", h=H),
                                     c_raw[:, 0:HD].rearrange("p (h b) -> p h b", h=H),
                                     c_fs[:, :].unsqueeze(2).broadcast_to([1, H, HB]), ALU.mult).then_inc(f_crow, 1)

                def last_node(gy):
                    ve.wait_ge(f_C5, gy + 1)
                    ve.wait_ge(f_crow, gy + 1)
                    ve.tensor_copy(c_raw[:, :], turned[0:1, 0:SR]).then_inc(f_craw, 1)

                def step(gx, px, kx, gy, py, ky, last=False):
                    if gx is not None:
                        onehot(gx, px, 0)
                        onehot(gx, px, 1)
                    if gy is not None:
                        scores(gy, py, ky)
                    for j in range(J):
                        if gx is not None:
                            product(gx, px, j)
                            if j:
                                add_up(gx, px, j - 1)
                        if gx is not None and j in (0, 3, 6):
                            onehot(gx, px, j // 3 + 2)
                        if gy is not None and j == 1:
                            running_maxima(gy, py)
                        if gy is not None and j == 3:
                            keep_last(gy, py)
                        if gy is not None and j == 5:
                            window_maxima(gy)
                        if gy is not None and j == 7:
                            shift(gy)
                        if gy is not None and j in (9, 11, 13):
                            messages(gy, py, (j - 9) // 2)
                        if gy is not None and j == 13:
                            carried(gy)
                    if gx is not None:
                        add_up(gx, px, J - 1)
                    if gy is not None:
                        last_node(gy)

                step(0, 0, 0, None, None, None)
                with ve.Fori(0, G // 2 - 1) as i:
                    step(2 * i + 1, 1, i, 2 * i, 0, i)
                    step(2 * i + 2, 0, i + 1, 2 * i + 1, 1, i)
                step(G - 1, 1, G // 2 - 1, G - 2, 0, G // 2 - 1, last=True)
                step(None, None, None, G - 1, 1, G // 2 - 1)

            steps = 0

            def did(ins, s=f_natd):
                nonlocal steps
                ins.then_inc(s, 1)
                steps += 1
                ve.wait_ge(s, steps)

            ve.wait_ge(s_initst, 16)
            ve.wait_ge(f_pad, 16)
            ve.wait_ge(f_nat[0], 16)
            ve.wait_ge(f_nat[1], 16)
            did(ve.memset(nat_f[:, 0:1], -1.0))
            did(ve.memset(nat_f[:, GE + 1:GE + 2], -1.0))
            did(ve.tensor_copy(nat_f[:, 1:GE + 1], nat_dst[:, :].bitcast(I32)))
            did(ve.tensor_copy(nat_nextf[:, :], nat_next[:, :]))
            did(ve.tensor_tensor(nat_dst[:, 0:GE - 1], nat_f[:, 2:GE + 1], nat_f[:, 1:GE], ALU.subtract))
            did(ve.tensor_reduce(nat_gap[:, 0:1], nat_dst[:, 0:GE - 1], AX.X, ALU.min))
            did(ve.tensor_tensor(nat_gap[:, 1:2], nat_nextf[:, :], nat_f[:, GE:GE + 1], ALU.subtract))
            did(ve.tensor_tensor(nat_str[:, :], nat_nextf[:, :], nat_f[:, GE:GE + 1], ALU.is_equal))
            did(ve.tensor_tensor(nat_loc[:, :], nat_f[:, GE:GE + 1], nat_f[:, 1:2], ALU.subtract))
            did(ve.tensor_scalar(nat_gap[:, 2:3], nat_loc[:, :], -1.0, float(W - 1), ALU.mult, ALU.add))
            did(ve.tensor_reduce(nat_ok[:, :], nat_gap[:, 0:3], AX.X, ALU.min))
            did(ve.tensor_scalar(nat_dst[:, :], nat_f[:, 1:GE + 1], nat_f[:, 1:2], None, ALU.subtract))
            did(ve.tensor_tensor(nat_new[:, :], nat_f[:, 1:GE + 2], nat_f[:, 0:GE + 1], ALU.not_equal))
            did(ve.memset(nat_new[:, 0:GE + 1:T], 1.0))
            ve.wait_ge(f_nat[2], 16)
            did(ve.tensor_copy(nat_src[:, :], nat_src[:, :].bitcast(I32)))
            assert steps == NAT_STEPS
            ve.wait_ge(f_rows, 1)
            ve.tensor_reduce(ok[:, 0:1], bank[6][0:1, 0:G], AX.X, ALU.min).then_inc(f_natd, 1)
            ve.wait_ge(f_natd, NAT_STEPS + 1)
            ve.tensor_scalar(ok_i[:, :], ok[:, 0:1], 0.0, None, ALU.is_ge).then_inc(f_ok, 1)
            ve.tensor_copy(base_i[:, :], bank[6][0:1, 128:128 + G]).then_inc(f_ok, 1)
            ve.tensor_copy(straddle[:, 1:G + 1], bank[6][0:1, 256:256 + G]).then_inc(f_ok, 1)
            ve.tensor_scalar(last_hot[:, :], bank[6][:, 384:384 + G], iota_p[:, :], None,
                             ALU.is_equal).then_inc(f_ok, 1)
            for n in COLUMNS_VEC:
                ve.wait_ge(f_turn, n + 1)
                kind, dest, _, scale = column_batches[n]
                ve.tensor_scalar(dest, bank[n % 4][0:T, 0:G * dest.shape[1]].rearrange("p (j g) -> p j g", g=G),
                                 scale, None, ALU.mult).then_inc(f_colv, 1)
            ve.wait_ge(f_cola, COLA)
            ve.wait_ge(f_colv, COLV)

            ve.wait_ge(f_ok, 4)
            grouped = ve.value_load(ok_i[0:1, 0:1], min_val=0, max_val=1)
            with ve.If(grouped == 1):
                in_groups()
            with ve.Else():
                any_order()

            with ve.Fori(0, NT // 2) as i:
                for par in range(2):
                    t = 2 * i + par
                    ve.wait_ge(s_st[par], 16 * i + 16)
                    sums = st[:, par, 0:HD].rearrange("p (h b) -> p h b", h=H)
                    ve.tensor_scalar(den[:, par, :].unsqueeze(2), sums[:, :, DH:HB], 1e-10, None,
                                     ALU.max).then_inc(s_den, 1)
                    ve.wait_ge(s_den, t + 1)
                    ve.reciprocal(rden[:, par, :], den[:, par, :]).then_inc(s_rden, 1)
                    ve.wait_ge(s_rden, t + 1)
                    ve.tensor_tensor(agg[:, par, :].rearrange("p (h d) -> p h d", h=H),
                                     sums[:, :, 0:DH],
                                     rden[:, par, :].unsqueeze(2).broadcast_to([T, H, DH]), ALU.mult).then_inc(s_agg, 1)
                    ve.wait_ge(s_agg, t + 1)
                    tile = X[:, bass.ds(t, 1), :].rearrange("p a f -> p (a f)")
                    ve.tensor_tensor(tile, tile, agg[:, par, :], ALU.add).then_inc(s_x1, 1)
            ve.wait_ge(s_x1, NT + 2)
            with ve.Fori(0, LOADS) as i:
                part_stats(i, LOADS + i)
            rsqrt_all(1)
            with ve.Fori(0, NT // 2) as i:
                for par in range(2):
                    t = 2 * i + par
                    ve.wait_ge(s_yT, t + 1)
                    normalise(xn[:, par, :], t).then_inc(s_yr, 1)
            ve.wait_ge(s_yTr, NT + 2)
            ve.tensor_reduce(ysum[:, :], xnT[:, :, :], AX.X, ALU.add).then_inc(s_ysum, 1)

            steps = 0

            def done(ins):
                nonlocal steps
                ins.then_inc(s_r, 1)
                steps += 1
                ve.wait_ge(s_r, steps)

            def softmax(a, top_, shifted_, e, total, rtotal, w, turn_):
                done(ve.tensor_reduce(top_[:, :], a[:, :], AX.X, ALU.max))
                ve.tensor_scalar(shifted_[:, :], a[:, :], top_[:, :], None, ALU.subtract).then_inc(s_ra, 1)
                ve.wait_ge(s_ra, turn_)
                done(ve.tensor_reduce(total[:, :], e[:, :], AX.X, ALU.add))
                done(ve.reciprocal(rtotal[:, :], total[:, :]))
                done(ve.tensor_scalar(w[:, :], e[:, :], rtotal[:, :], None, ALU.mult))

            ve.wait_ge(s_rp, 1)
            done(ve.scalar_tensor_tensor(out=r["tmp"][:, :], in0=bank[2][0:1, 0:X8], scalar=1.0 / N, in1=br[:, :],
                                         op0=ALU.mult, op1=ALU.add))
            softmax(r["tmp"], rs["max"], r["logits"], r["exp"], rs["sum"], rs["rsum"], r["w"], 2)
            done(ve.tensor_scalar(r["load"][:, :], r["w"][:, :], float(N), None, ALU.mult))
            done(ve.reciprocal(r["cap"][:, :], r["load"][:, :]))
            done(ve.tensor_scalar(r["cap"][:, :], r["cap"][:, :], CAPACITY, 1.0, ALU.mult, ALU.min))
            done(ve.tensor_tensor(r["load"][:, :], r["w"][:, :], r["cap"][:, :], ALU.mult))
            softmax(r["load"], rs["max2"], r["tmp"], r["exp2"], rs["sum2"], rs["rsum2"], r["w2"], 4)
            w_i = r["w2"][:, :].unsqueeze(2).broadcast_to([1, X8, X8])
            w_j = r["w2"][:, :].unsqueeze(1).broadcast_to([1, X8, X8])
            done(ve.tensor_tensor(pair[:, :, :], w_j, w_i, ALU.is_equal))
            done(ve.tensor_tensor(pair[:, :, :], pair[:, :, :], tri8[:, :, :], ALU.mult))
            done(ve.tensor_tensor(pair2[:, :, :], w_j, w_i, ALU.is_gt))
            done(ve.tensor_tensor(pair[:, :, :], pair[:, :, :], pair2[:, :, :], ALU.add))
            done(ve.tensor_reduce(r["rank"][:, :], pair[:, :, :], AX.X, ALU.add))
            for n in range(TOP):
                done(ve.tensor_scalar(r["first"][:, :], r["rank"][:, :], float(n), None, ALU.is_equal))
                done(ve.tensor_tensor(r["second"][:, :], r["first"][:, :], r["num"][:, :], ALU.mult))
                done(ve.tensor_reduce(topi[:, n:n + 1], r["second"][:, :], AX.X, ALU.add))
                done(ve.tensor_tensor(r["second"][:, :], r["first"][:, :], r["w2"][:, :], ALU.mult))
                done(ve.tensor_reduce(top[:, n:n + 1], r["second"][:, :], AX.X, ALU.add))
            ve.tensor_copy(topi_i[:, :], topi[:, :]).then_inc(s_topi, 1)
            ve.tensor_tensor(rs["diff"][:, :], top[:, 1:2], top[:, 0:1], ALU.subtract).then_inc(s_ra, 1)
            ve.wait_ge(s_ra, 6)
            done(ve.tensor_scalar(rs["e1"][:, :], rs["e"][:, :], 1.0, None, ALU.add))
            done(ve.reciprocal(topw[:, 0:1], rs["e1"][:, :]))
            ve.tensor_tensor(topw[:, 1:2], topw[:, 0:1], rs["e"][:, :], ALU.mult).then_inc(s_w2s, 1)
            ve.wait_ge(s_rp, 2)
            ve.tensor_copy(topwB[:, :], bank[3][:, 0:TOP]).then_inc(s_w2s, 1)
            ve.wait_ge(s_w2s, 2)
            ve.wait_ge(s_wx, 8 * 16)
            for n in range(TOP):
                ve.tensor_scalar(W2[:, n, :, :], W2[:, n, :, :], topwB[:, n:n + 1], None, ALU.mult).then_inc(s_w2s, 1)
                ve.tensor_scalar(b2[:, n, :], b2[:, n, :], topw[:, n:n + 1], None, ALU.mult).then_inc(s_w2s, 1)
            ve.wait_ge(s_w2s, 6)
            ve.tensor_tensor(bias_row[:, :], b2[:, 0, :], b2[:, 1, :], ALU.add).then_inc(s_w2s, 1)

            def outputs(c, cp, first=False):
                for half in range(2):
                    t = 2 * c + half
                    ve.wait_ge(s_l2, t + 5)
                    normalise(yrow[:, half, :], t).then_inc(s_yrow, 1)
                    ve.wait_ge(s_yrow, t + 1)
                    ve.tensor_tensor(z[:, half, :], yrow[:, half, :], bank[4 + 2 * cp + half][0:T, 0:D],
                                     ALU.add).then_inc(s_z, 1)
                    ve.wait_ge(s_z, t + 5)
                    ve.sem_inc(s_passed, 1)
                    ve.bn_stats(stats[:, half, :], z[:, half, :]).then_inc(s_zst, 1)
                    ve.wait_ge(s_zst, t + 1)
                    ve.sem_inc(s_passed, 1)
                    ve.bn_aggr(zmv[:, half, :], stats[:, half, :]).then_inc(s_zmv, 1)
                ve.wait_ge(s_zmv, 2 * c + 2)
                ve.tensor_scalar(zsd[:, :], zmv[:, :, 1:2].rearrange("p t a -> p (t a)"), EPS, None,
                                 ALU.add).then_inc(s_zvar, 1)
                ve.wait_ge(s_zsd, c + 1)
                ve.reciprocal(zr[:, :], zsd[:, :]).then_inc(s_zr, 1)
                ve.wait_ge(s_zr, c + 1)
                for half in range(2):
                    t = 2 * c + half
                    if not first:
                        ve.wait_ge(s_out[half], 16 * c)
                    ve.tensor_scalar(res[:, half, :], z[:, half, :], zmv[:, half, 0:1], zr[:, half:half + 1],
                                     ALU.subtract, ALU.mult).then_inc(s_n1, 1)
                    ve.wait_ge(s_n1, t + 1)
                    ve.tensor_tensor(res[:, half, :], res[:, half, :], gamma[:, :], ALU.mult).then_inc(s_n2, 1)
                    ve.wait_ge(s_n2, t + 1)
                    ve.tensor_tensor(res[:, half, :], res[:, half, :], beta[:, :], ALU.add).then_inc(s_n3, 1)
                    ve.wait_ge(s_n3, t + 1)
                    ve.tensor_tensor(res[:, half, :], res[:, half, :],
                                     X[:, bass.ds(t, 1), :].rearrange("p a f -> p (a f)"), ALU.add).then_inc(s_res, 1)

            outputs(0, 0, first=True)
            with ve.Fori(0, NCH // 2) as i:
                for cp in range(2):
                    outputs(2 * i + cp + 1, 1 - cp)


_INS = ["x", "src", "dst", "edge_attr_3", "L0_gnn_W", "L0_gnn_a_src", "L0_gnn_a_dst", "L0_gnn_edge_W",
        "L0_gnn_edge_b", "L0_gnn_bias", "L0_mix_W_qkv", "L0_mix_W_out", "L0_mix_b_out", "L0_ffn_Wr",
        "L0_ffn_br", "L0_ffn_W1", "L0_ffn_b1", "L0_ffn_W2", "L0_ffn_b2", "L0_ffn_gamma", "L0_ffn_beta"]


def kernel(**inputs):
    import numpy as _np
    import concourse.bacc as _bacc
    from concourse.bass_utils import run_bass_kernel_spmd as _run

    nc = _bacc.Bacc("TRN2", target_bir_lowering=False, num_devices=1)
    arrays, args = {}, []
    for name in _INS:
        a = _np.ascontiguousarray(inputs[name])
        arrays[f"in_{name}"] = a
        args.append(nc.dram_tensor(f"in_{name}", a.shape, mybir.dt.from_np(a.dtype), kind="ExternalInput").ap())
    out = nc.dram_tensor("out_0", (N, D), F32, kind="ExternalOutput").ap()
    gps_block(nc, *args, out)
    r = _run(nc, [arrays], core_ids=[0])
    return r.results[0]["out_0"]
```

```python
from contextlib import ExitStack
import math

import concourse.bass as bass
from concourse import mybir

F32 = mybir.dt.float32
BF16 = mybir.dt.bfloat16
I32 = mybir.dt.int32
ALU = mybir.AluOpType
ACT = mybir.ActivationFunctionType
AX = mybir.AxisListType

N, D = 6250, 256
E = 206250
H, DH = 8, 32
T = 125
NT = N // T
ET = E // T
K = 128
KC = D // K
HB = DH + 1
HD = H * HB
HR = HD + H
SR = HD + H
J = 15
GE = J * T
G = E // GE
W = 128
BT = 3
BN = J // BT
VT = 3
VN = J // VT
EQ = 4
EB = (J + EQ - 1) // EQ
EK = 32
NP = 3
QK = 128
MD = 32
X8 = 8
FF = 512
FC = FF // K
TOP = 2
CH = 2 * T
NCH = N // CH
LOADS = 10
PER_LOAD = NT // LOADS
EPS = 1e-5
LOW = -3.0e38
BREAK = -1.0e38
JR = J + 1
CAPACITY = float(math.ceil(N * 1.25 / X8))


def gps_block(nc, x, src, dst, edge_attr_3, L0_gnn_W, L0_gnn_a_src, L0_gnn_a_dst, L0_gnn_edge_W,
              L0_gnn_edge_b, L0_gnn_bias, L0_mix_W_qkv, L0_mix_W_out, L0_mix_b_out, L0_ffn_Wr,
              L0_ffn_br, L0_ffn_W1, L0_ffn_b1, L0_ffn_W2, L0_ffn_b2, L0_ffn_gamma, L0_ffn_beta, out):
    assert N % T == 0 and E % GE == 0 and NT % 2 == 0 and NCH % 2 == 1 and G % 2 == 0 and W <= 2 * T

    node_table = nc.dram_tensor("node_table", (N, HR), F32, kind="Internal").ap()
    state_table = nc.dram_tensor("state_table", (N + 2 * T, SR), F32, kind="Internal").ap()
    window_table = nc.dram_tensor("window_table", (N + 2 * T, NP * HD), BF16, kind="Internal").ap()

    with ExitStack() as ctx:
        ctx.enter_context(nc.allow_non_contiguous_dma(reason="weights of a few hundred elements"))

        def sb(name, shape, dt=F32):
            return ctx.enter_context(nc.sbuf_tensor(name, shape, dt))

        def sem(name):
            return ctx.enter_context(nc.semaphore(name))

        X = sb("X", [T, NT, D])
        xnT = sb("xnT", [K, KC, N])
        lent = xnT[:, :, :].rearrange("p k n -> p (k n)")
        shared = sb("shared", [K, NT * 2 * QK])
        KV = shared[0:T, :].rearrange("p (t f) -> p t f", t=NT)
        taken = 0

        def later(rows, shape, pattern, **sizes):
            nonlocal taken
            size = int(math.prod(shape))
            taken += size
            assert taken <= NT * 2 * QK
            return shared[0:rows, taken - size:taken].rearrange(pattern, **sizes)


        early = sb("early", [K, 4168])
        early_taken = 0

        def place(rows, shape, dt=F32, pattern=None, **sizes):
            nonlocal early_taken
            words = -(-int(math.prod(shape)) * (2 if dt == BF16 else 4) // 4)
            early_taken += words
            assert early_taken <= 4168
            view = early[0:rows, early_taken - words:early_taken]
            view = view if dt == F32 else view.bitcast(dt)
            return view.rearrange(pattern, **sizes) if pattern else view

        ident = sb("ident", [K, K])
        ones = sb("ones", [K, K])
        Wg = place(K, [KC, D], F32, "p (k f) -> p k f", k=KC)
        a_cols = sb("a_cols", [K, 2, KC])
        a_blocks = sb("a_blocks", [K, KC, 2 * H])
        Wnode = sb("Wnode", [K, KC, HR])
        Wenc = sb("Wenc", [4, HD])
        Wenc0 = place(4, [D])
        WencP = sb("WencP", [K, HD], BF16)
        ew_cols = sb("ew_cols", [K, KC, 4])
        ew_res = sb("ew_res", [K, KC, 4])
        ew_p = sb("ew_p", [K, NP, KC, 4], BF16)
        ew_parts = sb("ew_parts", [K, KC, EQ, EK], BF16)
        identb = sb("identb", [K, K], BF16)
        wrow_at = early_taken
        wrow = place(T, [2, NP, HD], BF16, "p (b n f) -> p b n f", b=2, n=NP)
        wres = place(T, [2, HD], F32, "p (b f) -> p b f", b=2)
        kexp = early[0:T, wrow_at:wrow_at + 10 * QK].rearrange("p (b j f) -> p b j f", b=2, j=5)
        assert wrow_at + 10 * QK <= early_taken
        Wqkv = sb("Wqkv", [K, KC, 3 * QK])
        WqT = place(QK, [D])
        Wo = place(QK, [D])
        biasB = place(T, [D])
        Wmix = place(K, [KC, D], F32, "p (k f) -> p k f", k=KC)
        bias_rows = sb("bias_rows", [1, 2, D])
        bias_row = sb("bias_row", [1, D])
        Wr = sb("Wr", [K, KC, X8])
        br = sb("br", [1, X8])
        gamma = sb("gamma", [T, D])
        beta = sb("beta", [T, D])
        b1 = sb("b1", [K, TOP, FC])

        stats = sb("stats", [T, PER_LOAD, 6])
        mvs = sb("mvs", [T, PER_LOAD, 2])
        mv = sb("mv", [T, NT, 2])
        rstd = sb("rstd", [T, NT])

        xn = sb("xn", [T, 2, D])
        xnTs = sb("xnTs", [K, 2, KC, T])
        hrow = place(T, [2, HR], F32, "p (b f) -> p b f", b=2)
        kmax = sb("kmax", [T, QK])
        kmaxT = sb("kmaxT", [QK, 1])
        nkmax = sb("nkmax", [1, QK])
        nkmaxB = sb("nkmaxB", [T, QK])
        ksum = sb("ksum", [QK, 1])
        ctxn = sb("ctxn", [QK, QK])
        ctxT = sb("ctxT", [QK, QK])
        ctxWo = place(QK, [D])
        onescol = sb("onescol", [T, 1])
        zrow = sb("zrow", [1, K])

        lower = sb("lower", [T, T])
        spare = sb("spare", [T, 1])
        src_i = sb("src_i", [T, 1], I32)
        dst_i = sb("dst_i", [T, 1], I32)
        dst_f = sb("dst_f", [T, 1])
        ea = sb("ea", [T, 4])
        eaT = sb("eaT", [4, T])
        Gs, Gd, S0, S1 = (later(T, [HR], "p f -> p f") for _ in range(4))
        same, apart, before = (later(T, [T], "p f -> p f") for _ in range(3))
        prod, msg = (later(T, [HD], "p f -> p f") for _ in range(2))
        score = sb("score", [T, H])
        score2 = sb("score2", [T, H])
        spread = later(T, [H, T], "p (h e) -> p h e", h=H)
        masked = later(T, [H, T], "p (h e) -> p h e", h=H)
        tmax = sb("tmax", [T, H])
        newmax = sb("newmax", [T, H])
        shifted = sb("shifted", [T, 2 * H])
        ew = sb("ew", [T, 2 * H])
        nbefore = sb("nbefore", [T, 1])
        to_f = sb("to_f", [T, 1])
        to_i = sb("to_i", [T, 1], I32)

        taken = 0
        nat_src = later(G, [GE], "p f -> p f")
        nat_dst = later(G, [GE], "p f -> p f")
        nat_ea = later(G, [3 * GE], "p f -> p f")
        nat_new = later(G, [GE], "p f -> p f")
        nat_next = sb("nat_next", [G, 1], I32)
        nat_nextf = sb("nat_nextf", [G, 1])
        nat_gap = sb("nat_gap", [G, 4])
        nat_ok = sb("nat_ok", [G, 1])
        nat_loc = sb("nat_loc", [G, 1])
        nat_str = sb("nat_str", [G, 1])
        base_i = sb("base_i", [1, G], I32)
        straddle = sb("straddle", [1, G + 1])
        ok = sb("ok", [1, 2])
        ok_i = sb("ok_i", [1, 1], I32)
        last_hot = sb("last_hot", [W, G])
        iota_p = sb("iota_p", [W, 1])
        C = G * J
        col_src = lent[0:T, 0:C].bitcast(I32)
        col_loc = lent[0:T, C:2 * C]
        col_new = lent[0:T, 2 * C:3 * C]
        rows_at = 3 * C
        any_new = lent[0:1, rows_at:rows_at + H * JR + 1]
        end_row = lent[0:1, rows_at + 256:rows_at + 256 + H * JR]
        head_row = lent[0:1, rows_at + 512:rows_at + 512 + H * JR]
        into_f = lent[0:1, rows_at + 768:rows_at + 768 + H * JR]
        into_b = lent[0:1, rows_at + 1024:rows_at + 1024 + H * JR + 1]
        col_ea = lent[0:T, 4 * C:7 * C]
        assert 1024 + H * JR < C and H * JR == K
        taken = 0
        early_taken = 0
        Gr = later(T, [2, J, HR], "p (b j f) -> p b j f", b=2, j=J)
        M = later(T, [2, J, W], "p (b j w) -> p b j w", b=2, j=J)
        MT_mem = sb("MT_mem", [W, 2 * J * T + 10], BF16)
        zpad = MT_mem[0:T, 0:NP * HD]
        init_row = MT_mem[0:T, NP * HD:NP * HD + 2 * SR].bitcast(F32)
        MT = MT_mem[:, 0:2 * J * T].rearrange("p (b j e) -> p b j e", b=2, j=J)
        nat_f = MT_mem[0:G, 0:2 * (GE + 2)].bitcast(F32)
        iota_w = sb("iota_w", [T, W])
        e0 = sb("e0", [1, W])
        src_g = sb("src_g", [T, 2, J], I32)
        win = place(W, [2, NP, HD], BF16, "p (b n f) -> p b n f", b=2, n=NP)
        es = sb("es", [T, EB * EQ, EK], BF16)
        es_res = sb("es_res", [T, J, 3])
        penB = sb("penB", [T, H, JR])
        eaTg = place(K, [2, EB, T], BF16, "p (b q e) -> p b q e", b=2, q=EB)
        penT = place(K, [2, T + 1], F32, "p (b e) -> p b e", b=2)
        er = place(T, [2, HD], F32, "p (b f) -> p b f", b=2)
        pr = place(T, [2, HD], F32, "p (b f) -> p b f", b=2)
        al = place(T, [2, J, H], F32, "p (b j h) -> p b j h", b=2, j=J)
        alx = place(T, [J, H], F32, "p (j h) -> p j h", j=J)
        alL = place(T, [H, JR], F32, "p (h k) -> p h k", h=H)
        by_tile = alL.rearrange("p h k -> p k h")[:, 0:J, :]
        run_f = place(K, [T])
        run_b = place(K, [T])
        ends = sb("ends", [K, 2])
        into = sb("into", [K, 2])
        c_old = sb("c_old", [1, H])
        part_from = sb("part_from", [1, G + 1])
        dsh = place(T, [J * H])
        hot = sb("hot", [W, 2])
        Ps = place(W, [2, HD], F32, "p (b f) -> p b f", b=2)
        c_raw = sb("c_raw", [1, HD])
        c_dif = sb("c_dif", [1, H])
        c_fac = sb("c_fac", [1, H])
        c_fs = sb("c_fs", [1, H])
        crow = sb("crow", [1, HD])
        taken = 0
        st = later(T, [2, PER_LOAD, SR], "p (b j f) -> p b j f", b=2, j=PER_LOAD)
        agg = later(T, [2, PER_LOAD, D], "p (b j f) -> p b j f", b=2, j=PER_LOAD)
        den = later(T, [2, PER_LOAD, H], "p (b j h) -> p b j h", b=2, j=PER_LOAD)
        rden = later(T, [2, PER_LOAD, H], "p (b j h) -> p b j h", b=2, j=PER_LOAD)
        taken = 0
        W1 = later(K, [TOP, KC, FF], "p (n k f) -> p n k f", n=TOP, k=KC)
        W2 = later(K, [TOP, FC, D], "p (n c f) -> p n c f", n=TOP, c=FC)
        hid = later(K, [2, TOP * FC, CH], "p (b j e) -> p b j e", b=2, j=TOP * FC)
        b2 = later(1, [TOP, D], "p (b f) -> p b f", b=TOP)
        yrow = later(T, [2, D], "p (b f) -> p b f", b=2)

        ysum = sb("ysum", [K, KC])
        r = {n: sb("r_" + n, [1, X8]) for n in
             ("logits", "exp", "w", "cap", "load", "exp2", "w2", "rank", "first", "second", "num", "tmp")}
        rs = {n: sb("rs_" + n, [1, 1]) for n in
              ("max", "sum", "rsum", "max2", "sum2", "rsum2", "diff", "e", "e1")}
        top = sb("top", [1, TOP])
        topi = sb("topi", [1, TOP])
        topi_i = sb("topi_i", [1, TOP], I32)
        topw = sb("topw", [1, TOP])
        topwB = sb("topwB", [K, TOP])
        pair = sb("pair", [1, X8, X8])
        pair2 = sb("pair2", [1, X8, X8])
        tri8 = sb("tri8", [1, X8, X8])
        z = later(T, [2, D], "p (b f) -> p b f", b=2)
        zmv = sb("zmv", [T, 2, 2])
        zsd = sb("zsd", [T, 2])
        zr = sb("zr", [T, 2])
        res = later(T, [2, D], "p (b f) -> p b f", b=2)

        bank = [ctx.enter_context(nc.psum_tensor(f"bank{i}", [K, 512], F32)) for i in range(8)]

        s_xload = [sem(f"s_xload{i}") for i in range(LOADS)]
        s_wload = sem("s_wload")
        s_wenc = sem("s_wenc")
        s_wencp = sem("s_wencp")
        s_ewp = sem("s_ewp")
        s_const = sem("s_const")
        s_setup_pe = sem("s_setup_pe")
        s_setup_ve = sem("s_setup_ve")
        s_stats = sem("s_stats")
        s_mvs = sem("s_mvs")
        s_mv = sem("s_mv")
        s_var = sem("s_var")
        s_sd = sem("s_sd")
        s_rstd = sem("s_rstd")
        s_xn = sem("s_xn")
        s_xnT = sem("s_xnT")
        s_xnTs = sem("s_xnTs")
        s_xnTr = sem("s_xnTr")
        s_rows = sem("s_rows")
        s_hrow = sem("s_hrow")
        s_kv = sem("s_kv")
        s_kmax = sem("s_kmax")
        s_hst = [sem(f"s_hst{i}") for i in range(2)]
        s_km = sem("s_km")
        s_kmp = sem("s_kmp")
        s_kshift = sem("s_kshift")
        s_kexp = sem("s_kexp")
        s_ctx = sem("s_ctx")
        s_fold_v = sem("s_fold_v")
        s_fold_p = sem("s_fold_p")
        s_stage = [sem(f"s_stage{i}") for i in range(2)]
        s_biased = sem("s_biased")
        s_mix = sem("s_mix")
        s_mixed = sem("s_mixed")
        s_passed = sem("s_passed")
        s_init = sem("s_init")
        s_initst = sem("s_initst")
        g_src, g_dst, g_ea = sem("g_src"), sem("g_dst"), sem("g_ea")
        g_Gs, g_Gd, g_S0 = sem("g_Gs"), sem("g_Gd"), sem("g_S0")
        V_STEPS = ("dstf same eaT apart before nbefore gap sel tof toi prod a1 a2 score spread masked masked "
                   "tmax newmax shift shift msg msg keep new").split()
        P_STEPS = "dstT eaTp enc spreadB sum".split()
        g_v, g_p, g_ew = sem("g_v"), sem("g_p"), sem("g_ew")

        def v_done(name, t):
            return len(V_STEPS) * t + len(V_STEPS) - V_STEPS[::-1].index(name)

        def p_done(name, t):
            return len(P_STEPS) * t + P_STEPS.index(name) + 1

        g_scatter = sem("g_scatter")
        g_done = sem("g_done")
        f_nat = [sem(f"f_nat{i}") for i in range(4)]
        f_natd = sem("f_natd")
        f_turn = sem("f_turn")
        f_colv, f_cola = sem("f_colv"), sem("f_cola")
        f_rows = sem("f_rows")
        f_ok = sem("f_ok")
        f_pad = sem("f_pad")
        f_wst = [sem(f"f_wst{i}") for i in range(2)]
        s_wp = sem("s_wp")
        s_wv = sem("s_wv")
        f_es = sem("f_es")
        f_esp = sem("f_esp")
        f_src = sem("f_src")
        f_hot = sem("f_hot")
        f_G = [sem(f"f_G{i}") for i in range(2)]
        f_win = [sem(f"f_win{i}") for i in range(2)]
        f_ET = sem("f_ET")
        f_eaT = sem("f_eaT")
        f_M = sem("f_M")
        f_MTp = sem("f_MTp")
        f_MT = sem("f_MT")
        f_enc = sem("f_enc")
        f_hd = sem("f_hd")
        f_relu = sem("f_relu")
        f_prod = sem("f_prod")
        f_red = sem("f_red")
        f_al0, f_al = sem("f_al0"), sem("f_al")
        f_C1 = sem("f_C1")
        f_C2 = sem("f_C2")
        f_C3 = sem("f_C3")
        f_C4 = sem("f_C4")
        f_w = sem("f_w")
        MAX_STEPS = ("old least lead fwd bwd head across_f across_b first dif clamp "
                     "into again_f again_b both shift").split()

        def w_done(name, g):
            return len(MAX_STEPS) * g + len(MAX_STEPS) + MAX_STEPS.index(name) + 1

        f_copied = sem("f_copied")
        f_exp = sem("f_exp")
        f_fac, f_fs, f_crow = sem("f_fac"), sem("f_fs"), sem("f_crow")
        f_v, f_vp = sem("f_v"), sem("f_vp")
        f_agg = sem("f_agg")
        f_P = sem("f_P")
        f_C5 = sem("f_C5")
        f_craw = sem("f_craw")
        f_store = sem("f_store")
        f_stored = sem("f_stored")
        s_st = [sem(f"s_st{i}") for i in range(2)]
        s_den, s_rden = sem("s_den"), sem("s_rden")
        s_agg = sem("s_agg")
        s_x1 = sem("s_x1")
        s_yr = sem("s_yr")
        s_yT = sem("s_yT")
        s_yTr = sem("s_yTr")
        s_ysum = sem("s_ysum")
        s_r, s_rp, s_ra = sem("s_r"), sem("s_rp"), sem("s_ra")
        s_topi = sem("s_topi")
        s_wx = sem("s_wx")
        s_w2s = sem("s_w2s")
        s_l1 = sem("s_l1")
        s_hid = sem("s_hid")
        s_l2 = sem("s_l2")
        s_yrow, s_z = sem("s_yrow"), sem("s_z")
        s_zst, s_zmv, s_zvar, s_zsd, s_zr = (sem(n) for n in ("s_zst", "s_zmv", "s_zvar", "s_zsd", "s_zr"))
        s_n1, s_n2, s_n3, s_res = (sem(n) for n in ("s_n1", "s_n2", "s_n3", "s_res"))
        s_out = [sem(f"s_out{i}") for i in range(2)]

        f_eaTb = sem("f_eaTb")
        NAT_STEPS = 15
        MESSAGES_AT, SUM_AT = (6, 8, 10, 12, 14), (8, 10, 12, 14, 14)
        assert BT == VT and len(SUM_AT) == VN
        VV = 3
        START = 9
        column_batches = []

        def batches(kind, dest, sources, scale=1.0):
            for a in range(0, len(sources), 4):
                part = sources[a:a + 4]
                column_batches.append((kind, dest[:, a:a + len(part), :], part, scale))

        def tiles_of(nat):
            return [nat[:, j * T:(j + 1) * T] for j in range(J)]

        batches("src", col_src.rearrange("p (g j) -> p j g", j=J), tiles_of(nat_src))
        batches("loc", col_loc.rearrange("p (g j) -> p j g", j=J), tiles_of(nat_dst))
        batches("new", col_new.rearrange("p (g j) -> p j g", j=J), tiles_of(nat_new), BREAK)
        batches("ea", col_ea.rearrange("p (g m) -> p m g", m=3 * J),
                [nat_ea[:, 3 * T * j + c:3 * T * (j + 1):3] for j in range(J) for c in range(3)])
        COLUMNS_VEC = [n for n, b in enumerate(column_batches) if b[0] == "src" or n % 2]
        COLUMNS_ACT = [n for n in range(len(column_batches)) if n not in COLUMNS_VEC]
        COLV, COLA = len(COLUMNS_VEC), len(COLUMNS_ACT)
        column_read = [(f_colv, COLUMNS_VEC.index(n) + 1) if n in COLUMNS_VEC else (f_cola, COLUMNS_ACT.index(n) + 1)
                       for n in range(len(column_batches))]

        block = ctx.enter_context(nc.Block())
        WEIGHT_LOADS = 15
        CONSTS = 34

        @block.sync
        def _(sp):
            x_tiles = x.rearrange("(t p) f -> p t f", p=T)
            weight_loads = [
                (Wg[:, :, :], L0_gnn_W.rearrange("(k p) i -> p k i", p=K)),
                (a_cols[:, 0, :], L0_gnn_a_src.rearrange("h d -> (h d)").rearrange("(k p) -> p k", p=K)),
                (a_cols[:, 1, :], L0_gnn_a_dst.rearrange("h d -> (h d)").rearrange("(k p) -> p k", p=K)),
                (Wenc0[0:3, :], L0_gnn_edge_W.rearrange("f c -> c f")),
                (Wenc0[3:4, :], L0_gnn_edge_b.unsqueeze(0)),
                (ew_cols[:, :, 0:3], L0_gnn_edge_W.rearrange("(k p) c -> p k c", p=K)),
                (ew_cols[:, :, 3:4], L0_gnn_edge_b.rearrange("(k p) -> p k", p=K).unsqueeze(2)),
                (Wqkv[:, :, :], L0_mix_W_qkv.rearrange("(k p) f -> p k f", p=K)),
                (Wo[:, :], L0_mix_W_out),
                (bias_rows[:, 0, :], L0_gnn_bias.unsqueeze(0)),
                (bias_rows[:, 1, :], L0_mix_b_out.unsqueeze(0)),
                (Wr[:, :, :], L0_ffn_Wr.rearrange("(k p) e -> p k e", p=K)),
                (br[:, :], L0_ffn_br.unsqueeze(0)),
                (gamma[:, :], L0_ffn_gamma.partition_broadcast(T)),
                (beta[:, :], L0_ffn_beta.partition_broadcast(T)),
            ]
            assert len(weight_loads) == WEIGHT_LOADS
            for i in range(LOADS):
                part = slice(i * PER_LOAD, (i + 1) * PER_LOAD)
                sp.dma_start(X[:, part, :], x_tiles[:, part, :]).then_inc(s_xload[i], 16)
                if i == 0:
                    for dest, source in weight_loads:
                        sp.dma_start(dest, source).then_inc(s_wload, 16)
            sp.wait_ge(s_init, 2)
            sp.dma_start(state_table.rearrange("(t p) c -> p t c", p=T),
                         init_row[:, :].unsqueeze(1).broadcast_to([T, NT + 2, SR])).then_inc(s_initst, 16)
            sp.wait_ge(s_const, CONSTS)
            sp.dma_start(window_table[N:N + 2 * T, :].rearrange("(t p) c -> p t c", p=T),
                         zpad[:, :].unsqueeze(1).broadcast_to([T, 2, NP * HD])).then_inc(f_pad, 16)
            with sp.Fori(0, NT // 2) as i:
                for par in range(2):
                    t = 2 * i + par
                    sp.wait_ge(s_hrow, t + 3)
                    sp.dma_start(node_table[bass.ds(t * T, T), :], hrow[:, par, :]).then_inc(s_hst[par], 16)
                    sp.wait_ge(s_wv, 4 * t + 12)
                    sp.dma_start(window_table[bass.ds(t * T, T), :],
                                 wrow[:, par, :, :].rearrange("p n f -> p (n f)")).then_inc(f_wst[par], 16)
            def any_order():
                with sp.Fori(0, ET) as t:
                    sp.wait_ge(g_done, t + 1)
                    sp.dma_start(src_i[:, :], src[bass.ds(t * T, T)].unsqueeze(1)).then_inc(g_src, 16)
                    sp.dma_start(dst_i[:, :], dst[bass.ds(t * T, T)].unsqueeze(1)).then_inc(g_dst, 16)
                    sp.dma_start(ea[:, 0:3], edge_attr_3[bass.ds(t * T, T), :]).then_inc(g_ea, 16)

                sp.wait_ge(g_done, ET + 1)

            def in_groups():
                def load(g, par):
                    sp.wait_ge(f_hd, J * g + J)
                    first = sp.value_load(base_i[0:1, bass.ds(g, 1)], min_val=0, max_val=N - 1)
                    sp.dma_start(win[:, par, :, :].rearrange("p n f -> p (n f)"),
                                 window_table[bass.ds(first, W), :]).then_inc(f_win[par], 16)

                def store(g, par):
                    sp.wait_ge(f_P, g + 2)
                    first = sp.value_load(base_i[0:1, bass.ds(g, 1)], min_val=0, max_val=N - 1)
                    sp.dma_start(state_table[bass.ds(first, W), 0:HD], Ps[:, par, :]).then_inc(f_store, 16)
                    sp.wait_ge(f_store, 16 * g + 16)
                    sp.sem_inc(f_stored, 1)

                for par in range(2):
                    sp.wait_ge(f_wst[par], NT // 2 * 16)
                sp.wait_ge(f_pad, 16)
                sp.wait_ge(s_initst, 16)
                load(0, 0)
                load(1, 1)
                with sp.Fori(0, G // 2 - 1) as i:
                    for par in range(2):
                        load(2 * i + par + 2, par)
                        store(2 * i + par, par)
                store(G - 2, 0)
                store(G - 1, 1)

            sp.sem_inc(f_stored, 2)
            sp.wait_ge(s_ctx, NT + 10)
            sp.dma_start(nat_dst[:, :].bitcast(I32), dst.rearrange("(g e) -> g e", e=GE)).then_inc(f_nat[0], 16)
            sp.dma_start(nat_next[0:G - 1, :], dst.rearrange("(g e) -> g e", e=GE)[1:G, 0:1]).then_inc(f_nat[1], 16)
            sp.dma_start(nat_src[:, :].bitcast(I32), src.rearrange("(g e) -> g e", e=GE)).then_inc(f_nat[2], 16)
            sp.dma_start(nat_ea[:, :], edge_attr_3.rearrange("(g e) c -> g (e c)", e=GE)).then_inc(f_nat[3], 16)

            sp.wait_ge(f_ok, 4)
            grouped = sp.value_load(ok_i[0:1, 0:1], min_val=0, max_val=1)
            with sp.If(grouped == 1):
                in_groups()
            with sp.Else():
                any_order()
            with sp.Fori(0, LOADS // 2) as i:
                for par in range(2):
                    part = 2 * i + par
                    sp.wait_ge(s_agg, part + 1)
                    sp.dma_start(st[:, par, :, :], state_table[bass.ds(part * PER_LOAD * T, PER_LOAD * T), :]
                                 .rearrange("(j p) c -> p j c", p=T)).then_inc(s_st[par], 16)
            sp.wait_ge(s_topi, 1)
            for n in range(TOP):
                e = sp.value_load(topi_i[0:1, n:n + 1], min_val=0, max_val=X8 - 1)
                sp.dma_start(W1[:, n, :, :], L0_ffn_W1[bass.ds(e, 1), :, :]
                             .rearrange("a (k p) f -> p (a k) f", p=K)).then_inc(s_wx, 16)
                sp.dma_start(b1[:, n, :], L0_ffn_b1[bass.ds(e, 1), :]
                             .rearrange("a (c p) -> p (a c)", p=K)).then_inc(s_wx, 16)
                sp.dma_start(W2[:, n, :, :], L0_ffn_W2[bass.ds(e, 1), :, :]
                             .rearrange("a (c p) f -> p (a c) f", p=K)).then_inc(s_wx, 16)
                sp.dma_start(b2[:, n, :], L0_ffn_b2[bass.ds(e, 1), :]).then_inc(s_wx, 16)
            with sp.Fori(0, NCH) as c:
                for par in range(2):
                    t = 2 * c + par
                    sp.wait_ge(s_res, t + 1)
                    sp.dma_start(out[bass.ds(t * T, T), :], res[:, par, :]).then_inc(s_out[par], 16)
            for par in range(2):
                sp.wait_ge(s_out[par], NCH * 16)

        @block.gpsimd
        def _(po):
            po.sem_inc(s_xnTr, 2)
            po.sem_inc(s_agg, 2)
            po.memset(Wenc[:, :], 0.0).then_inc(s_wenc, 1)
            po.wait_ge(s_wenc, 1)
            po.affine_select(out=Wenc[:, :], in_=Wenc[:, :], compare_op=ALU.not_equal, fill=1.0,
                             base=-3, pattern=[[0, HD]], channel_multiplier=1).then_inc(s_wenc, 1)
            po.memset(init_row[:, :], 0.0).then_inc(s_init, 1)
            po.memset(ones[:, :], 1.0).then_inc(s_const, 1)
            po.memset(ident[:, :], 0.0).then_inc(s_const, 1)
            po.memset(lower[:, :], 1.0).then_inc(s_const, 1)
            po.memset(tri8[:, :, :], 1.0).then_inc(s_const, 1)
            po.memset(ea[:, :], 1.0).then_inc(s_const, 1)
            po.memset(onescol[:, :], 1.0).then_inc(s_const, 1)
            po.memset(ctxn[:, :], 0.0).then_inc(s_const, 1)
            po.memset(zrow[:, :], 0.0).then_inc(s_const, 1)
            po.iota(spare[:, :], pattern=[[0, 1]], base=N, channel_multiplier=1,
                    allow_small_or_imprecise_dtypes=True).then_inc(s_const, 1)
            po.iota(iota_p[:, :], pattern=[[0, 1]], base=0, channel_multiplier=1,
                    allow_small_or_imprecise_dtypes=True).then_inc(s_const, 1)
            po.iota(iota_w[:, :], pattern=[[1, W]], base=0, channel_multiplier=0,
                    allow_small_or_imprecise_dtypes=True).then_inc(s_const, 1)
            po.memset(identb[:, :], 0.0).then_inc(s_const, 1)
            po.memset(WencP[:, :], 0.0).then_inc(s_const, 1)
            po.memset(ew_parts[:, :, :, :], 0.0).then_inc(s_const, 1)
            po.memset(zpad[:, :], 0.0).then_inc(s_const, 1)
            po.memset(e0[:, :], 0.0).then_inc(s_const, 1)
            po.memset(es[:, :, :], 0.0).then_inc(s_const, 1)
            po.memset(straddle[:, :], 0.0).then_inc(s_const, 1)
            po.memset(nat_next[:, :], N).then_inc(s_const, 1)
            po.iota(r["num"][:, :], pattern=[[1, X8]], base=0, channel_multiplier=0,
                    allow_small_or_imprecise_dtypes=True).then_inc(s_const, 1)
            n = 20
            po.wait_ge(s_init, 1)
            po.memset(init_row[:, HD:SR], LOW).then_inc(s_init, 1)
            po.wait_ge(s_const, n)
            po.affine_select(out=ident[:, :], in_=ident[:, :], compare_op=ALU.not_equal, fill=1.0,
                             base=0, pattern=[[-1, K]], channel_multiplier=1).then_inc(s_const, 1)
            po.affine_select(out=identb[:, :], in_=identb[:, :], compare_op=ALU.not_equal, fill=1.0,
                             base=0, pattern=[[-1, K]], channel_multiplier=1).then_inc(s_const, 1)
            po.memset(e0[:, 0:1], 1.0).then_inc(s_const, 1)
            po.memset(es[:, 0:J, 18:21], 1.0).then_inc(s_const, 1)
            po.affine_select(out=lower[:, :], in_=lower[:, :], compare_op=ALU.is_gt, fill=0.0,
                             base=0, pattern=[[-1, T]], channel_multiplier=1).then_inc(s_const, 1)
            po.affine_select(out=tri8[:, :, :], in_=tri8[:, :, :], compare_op=ALU.is_gt, fill=0.0,
                             base=0, pattern=[[1, X8], [-1, X8]], channel_multiplier=0).then_inc(s_const, 1)
            po.wait_ge(s_wload, WEIGHT_LOADS * 16)
            for k in range(KC):
                for s in range(2):
                    po.tensor_copy(a_blocks[:, k, s * H:(s + 1) * H],
                                   a_cols[:, s, k:k + 1].broadcast_to([K, H])).then_inc(s_const, 1)
            n += 6 + 4
            po.wait_ge(s_const, n)
            for k in range(KC):
                blk = a_blocks[:, k, :].rearrange("p (s h) -> p s h", s=2)
                po.affine_select(out=blk, in_=blk, compare_op=ALU.is_ge, fill=0.0,
                                 base=K * k, pattern=[[0, 2], [-DH, H]], channel_multiplier=1).then_inc(s_const, 1)
                n += 1
                po.wait_ge(s_const, n)
                po.affine_select(out=blk, in_=blk, compare_op=ALU.is_ge, fill=0.0,
                                 base=DH - 1 - K * k, pattern=[[0, 2], [DH, H]],
                                 channel_multiplier=-1).then_inc(s_const, 1)
                n += 1
            assert n == CONSTS
            po.wait_ge(s_setup_ve, 8)
            ones_at = WencP[:, :].rearrange("p (h b) -> p h b", h=H)[:, :, DH:HB]
            for q in range(EQ):
                po.affine_select(out=ones_at, in_=ones_at, compare_op=ALU.not_equal, fill=1.0,
                                 base=-(EK * q + 18), pattern=[[0, H], [0, 1]], channel_multiplier=1
                                 ).then_inc(s_wencp, 1)
                po.wait_ge(s_wencp, q + 1)
            with po.Fori(0, NT // 2) as i:
                for par in range(2):
                    t = 2 * i + par
                    po.wait_ge(s_xnTs, t + 3)
                    po.tensor_copy(xnT[:, :, bass.ds(t * T, T)], xnTs[:, par, :, :]).then_inc(s_xnTr, 1)
            po.wait_ge(s_xnTr, NT + 2)
            po.wait_ge(s_rows, NT + 2)
            with po.Fori(0, NT // 2) as i:
                po.wait_ge(s_mix, 2 * i + 1)
                po.tensor_copy(xnTs[:, 0, :, :], xnT[:, :, bass.ds(2 * T * i, T)]).then_inc(s_stage[0], 1)
            for par in range(2):
                po.wait_ge(s_hst[par], NT // 2 * 16)
            po.wait_ge(s_initst, 16)
            def any_order():
                with po.Fori(0, ET) as t:
                    po.wait_ge(g_src, 16 * t + 16)
                    po.wait_ge(g_dst, 16 * t + 16)
                    po.sem_inc(s_passed, 1)
                    for rows, table, index, landed in ((Gs, node_table, src_i, g_Gs), (Gd, node_table, dst_i, g_Gd),
                                                       (S0, state_table, dst_i, g_S0)):
                        po.indirect_dma_start(out=rows[:, :], out_offset=None, in_=table,
                                              in_offset=bass.IndirectOffsetOnAxis(ap=index[:, :], axis=0)
                                              ).then_inc(landed, 16)
                    po.wait_ge(g_v, v_done("new", t))
                    po.wait_ge(g_v, v_done("newmax", t))
                    po.wait_ge(g_v, v_done("toi", t))
                    po.wait_ge(g_S0, 16 * t + 16)
                    po.sem_inc(s_passed, 1)
                    po.indirect_dma_start(out=state_table, out_offset=bass.IndirectOffsetOnAxis(ap=to_i[:, :], axis=0),
                                          in_=S1[:, :], in_offset=None).then_inc(g_scatter, 16)


            def in_groups():
                def gathers(g, par, piece):
                    po.wait_ge(f_agg, VN * g + piece + 1)
                    po.sem_inc(s_passed, 1)
                    for j in range(VT * piece, VT * piece + VT):
                        po.indirect_dma_start(out=Gr[:, par, j, :], out_offset=None, in_=node_table,
                                              in_offset=bass.IndirectOffsetOnAxis(ap=src_g[:, par, j:j + 1], axis=0)
                                              ).then_inc(f_G[par], 16)

                def attributes(g):
                    if g is not zero:
                        po.wait_ge(f_ET, g)
                        po.sem_inc(s_passed, 1)
                    ea_g = col_ea[:, bass.ds(3 * J * g, 3 * J)].rearrange("p (j c) -> p j c", c=3)
                    po.tensor_copy(es[:, 0:J, 0:3], ea_g).then_inc(f_esp, 1)
                    po.wait_ge(f_esp, 5 * g + 1)
                    po.sem_inc(s_passed, 1)
                    po.tensor_tensor(es_res[:, :, :], ea_g, es[:, 0:J, 0:3], ALU.subtract).then_inc(f_esp, 1)
                    po.wait_ge(f_esp, 5 * g + 2)
                    po.sem_inc(s_passed, 1)
                    po.tensor_copy(es[:, 0:J, 6:9], es_res[:, :, :]).then_inc(f_esp, 1)
                    po.wait_ge(f_esp, 5 * g + 3)
                    po.sem_inc(s_passed, 1)
                    po.tensor_tensor(es_res[:, :, :], es_res[:, :, :], es[:, 0:J, 6:9], ALU.subtract).then_inc(f_esp, 1)
                    po.wait_ge(f_esp, 5 * g + 4)
                    po.sem_inc(s_passed, 1)
                    po.tensor_copy(es[:, 0:J, 12:15], es_res[:, :, :]).then_inc(f_esp, 1)
                    po.tensor_copy(penB[:, :, 0:J], col_new[:, bass.ds(J * g, J)].unsqueeze(1)
                                   .broadcast_to([T, H, J])).then_inc(f_es, 1)

                zero = 0

                def messages(g, par):
                    po.wait_ge(f_exp, g + 1)
                    po.sem_inc(s_passed, 1)
                    for piece in range(VV, VN):
                        rows = Gr[:, par, VT * piece:VT * (piece + 1), 0:HD].rearrange("p j (h b) -> p j h b", h=H)
                        po.tensor_tensor(rows[:, :, :, 0:DH], rows[:, :, :, 0:DH],
                                         rows[:, :, :, DH:HB].broadcast_to([T, VT, H, DH]), ALU.mult).then_inc(f_vp, 1)

                def group(g, par, before=None, last=False):
                    if before is not None:
                        messages(before, par)
                    po.wait_ge(f_agg, VN * g + 1)
                    po.sem_inc(s_passed, 1)
                    po.tensor_copy(src_g[:, par, :], col_src[:, bass.ds(J * g, J)]).then_inc(f_src, 1)
                    po.wait_ge(f_src, g + 1)
                    gathers(g, par, 0)
                    if not last:
                        attributes(g + 1)
                    for piece in range(1, VN):
                        gathers(g, par, piece)
                    po.wait_ge(f_craw, g + 2)
                    po.sem_inc(s_passed, 1)
                    po.tensor_copy(hot[:, par:par + 1], last_hot[:, bass.ds(g, 1)]).then_inc(f_hot, 1)

                for buffer, value in ((hot[:, 1:2], 0.0), (Ps[:, 1, :], 0.0), (into_f, 0.0),
                                      (into_b, 0.0), (any_new, BREAK), (penB[:, :, :], BREAK), (alL[:, :, :], 0.0),
                                      (penT[:, 0, T:T + 1], 0.0), (penT[:, 1, T:T + 1], 0.0)):
                    po.memset(buffer, value).then_inc(f_hot, 1)
                po.wait_ge(f_hot, START)
                attributes(zero)
                group(zero, 0)
                group(1, 1)
                with po.Fori(0, G // 2 - 2) as i:
                    group(2 * i + 2, 0, before=2 * i)
                    group(2 * i + 3, 1, before=2 * i + 1)
                group(G - 2, 0, before=G - 4)
                group(G - 1, 1, before=G - 3, last=True)
                messages(G - 2, 0)
                messages(G - 1, 1)

            po.wait_ge(f_colv, COLV)
            po.wait_ge(f_cola, COLA)

            po.wait_ge(f_ok, 4)
            grouped = po.value_load(ok_i[0:1, 0:1], min_val=0, max_val=1)
            with po.If(grouped == 1):
                in_groups()
            with po.Else():
                any_order()

            with po.Fori(0, LOADS // 2) as i:
                for par in range(2):
                    part = 2 * i + par
                    po.wait_ge(s_rden, part + 1)
                    po.wait_ge(s_x1, part + 1)
                    po.sem_inc(s_passed, 1)
                    sums = st[:, par, :, 0:HD].rearrange("p j (h b) -> p j h b", h=H)
                    po.tensor_tensor(agg[:, par, :, :].rearrange("p j (h d) -> p j h d", h=H), sums[:, :, :, 0:DH],
                                     rden[:, par, :, :].unsqueeze(3).broadcast_to([T, PER_LOAD, H, DH]),
                                     ALU.mult).then_inc(s_agg, 1)

        @block.tensor
        def _(pe):
            for s, credit in ((s_xnT, 2), (s_rows, 2), (s_ctx, 10), (s_mix, 2), (s_yT, 2), (s_l2, 4), (f_hd, 2 * J), (f_agg, 2 * VN)):
                pe.sem_inc(s, credit)
            pe.wait_ge(s_const, CONSTS)
            pe.wait_ge(s_wload, WEIGHT_LOADS * 16)
            for ki in range(KC):
                for kh in range(KC):
                    mm = pe.transpose(bank[ki][:, kh * K:(kh + 1) * K], Wg[:, kh, ki * K:(ki + 1) * K], ident[:, :])
                mm.then_inc(s_setup_pe, 1)
            for ki in range(KC):
                for kh in range(KC):
                    mm = pe.matmul(bank[2 + ki][:, 0:2 * H], Wg[:, kh, ki * K:(ki + 1) * K], a_blocks[:, kh, :],
                                   start=(kh == 0), stop=(kh == KC - 1))
                mm.then_inc(s_setup_pe, 1)
            for ki in range(KC):
                mm = pe.transpose(bank[4][:, ki * K:(ki + 1) * K], Wqkv[:, ki, 0:QK], ident[:, :])
            mm.then_inc(s_setup_pe, 1)
            pe.wait_ge(s_ewp, 15)
            for k in range(KC):
                mm = pe.transpose(bank[5][:, k * K // 2:(k + 1) * K // 2].bitcast(BF16),
                                  ew_parts[:, k, :, :].rearrange("p q r -> p (q r)"), identb[:, :])
            mm.then_inc(s_setup_pe, 1)
            pe.wait_ge(s_setup_ve, 8)

            def turn(t, par):
                pe.wait_ge(s_xn, t + 1)
                pe.wait_ge(s_xnTs, t + 1)
                for k in range(KC):
                    mm = pe.transpose(bank[par][:, k * T:(k + 1) * T], xn[:, par, k * K:(k + 1) * K], ident[0:T, 0:T])
                mm.then_inc(s_xnT, 1)

            def node_rows(t, par):
                pe.wait_ge(s_xnTs, t + 3)
                pe.wait_ge(s_hrow, t + 1)
                pe.wait_ge(s_kmax, t + 1)
                for k in range(KC):
                    pe.matmul(bank[2 + par][0:T, 0:HR], xnTs[:, par, k, :], Wnode[:, k, :],
                              start=(k == 0), stop=(k == KC - 1))
                for k in range(KC):
                    mm = pe.matmul(bank[4 + par][0:T, 0:2 * QK], xnTs[:, par, k, :], Wqkv[:, k, QK:3 * QK],
                                   start=(k == 0), stop=(k == KC - 1))
                mm.then_inc(s_rows, 1)

            turn(0, 0)
            with pe.Fori(0, NT // 2 - 1) as i:
                for par in range(2):
                    turn(2 * i + par + 1, 1 - par)
                    node_rows(2 * i + par, par)
            turn(NT - 1, 1)
            node_rows(NT - 2, 0)
            node_rows(NT - 1, 1)

            pe.wait_ge(s_kmax, NT + 2)
            pe.wait_ge(s_xnTs, NT + 2)
            pe.wait_ge(s_hrow, NT + 2)
            pe.transpose(bank[0][:, 0:T], kmax[:, :], ident[0:T, 0:T]).then_inc(s_kmp, 1)
            pe.wait_ge(s_km, 1)
            pe.transpose(bank[1][0:1, 0:K], kmaxT[:, :], ident[:, :]).then_inc(s_kmp, 1)
            pe.wait_ge(s_km, 2)
            pe.matmul(bank[2][0:T, 0:QK], ones[0:1, 0:T], nkmax[:, :], start=True, stop=True).then_inc(s_kmp, 1)
            pe.matmul(bank[6][:, 0:QK], zrow[:, :], zrow[:, :], start=True, stop=False)
            pe.matmul(bank[7][:, 0:1], zrow[:, :], zrow[:, 0:1], start=True, stop=False)
            with pe.Fori(0, NT // 10) as i:
                for j in range(10):
                    if j % 5 == 0:
                        pe.wait_ge(s_kexp, 2 * i + j // 5 + 1)
                    k_exp = kexp[:, j // 5, j % 5, :]
                    v_rows = KV[:, bass.ds(10 * i + j, 1), QK:2 * QK].rearrange("p a f -> p (a f)")
                    pe.matmul(bank[6][:, 0:QK], k_exp, v_rows, start=False, stop=False)
                    pe.matmul(bank[7][:, 0:1], k_exp, onescol[:, :], start=False, stop=False).then_inc(s_ctx, 1)
            pe.matmul(bank[6][:, 0:QK], zrow[:, :], zrow[:, :], start=False, stop=True)
            pe.matmul(bank[7][:, 0:1], zrow[:, :], zrow[:, 0:1], start=False, stop=True).then_inc(s_fold_p, 1)
            pe.wait_ge(s_fold_v, 5)
            pe.transpose(bank[4][:, 0:QK], ctxn[:, :], ident[:, :]).then_inc(s_fold_p, 1)
            pe.wait_ge(s_fold_v, 6)
            pe.matmul(bank[5][:, 0:D], ctxT[:, :], Wo[:, :], start=True, stop=True).then_inc(s_fold_p, 1)
            pe.wait_ge(s_fold_v, 7)
            for k in range(KC):
                mm = pe.matmul(bank[2 + k][:, 0:D], WqT[:, k * K:(k + 1) * K], ctxWo[:, :], start=True, stop=True)
            mm.then_inc(s_fold_p, 1)
            pe.wait_ge(s_fold_v, 10)
            pe.matmul(bank[4][0:T, 0:D], ones[0:1, 0:T], bias_row[:, :], start=True, stop=True).then_inc(s_fold_p, 1)
            with pe.Fori(0, NT // 2) as i:
                for par in range(2):
                    t = 2 * i + par
                    pe.wait_ge(s_stage[par], i + 1)
                    pe.wait_ge(s_mixed, t + 1)
                    for k in range(KC):
                        mm = pe.matmul(bank[par][0:T, 0:D], xnTs[:, par, k, :], Wmix[:, k, :],
                                       start=(k == 0), stop=(k == KC - 1))
                    mm.then_inc(s_mix, 1)

            pe.wait_ge(s_mixed, NT + 2)
            for par in range(2):
                pe.wait_ge(f_wst[par], NT // 2 * 16)
                pe.wait_ge(s_hst[par], NT // 2 * 16)
            pe.wait_ge(f_natd, NAT_STEPS)
            pe.wait_ge(f_nat[3], 16)
            idg = ident[0:G, 0:G]
            pe.transpose(bank[6][0:1, 0:G], nat_ok[:, :], idg)
            pe.transpose(bank[6][0:1, 128:128 + G], nat_f[:, 1:2], idg)
            pe.transpose(bank[6][0:1, 256:256 + G], nat_str[:, :], idg)
            pe.transpose(bank[6][:, 384:384 + G], nat_loc[:, :].broadcast_to([G, W]), idg).then_inc(f_rows, 1)
            for n, (kind, dest, sources, scale) in enumerate(column_batches):
                if n >= 4:
                    done, count = column_read[n - 4]
                    pe.wait_ge(done, count)
                for k, source in enumerate(sources):
                    mm = pe.transpose(bank[n % 4][0:T, k * G:(k + 1) * G], source, idg)
                mm.then_inc(f_turn, 1)
            pe.wait_ge(f_colv, COLV)
            pe.wait_ge(f_cola, COLA)
            def any_order():
                with pe.Fori(0, ET) as t:
                    pe.wait_ge(g_done, t + 1)
                    pe.wait_ge(g_v, v_done("dstf", t))
                    pe.transpose(bank[0][0:T, 0:T], dst_f[:, :].broadcast_to([T, T]), ident[0:T, 0:T]).then_inc(g_p, 1)
                    pe.wait_ge(g_ea, 16 * t + 16)
                    pe.transpose(bank[1][0:4, 0:T], ea[:, :], ident[0:T, 0:T]).then_inc(g_p, 1)
                    pe.wait_ge(g_v, v_done("eaT", t))
                    pe.matmul(bank[2][0:T, 0:HD], eaT[:, :], Wenc[:, :], start=True, stop=True).then_inc(g_p, 1)
                    pe.wait_ge(g_v, v_done("spread", t))
                    for b in range(2):
                        mm = pe.matmul(bank[3 + b][0:T, 0:4 * T], ones[0:T, 0:T],
                                       spread[:, 4 * b:4 * b + 4, :].rearrange("p h e -> p (h e)"), start=True, stop=True)
                    mm.then_inc(g_p, 1)
                    pe.wait_ge(g_v, v_done("msg", t))
                    pe.wait_ge(g_v, v_done("same", t))
                    pe.matmul(bank[5][0:T, 0:HD], same[:, :], msg[:, :], start=True, stop=True).then_inc(g_p, 1)


            def in_groups():
                enc, spread_h, mt, sums, small, turned = bank[0:2], bank[2:4], bank[4], bank[5], bank[6], bank[7]

                def turn_attributes(g, n):
                    pe.wait_ge(f_es, 3 * g + 3)
                    pe.wait_ge(f_eaT, g + 1)
                    pe.wait_ge(f_craw, g + 1)
                    for b in range(EB):
                        pe.transpose(turned[:, 64 * b:64 * b + 64].bitcast(BF16)[:, 0:T],
                                     es[:, EQ * b:EQ * b + EQ, :].rearrange("p j r -> p (j r)"), identb[0:T, 0:T])
                    pe.transpose(turned[:, 256:256 + T], penB[:, :, :].rearrange("p h k -> p (h k)"),
                                 ident[0:T, 0:T]).then_inc(f_ET, 1)

                def turn_onehot(gx, px, b):
                    pe.wait_ge(f_M, BN * gx + b + 1)
                    pe.wait_ge(f_MT, BN * gx + b + 1)
                    for k in range(BT):
                        mm = pe.transpose(mt[:, k * T:(k + 1) * T], M[:, px, BT * b + k, :], ident[0:T, 0:T])
                    mm.then_inc(f_MTp, 1)

                def tile(gx, px, kx, j):
                    if j == 0:
                        pe.wait_ge(f_eaT, gx + 2)
                        pe.wait_ge(f_win[px], 16 * kx + 16)
                    if j % BT == 0:
                        pe.wait_ge(f_MT, BN * gx + j // BT + 2)
                    q, n = j % EQ, (px + j) % 2
                    pe.wait_ge(f_relu, J * gx + j + 1)
                    pe.matmul(enc[n][0:T, 0:HD], eaTg[EK * q:EK * (q + 1), px, j // EQ, :],
                              WencP[EK * q:EK * (q + 1), :], start=True, stop=True).then_inc(f_enc, 1)
                    pe.wait_ge(f_prod, J * gx + j + 1)
                    for part in range(NP):
                        mm = pe.matmul(spread_h[n][0:T, 0:HD], MT[:, px, j, :], win[:, px, part, :],
                                       start=(part == 0), stop=(part == NP - 1))
                    mm.then_inc(f_hd, 1)

                def scores_to_rows(gy):
                    pe.wait_ge(f_al, gy + 1)
                    pe.wait_ge(f_w, w_done("shift", gy) - len(MAX_STEPS))
                    pe.transpose(small[:, 0:T], alL[:, :, :].rearrange("p h k -> p (h k)"), ident[0:T, 0:T])
                    pe.wait_ge(f_w, w_done("least", gy))
                    pe.transpose(small[0:1, 384:384 + K], ends[:, 1:2], ident[:, :]).then_inc(f_C1, 1)

                def ends_to_row(gy):
                    pe.wait_ge(f_w, w_done("head", gy))
                    pe.wait_ge(f_copied, 3 * gy + 1)
                    pe.transpose(small[0:1, 128:128 + K], run_f[:, T - 1:T], ident[:, :])
                    pe.transpose(small[0:1, 256:256 + K], ends[:, 0:1], ident[:, :]).then_inc(f_C2, 1)

                def into_to_columns(gy):
                    pe.wait_ge(f_w, w_done("across_b", gy))
                    pe.sem_inc(s_passed, 1)
                    for n, row in enumerate((into_f, into_b[:, 1:K + 1])):
                        mm = pe.transpose(small[:, 126 + n:127 + n], row, ident[0:1, 0:1])
                    mm.then_inc(f_C3, 1)

                def maxima_to_edges(gy):
                    pe.wait_ge(f_w, w_done("both", gy))
                    pe.transpose(small[0:T, 0:K], run_f[:, :], ident[:, :]).then_inc(f_C4, 1)

                def add_messages(gy, py, piece):
                    if piece < VV:
                        pe.wait_ge(f_v, VV * gy + piece + 1)
                    else:
                        pe.wait_ge(f_vp, (VN - VV) * gy + piece - VV + 1)
                    if piece == 0:
                        pe.wait_ge(f_P, gy + 1)
                    for j in range(VT * piece, VT * piece + VT):
                        mm = pe.matmul(sums[:, 0:HD], M[:, py, j, :], Gr[:, py, j, 0:HD], start=(j == 0), stop=False)
                    if piece == VN - 1:
                        pe.wait_ge(f_crow, gy + 1)
                        mm = pe.matmul(sums[:, 0:HD], e0[:, :], crow[:, :], start=False, stop=True)
                    mm.then_inc(f_agg, 1)

                def last_node_before(gy, py):
                    pe.wait_ge(f_P, gy + 1)
                    pe.wait_ge(f_hot, gy + START)
                    pe.wait_ge(f_eaT, gy + 2)
                    pe.matmul(turned[0:1, 0:HD], hot[:, 1 - py:2 - py], Ps[:, 1 - py, :],
                              start=True, stop=True).then_inc(f_C5, 1)

                def step(gx, px, kx, gy, py, ky, last=False):
                    if gx is not None:
                        turn_onehot(gx, px, 0)
                    if gy is not None:
                        scores_to_rows(gy)
                    if gx is not None:
                        turn_onehot(gx, px, 1)
                    for j in range(J):
                        if gx is not None:
                            tile(gx, px, kx, j)
                        if gy is not None and j == 1:
                            ends_to_row(gy)
                        if gy is not None and j == 3:
                            into_to_columns(gy)
                        if gx is not None and j in (2, 5, 8):
                            turn_onehot(gx, px, j // 3 + 2)
                        if gy is not None and j == 4:
                            maxima_to_edges(gy)
                        if gy is not None and j == 6:
                            last_node_before(gy, py)
                        if gx is not None and j == 10 and not last:
                            turn_attributes(gx + 1, gx + 2)
                        for piece in range(VN):
                            if gy is not None and j == SUM_AT[piece]:
                                add_messages(gy, py, piece)

                turn_attributes(0, 1)
                step(0, 0, 0, None, None, None)
                with pe.Fori(0, G // 2 - 1) as i:
                    step(2 * i + 1, 1, i, 2 * i, 0, i)
                    step(2 * i + 2, 0, i + 1, 2 * i + 1, 1, i)
                step(G - 1, 1, G // 2 - 1, G - 2, 0, G // 2 - 1, last=True)
                step(None, None, None, G - 1, 1, G // 2 - 1)

            pe.wait_ge(f_ok, 4)
            grouped = pe.value_load(ok_i[0:1, 0:1], min_val=0, max_val=1)
            with pe.If(grouped == 1):
                in_groups()
            with pe.Else():
                any_order()

            pe.wait_ge(s_yr, 1)
            pe.matmul(bank[7][:, 0:KC], zrow[:, :], zrow[:, 0:KC], start=True, stop=False)
            with pe.Fori(0, NT // 2) as i:
                for par in range(2):
                    t = 2 * i + par
                    pe.wait_ge(s_yr, t + 1)
                    pe.wait_ge(s_yTr, t + 1)
                    for k in range(KC):
                        pe.matmul(bank[7][:, k:k + 1], xn[:, par, k * K:(k + 1) * K], onescol[:, :],
                                  start=False, stop=False)
                    for k in range(KC):
                        mm = pe.transpose(bank[par][:, k * T:(k + 1) * T], xn[:, par, k * K:(k + 1) * K], ident[0:T, 0:T])
                    mm.then_inc(s_yT, 1)
            pe.matmul(bank[7][:, 0:KC], zrow[:, :], zrow[:, 0:KC], start=False, stop=True).then_inc(s_ysum, 1)
            pe.wait_ge(s_ysum, 2)
            for k in range(KC):
                mm = pe.matmul(bank[2][0:1, 0:X8], ysum[:, k:k + 1], Wr[:, k, :], start=(k == 0), stop=(k == KC - 1))
            mm.then_inc(s_rp, 1)
            pe.wait_ge(s_w2s, 1)
            pe.matmul(bank[3][:, 0:TOP], ones[0:1, :], topw[:, :], start=True, stop=True).then_inc(s_rp, 1)
            pe.wait_ge(s_w2s, 2)
            pe.wait_ge(s_wx, 8 * 16)
            pe.wait_ge(s_yTr, NT + 2)

            def hidden(c, cp):
                for j in range(TOP * FC):
                    n, f = j // FC, j % FC
                    pe.wait_ge(s_hid, TOP * FC * c + j + 1)
                    for k in range(KC):
                        mm = pe.matmul(bank[j % 4][:, 0:CH], W1[:, n, k, f * K:(f + 1) * K],
                                       xnT[:, k:k + 1, bass.ds(c * CH, CH)].rearrange("p a e -> p (a e)"),
                                       start=(k == 0), stop=(k == KC - 1))
                    mm.then_inc(s_l1, 1)

            def experts(c, cp):
                pe.wait_ge(s_hid, TOP * FC * c + TOP * FC + 4)
                for half in range(2):
                    pe.wait_ge(s_z, 2 * c + half + 1)
                    ps = bank[4 + 2 * cp + half][0:T, 0:D]
                    for j in range(TOP * FC):
                        mm = pe.matmul(ps, hid[:, cp, j, half * T:(half + 1) * T], W2[:, j // FC, j % FC, :],
                                       start=(j == 0), stop=(j == TOP * FC - 1))
                    mm.then_inc(s_l2, 1)

            hidden(0, 0)
            pe.wait_ge(s_w2s, 7)
            pe.matmul(bank[7][0:T, 0:D], ones[0:1, 0:T], bias_row[:, :], start=True, stop=True).then_inc(s_rp, 1)
            pe.wait_ge(s_w2s, 8)
            with pe.Fori(0, NCH // 2) as i:
                for cp in range(2):
                    hidden(2 * i + cp + 1, 1 - cp)
                    experts(2 * i + cp, cp)
            experts(NCH - 1, 0)

        @block.scalar
        def _(ac):
            for s, credit in ((s_xnTs, 2), (s_hrow, 2), (s_yTr, 2), (s_hid, 4), (f_eaT, 1), (f_MT, 1), (f_relu, 2), (f_P, 1), (f_craw, 2)):
                ac.sem_inc(s, credit)
            ac.wait_ge(s_var, 1)
            ac.activation(rstd[:, :], rstd[:, :], ACT.Sqrt).then_inc(s_sd, 1)

            def stage(t, par):
                ac.wait_ge(s_xnT, t + 3)
                ac.wait_ge(s_rows, t + 1)
                ac.wait_ge(s_xnTr, t + 1)
                ac.activation(xnTs[:, par, :, :], bank[par][:, 0:KC * T].rearrange("p (k e) -> p k e", k=KC),
                              ACT.Copy).then_inc(s_xnTs, 1)

            def h_row(t, par, i):
                ac.wait_ge(s_rows, t + 3)
                ac.wait_ge(s_wv, 4 * t + 4)
                if i is not None:
                    ac.wait_ge(s_hst[par], 16 * i)
                    ac.wait_ge(f_wst[par], 16 * i)
                ac.activation(wrow[:, par, 0, :], bank[2 + par][0:T, 0:HD], ACT.Copy).then_inc(s_wp, 1)
                ac.activation(hrow[:, par, :], bank[2 + par][0:T, 0:HR], ACT.Copy).then_inc(s_hrow, 1)

            stage(0, 0)
            for par in range(2):
                stage(par + 1, 1 - par)
                h_row(par, par, None)
            with ac.Fori(1, NT // 2 - 1) as i:
                for par in range(2):
                    stage(2 * i + par + 1, 1 - par)
                    h_row(2 * i + par, par, i)
            stage(NT - 1, 1)
            h_row(NT - 2, 0, NT // 2 - 1)
            h_row(NT - 1, 1, NT // 2 - 1)
            for par in range(2):
                ac.wait_ge(f_wst[par], NT // 2 * 16)
            with ac.Fori(0, NT // 10) as i:
                ac.wait_ge(s_kshift, i + 1)
                for par in range(2):
                    ac.wait_ge(s_ctx, 10 * i + 5 * par + 5)
                    ac.activation(kexp[:, par, :, :], KV[:, bass.ds(10 * i + 5 * par, 5), 0:QK],
                                  ACT.Exp).then_inc(s_kexp, 1)
            ac.wait_ge(s_xnTr, NT + 2)
            ac.wait_ge(s_rows, NT + 2)
            with ac.Fori(0, NT // 2) as i:
                ac.wait_ge(s_mix, 2 * i + 2)
                ac.activation(xnTs[:, 1, :, :], xnT[:, :, bass.ds(2 * T * i + T, T)], ACT.Copy).then_inc(s_stage[1], 1)
            def any_order():
                with ac.Fori(0, ET) as t:
                    ac.wait_ge(g_v, v_done("shift", t))
                    ac.activation(ew[:, :], shifted[:, :], ACT.Exp).then_inc(g_ew, 1)


            def in_groups():
                enc, mt, sums, small, turned = bank[0:2], bank[4], bank[5], bank[6], bank[7]

                def attributes(g):
                    ac.wait_ge(f_ET, g + 1)
                    par = attributes.par
                    ac.activation(eaTg[:, par, :, :],
                                  turned[:, 0:64 * EB].bitcast(BF16).rearrange("p (b e) -> p b e", b=EB)[:, :, 0:T],
                                  ACT.Copy).then_inc(f_eaTb, 1)
                    ac.activation(penT[:, par, 0:T], turned[:, 256:256 + T], ACT.Copy).then_inc(f_eaT, 1)

                def onehot(gx, px, b):
                    ac.wait_ge(f_MTp, BN * gx + b + 1)
                    ac.activation(MT[:, px, BT * b:BT * (b + 1), :],
                                  mt[:, 0:BT * T].rearrange("p (k e) -> p k e", k=BT), ACT.Copy).then_inc(f_MT, 1)

                def repeated(g):
                    ac.wait_ge(f_esp, 5 * g + 5)
                    pairs = es[:, 0:J, 3:15].rearrange("p j (n c) -> p j n c", c=6)[:, :, :, 0:3]
                    ac.activation(pairs, es[:, 0:J, 0:3].unsqueeze(2).broadcast_to([T, J, 2, 3]),
                                  ACT.Copy).then_inc(f_es, 1)
                    ac.activation(es[:, 0:J, 15:18], es[:, 0:J, 6:9], ACT.Copy).then_inc(f_es, 1)

                def breaks(gy):
                    ac.wait_ge(f_w, w_done("bwd", gy))
                    ac.activation(any_new[:, 1:K + 1], small[0:1, 384:384 + K], ACT.Copy).then_inc(f_copied, 1)

                def ends(gy):
                    ac.wait_ge(f_C2, gy + 1)
                    ac.activation(end_row.rearrange("p (h k) -> p h k", k=JR)[:, :, 1:JR],
                                  small[0:1, 128:128 + K].rearrange("p (h k) -> p h k", k=JR)[:, :, 0:J],
                                  ACT.Copy).then_inc(f_copied, 1)
                    ac.activation(head_row, small[0:1, 256:256 + K], ACT.Copy).then_inc(f_copied, 1)

                def last_node_before(gy):
                    ac.wait_ge(f_C5, gy + 1)
                    ac.activation(c_raw[:, :], turned[0:1, 0:HD], ACT.Copy).then_inc(f_craw, 1)

                def encode(gx, px, j):
                    n = (px + j) % 2
                    ac.wait_ge(f_enc, J * gx + j + 1)
                    ac.wait_ge(f_prod, J * gx + j + 1)
                    ac.activation(er[:, n, :], enc[n][0:T, 0:HD], ACT.Relu).then_inc(f_relu, 1)

                def step(gx, px, kx, gy, py, ky, last=False):
                    if gx is not None:
                        onehot(gx, px, 0)
                        onehot(gx, px, 1)
                    if gy is not None:
                        breaks(gy)
                    for j in range(J):
                        if gx is not None:
                            encode(gx, px, j)
                        if gy is not None and j == 1:
                            ends(gy)
                        if gy is not None and j == 7:
                            last_node_before(gy)
                        if gx is not None and j == 8 and not last:
                            repeated(gx + 1)
                        if gx is not None and j in (2, 5, 8):
                            onehot(gx, px, j // 3 + 2)
                        if gy is not None and j == 4:
                            ac.wait_ge(f_w, w_done("clamp", gy))
                            ac.activation(c_fac[:, :], c_dif[:, :], ACT.Exp).then_inc(f_fac, 1)
                        if gy is not None and j == 6:
                            ac.wait_ge(f_w, w_done("shift", gy))
                            ac.activation(Gr[:, py, :, 0:HD].rearrange("p j (h b) -> p j h b", h=H)[:, :, :, DH:HB],
                                          dsh[:, :].rearrange("p (j h) -> p j h", h=H).unsqueeze(3),
                                          ACT.Exp).then_inc(f_exp, 1)
                        if gx is not None and j == 10 and not last:
                            attributes.par = 1 - px
                            attributes(gx + 1)
                    if gy is not None:
                        ac.wait_ge(f_agg, VN * gy + 3 * VN)
                        ac.wait_ge(f_stored, gy + 1)
                        ac.activation(Ps[:, py, :], sums[:, 0:HD], ACT.Copy).then_inc(f_P, 1)

                repeated(0)
                attributes.par = 0
                attributes(0)
                step(0, 0, 0, None, None, None)
                with ac.Fori(0, G // 2 - 1) as i:
                    step(2 * i + 1, 1, i, 2 * i, 0, i)
                    step(2 * i + 2, 0, i + 1, 2 * i + 1, 1, i)
                step(G - 1, 1, G // 2 - 1, G - 2, 0, G // 2 - 1, last=True)
                step(None, None, None, G - 1, 1, G // 2 - 1)

            for n in COLUMNS_ACT:
                ac.wait_ge(f_turn, n + 1)
                kind, dest, _, scale = column_batches[n]
                ac.activation(dest, bank[n % 4][0:T, 0:G * dest.shape[1]].rearrange("p (j g) -> p j g", g=G),
                              ACT.Copy, scale=scale).then_inc(f_cola, 1)

            ac.wait_ge(f_ok, 4)
            grouped = ac.value_load(ok_i[0:1, 0:1], min_val=0, max_val=1)
            with ac.If(grouped == 1):
                in_groups()
            with ac.Else():
                any_order()

            ac.wait_ge(s_var, 2)
            ac.activation(rstd[:, :], rstd[:, :], ACT.Sqrt).then_inc(s_sd, 1)
            with ac.Fori(0, NT // 2) as i:
                for par in range(2):
                    t = 2 * i + par
                    ac.wait_ge(s_yT, t + 3)
                    ac.activation(xnT[:, :, bass.ds(t * T, T)],
                                  bank[par][:, 0:KC * T].rearrange("p (k e) -> p k e", k=KC),
                                  ACT.Copy).then_inc(s_yTr, 1)
            for n, (a, b) in enumerate((("logits", "exp"), ("tmp", "exp2"))):
                ac.wait_ge(s_ra, 2 * n + 1)
                ac.activation(r[b][:, :], r[a][:, :], ACT.Exp).then_inc(s_ra, 1)
            ac.wait_ge(s_ra, 5)
            ac.activation(rs["e"][:, :], rs["diff"][:, :], ACT.Exp).then_inc(s_ra, 1)
            ac.wait_ge(s_wx, 8 * 16)

            def gelus(c, cp):
                ac.wait_ge(s_l2, 2 * c + 2)
                for j in range(TOP * FC):
                    ac.wait_ge(s_l1, TOP * FC * c + j + 1)
                    ac.activation(hid[:, cp, j, :], bank[j % 4][:, 0:CH], ACT.Gelu,
                                  bias=b1[:, j // FC, j % FC:j % FC + 1]).then_inc(s_hid, 1)

            def roots(c):
                ac.wait_ge(s_zvar, c + 1)
                ac.activation(zsd[:, :], zsd[:, :], ACT.Sqrt).then_inc(s_zsd, 1)

            gelus(0, 0)
            with ac.Fori(0, NCH // 2) as i:
                for cp in range(2):
                    gelus(2 * i + cp + 1, 1 - cp)
                    roots(2 * i + cp)
            roots(NCH - 1)

        @block.vector
        def _(ve):
            ve.memset(kmax[:, :], LOW).then_inc(s_kmax, 2)
            for s, credit in ((s_mixed, 2), (s_x1, 2), (s_z, 4), (g_done, 1), (s_wv, 8), (f_prod, 2), (f_red, 2), (f_w, len(MAX_STEPS))):
                ve.sem_inc(s, credit)

            def part_stats(part, n):
                ve.wait_ge(s_mv, n)
                ve.sem_inc(s_passed, 1)
                for j in range(PER_LOAD):
                    ve.bn_stats(stats[:, j, :], X[:, bass.ds(PER_LOAD * part + j, 1), :]
                                .rearrange("p a f -> p (a f)")).then_inc(s_stats, 1)
                ve.wait_ge(s_stats, PER_LOAD * (n + 1))
                ve.sem_inc(s_passed, 1)
                for j in range(PER_LOAD):
                    ve.bn_aggr(mvs[:, j, :], stats[:, j, :]).then_inc(s_mvs, 1)
                ve.wait_ge(s_mvs, PER_LOAD * (n + 1))
                ve.tensor_copy(mv[:, bass.ds(PER_LOAD * part, PER_LOAD), :], mvs[:, :, :]).then_inc(s_mv, 1)

            def rsqrt_all(n):
                ve.wait_ge(s_mv, LOADS * (n + 1))
                ve.tensor_scalar(rstd[:, :], mv[:, :, 1:2].rearrange("p t a -> p (t a)"), EPS, None,
                                 ALU.add).then_inc(s_var, 1)
                ve.wait_ge(s_sd, n + 1)
                ve.reciprocal(rstd[:, :], rstd[:, :]).then_inc(s_rstd, 1)
                ve.wait_ge(s_rstd, n + 1)

            def normalise(out, t):
                return ve.tensor_scalar(out, X[:, bass.ds(t, 1), :].rearrange("p a f -> p (a f)"),
                                        mv[:, bass.ds(t, 1), 0:1].rearrange("p a f -> p (a f)"),
                                        rstd[:, bass.ds(t, 1)], ALU.subtract, ALU.mult)

            ve.wait_ge(s_wload, WEIGHT_LOADS * 16)
            ve.wait_ge(s_const, CONSTS)
            ve.tensor_copy(ew_p[:, 0, :, :], ew_cols[:, :, :]).then_inc(s_ewp, 1)
            for n in range(1, NP):
                ve.wait_ge(s_ewp, 2 * n - 1)
                ve.tensor_tensor(ew_res[:, :, :], ew_cols[:, :, :] if n == 1 else ew_res[:, :, :],
                                 ew_p[:, n - 1, :, :], ALU.subtract).then_inc(s_ewp, 1)
                ve.wait_ge(s_ewp, 2 * n)
                ve.tensor_copy(ew_p[:, n, :, :], ew_res[:, :, :]).then_inc(s_ewp, 1)
            ve.wait_ge(s_ewp, 5)
            ve.wait_ge(s_wenc, 2)
            ve.tensor_copy(Wenc[:, :].rearrange("c (h b) -> c h b", h=H)[:, :, 0:DH],
                           Wenc0[:, :].rearrange("c (h d) -> c h d", h=H)).then_inc(s_ewp, 1)
            for at, n in ((0, 0), (3, 1), (6, 0), (9, 2), (12, 0), (15, 1)):
                ve.tensor_copy(ew_parts[:, :, :, at:at + 3],
                               ew_p[:, n, :, 0:3].unsqueeze(2).broadcast_to([K, KC, EQ, 3])).then_inc(s_ewp, 1)
            for n in range(NP):
                ve.tensor_copy(ew_parts[:, :, :, 18 + n:19 + n],
                               ew_p[:, n, :, 3:4].unsqueeze(2).broadcast_to([K, KC, EQ, 1])).then_inc(s_ewp, 1)
            for part in range(LOADS):
                ve.wait_ge(s_xload[part], 16)
                part_stats(part, part)
            rsqrt_all(0)
            ve.wait_ge(s_setup_pe, 2 * KC + 1)
            for ki in range(KC):
                blocks = Wnode[:, ki, 0:HD].rearrange("p (h b) -> p h b", h=H)
                ve.tensor_copy(blocks[:, :, 0:DH], bank[ki][:, 0:D].rearrange("p (h d) -> p h d", h=H)
                               ).then_inc(s_setup_ve, 1)
                ve.tensor_copy(blocks[:, :, DH:HB], bank[2 + ki][:, H:2 * H].unsqueeze(2)).then_inc(s_setup_ve, 1)
                ve.tensor_copy(Wnode[:, ki, HD:HR], bank[2 + ki][:, 0:H]).then_inc(s_setup_ve, 1)
            ve.tensor_copy(WqT[:, :], bank[4][:, 0:D]).then_inc(s_setup_ve, 1)
            ve.wait_ge(s_setup_pe, 2 * KC + 2)
            ve.tensor_copy(WencP[:, :].rearrange("p (h b) -> p h b", h=H)[:, :, 0:DH],
                           bank[5][:, 0:K].bitcast(BF16).rearrange("p (h d) -> p h d", h=H)).then_inc(s_setup_ve, 1)

            def normal_tile(t, par):
                ve.wait_ge(s_xnT, t + 1)
                normalise(xn[:, par, :], t).then_inc(s_xn, 1)

            def kv_rows(t, par):
                ve.wait_ge(s_rows, t + 3)
                ve.tensor_copy(KV[:, bass.ds(t, 1), :].rearrange("p a f -> p (a f)"),
                               bank[4 + par][0:T, 0:2 * QK]).then_inc(s_kv, 1)
                ve.wait_ge(s_kmax, t + 2)
                ve.tensor_tensor(kmax[:, :], kmax[:, :], bank[4 + par][0:T, 0:QK], ALU.max).then_inc(s_kmax, 1)

            def split_rows(t, par):
                ve.wait_ge(s_hrow, t + 3)
                ve.wait_ge(s_wp, t + 1)
                ve.tensor_tensor(wres[:, par, :], hrow[:, par, 0:HD], wrow[:, par, 0, :], ALU.subtract).then_inc(s_wv, 1)
                ve.wait_ge(s_wv, 4 * t + 9)
                ve.tensor_copy(wrow[:, par, 1, :], wres[:, par, :]).then_inc(s_wv, 1)
                ve.wait_ge(s_wv, 4 * t + 10)
                ve.tensor_tensor(wres[:, par, :], wres[:, par, :], wrow[:, par, 1, :], ALU.subtract).then_inc(s_wv, 1)
                ve.wait_ge(s_wv, 4 * t + 11)
                ve.tensor_copy(wrow[:, par, 2, :], wres[:, par, :]).then_inc(s_wv, 1)

            normal_tile(0, 0)
            normal_tile(1, 1)
            with ve.Fori(0, NT // 2 - 1) as i:
                for par in range(2):
                    normal_tile(2 * i + par + 2, par)
                    kv_rows(2 * i + par, par)
                    split_rows(2 * i + par, par)
            for par in range(2):
                kv_rows(NT - 2 + par, par)
                split_rows(NT - 2 + par, par)

            ve.wait_ge(s_kmp, 1)
            ve.tensor_reduce(kmaxT[:, :], bank[0][:, 0:T], AX.X, ALU.max).then_inc(s_km, 1)
            ve.wait_ge(s_kmp, 2)
            ve.tensor_scalar(nkmax[:, :], bank[1][0:1, 0:K], -1.0, None, ALU.mult).then_inc(s_km, 1)
            ve.wait_ge(s_kmp, 3)
            ve.tensor_copy(nkmaxB[:, :], bank[2][0:T, 0:QK]).then_inc(s_km, 1)
            ve.wait_ge(s_km, 3)
            ve.wait_ge(s_kv, NT)
            with ve.Fori(0, NT // 10) as i:
                part = KV[:, bass.ds(10 * i, 10), 0:QK]
                ve.tensor_tensor(part, part, nkmaxB[:, :].unsqueeze(1).broadcast_to([T, 10, QK]),
                                 ALU.add).then_inc(s_kshift, 1)
            ve.wait_ge(s_fold_p, 1)
            ve.reciprocal(ksum[:, :], bank[7][:, 0:1]).then_inc(s_fold_v, 1)
            ve.wait_ge(s_fold_v, 1)
            for a in range(QK // MD):
                q = slice(a * MD, (a + 1) * MD)
                ve.tensor_scalar(ctxn[q, q], bank[6][q, q], ksum[q, :], MD ** -0.5,
                                 ALU.mult, ALU.mult).then_inc(s_fold_v, 1)
            ve.wait_ge(s_fold_p, 2)
            ve.tensor_copy(ctxT[:, :], bank[4][:, 0:QK]).then_inc(s_fold_v, 1)
            ve.wait_ge(s_fold_p, 3)
            ve.tensor_copy(ctxWo[:, :], bank[5][:, 0:D]).then_inc(s_fold_v, 1)
            ve.wait_ge(s_fold_p, 4)
            for k in range(KC):
                ve.tensor_copy(Wmix[:, k, :], bank[2 + k][:, 0:D]).then_inc(s_fold_v, 1)
            ve.tensor_tensor(bias_row[:, :], bias_rows[:, 0, :], bias_rows[:, 1, :], ALU.add).then_inc(s_fold_v, 1)
            ve.wait_ge(s_fold_p, 5)
            ve.tensor_copy(biasB[:, :], bank[4][0:T, 0:D]).then_inc(s_fold_v, 1)
            ve.wait_ge(s_fold_v, 11)
            with ve.Fori(0, LOADS) as i:
                part = X[:, bass.ds(PER_LOAD * i, PER_LOAD), :]
                ve.tensor_tensor(part, part, biasB[:, :].unsqueeze(1).broadcast_to([T, PER_LOAD, D]),
                                 ALU.add).then_inc(s_biased, 1)
            ve.wait_ge(s_biased, LOADS)
            with ve.Fori(0, NT // 2) as i:
                for par in range(2):
                    t = 2 * i + par
                    ve.wait_ge(s_mix, t + 3)
                    tile = X[:, bass.ds(t, 1), :].rearrange("p a f -> p (a f)")
                    ve.tensor_tensor(tile, tile, bank[par][0:T, 0:D], ALU.add).then_inc(s_mixed, 1)

            def any_order():
                with ve.Fori(0, ET) as t:
                    ve.wait_ge(g_dst, 16 * t + 16)
                    ve.tensor_copy(dst_f[:, :], dst_i[:, :]).then_inc(g_v, 1)
                    ve.wait_ge(g_p, p_done("dstT", t))
                    ve.wait_ge(g_v, v_done("dstf", t))
                    ve.tensor_scalar(same[:, :], bank[0][0:T, 0:T], dst_f[:, :], None, ALU.is_equal).then_inc(g_v, 1)
                    ve.wait_ge(g_p, p_done("eaTp", t))
                    ve.tensor_copy(eaT[:, :], bank[1][0:4, 0:T]).then_inc(g_v, 1)
                    ve.wait_ge(g_v, v_done("same", t))
                    ve.tensor_scalar(apart[:, :], same[:, :], 1.0, -LOW, ALU.subtract, ALU.mult).then_inc(g_v, 1)
                    ve.tensor_tensor(before[:, :], same[:, :], lower[:, :], ALU.mult).then_inc(g_v, 1)
                    ve.wait_ge(g_v, v_done("before", t))
                    ve.tensor_reduce(nbefore[:, :], before[:, :], AX.X, ALU.max).then_inc(g_v, 1)
                    ve.tensor_tensor(to_f[:, :], spare[:, :], dst_f[:, :], ALU.subtract).then_inc(g_v, 1)
                    ve.wait_ge(g_v, v_done("gap", t))
                    ve.wait_ge(g_v, v_done("nbefore", t))
                    ve.tensor_tensor(to_f[:, :], to_f[:, :], nbefore[:, :], ALU.mult).then_inc(g_v, 1)
                    ve.wait_ge(g_v, v_done("sel", t))
                    ve.tensor_tensor(to_f[:, :], to_f[:, :], dst_f[:, :], ALU.add).then_inc(g_v, 1)
                    ve.wait_ge(g_v, v_done("tof", t))
                    ve.tensor_copy(to_i[:, :], to_f[:, :]).then_inc(g_v, 1)
                    ve.wait_ge(g_p, p_done("enc", t))
                    ve.wait_ge(g_Gs, 16 * t + 16)
                    ve.wait_ge(g_Gd, 16 * t + 16)
                    ve.wait_ge(g_S0, 16 * t + 16)
                    ve.scalar_tensor_tensor(out=prod[:, :], in0=bank[2][0:T, 0:HD], scalar=0.0, in1=Gd[:, 0:HD],
                                            op0=ALU.max, op1=ALU.mult).then_inc(g_v, 1)
                    ve.wait_ge(g_v, v_done("prod", t))
                    ve.tensor_reduce(score[:, :], prod[:, :].rearrange("p (h b) -> p h b", h=H), AX.X,
                                     ALU.add).then_inc(g_v, 1)
                    ve.wait_ge(g_v, v_done("a1", t))
                    ve.tensor_tensor(score[:, :], score[:, :], Gs[:, HD:HR], ALU.add).then_inc(g_v, 1)
                    ve.wait_ge(g_v, v_done("a2", t))
                    ve.scalar_tensor_tensor(out=score2[:, :], in0=score[:, :], scalar=0.2, in1=score[:, :],
                                            op0=ALU.mult, op1=ALU.max).then_inc(g_v, 1)
                    ve.wait_ge(g_v, v_done("score", t))
                    ve.tensor_tensor(spread[:, :, :], score2[:, :].unsqueeze(2).broadcast_to([T, H, T]),
                                     ident[0:T, 0:T].unsqueeze(1).broadcast_to([T, H, T]), ALU.mult).then_inc(g_v, 1)
                    ve.wait_ge(g_p, p_done("spreadB", t))
                    ve.wait_ge(g_v, v_done("apart", t))
                    for b in range(2):
                        ve.tensor_tensor(masked[:, 4 * b:4 * b + 4, :],
                                         bank[3 + b][0:T, 0:4 * T].rearrange("p (h e) -> p h e", h=4),
                                         apart[:, :].unsqueeze(1).broadcast_to([T, 4, T]), ALU.add).then_inc(g_v, 1)
                    ve.wait_ge(g_v, v_done("masked", t))
                    ve.tensor_reduce(tmax[:, :], masked[:, :, :], AX.X, ALU.max).then_inc(g_v, 1)
                    ve.wait_ge(g_v, v_done("tmax", t))
                    ve.tensor_tensor(S1[:, HD:SR], tmax[:, :], S0[:, HD:SR], ALU.max).then_inc(g_v, 1)
                    ve.wait_ge(g_v, v_done("newmax", t))
                    ve.tensor_tensor(shifted[:, 0:H], score2[:, :], S1[:, HD:SR], ALU.subtract).then_inc(g_v, 1)
                    ve.tensor_tensor(shifted[:, H:2 * H], S0[:, HD:SR], S1[:, HD:SR], ALU.subtract).then_inc(g_v, 1)
                    ve.wait_ge(g_ew, t + 1)
                    msg_blocks = msg[:, :].rearrange("p (h b) -> p h b", h=H)
                    ve.tensor_tensor(msg_blocks[:, :, 0:DH], Gs[:, 0:HD].rearrange("p (h b) -> p h b", h=H)[:, :, 0:DH],
                                     ew[:, 0:H].unsqueeze(2).broadcast_to([T, H, DH]), ALU.mult).then_inc(g_v, 1)
                    ve.tensor_copy(msg_blocks[:, :, DH:HB], ew[:, 0:H].unsqueeze(2)).then_inc(g_v, 1)
                    ve.tensor_tensor(S1[:, 0:HD].rearrange("p (h b) -> p h b", h=H),
                                     S0[:, 0:HD].rearrange("p (h b) -> p h b", h=H),
                                     ew[:, H:2 * H].unsqueeze(2).broadcast_to([T, H, HB]), ALU.mult).then_inc(g_v, 1)
                    ve.wait_ge(g_v, v_done("keep", t))
                    ve.wait_ge(g_p, p_done("sum", t))
                    ve.tensor_tensor(S1[:, 0:HD], S1[:, 0:HD], bank[5][0:T, 0:HD], ALU.add).then_inc(g_v, 1)
                    ve.wait_ge(g_scatter, 16 * t + 16)
                    ve.sem_inc(g_done, 1)


            def in_groups():
                spread_h, small, turned = bank[2:4], bank[6], bank[7]

                def onehot(gx, px, b):
                    ve.wait_ge(f_agg, VN * gx + b + 1)
                    loc = col_loc[:, bass.ds(J * gx + BT * b, BT)]
                    ve.tensor_tensor(M[:, px, BT * b:BT * (b + 1), :], iota_w[:, :].unsqueeze(1).broadcast_to([T, BT, W]),
                                     loc.unsqueeze(2).broadcast_to([T, BT, W]), ALU.is_equal).then_inc(f_M, 1)

                def product(gx, px, j):
                    n = (px + j) % 2
                    ve.wait_ge(f_relu, J * gx + j + 3)
                    ve.wait_ge(f_hd, J * gx + j + 1 + 2 * J)
                    ve.wait_ge(f_red, J * gx + j + 1)
                    ve.tensor_tensor(pr[:, n, :], er[:, n, :], spread_h[n][0:T, 0:HD], ALU.mult).then_inc(f_prod, 1)

                def add_up(gx, px, j):
                    n = (px + j) % 2
                    ve.wait_ge(f_prod, J * gx + j + 3)
                    ve.tensor_reduce(al[:, px, j, :], pr[:, n, :].rearrange("p (h b) -> p h b", h=H), AX.X,
                                     ALU.add).then_inc(f_red, 1)

                def scores(gy, py, ky):
                    ve.wait_ge(f_red, J * gy + J + 2)
                    ve.wait_ge(f_G[py], 16 * J * ky + 16 * J)
                    ve.tensor_tensor(alx[:, :, :], al[:, py, :, :], Gr[:, py, :, HD:HR], ALU.add).then_inc(f_al0, 1)
                    ve.wait_ge(f_al0, gy + 1)
                    ve.scalar_tensor_tensor(out=by_tile, in0=alx[:, :, :], scalar=0.2, in1=alx[:, :, :],
                                            op0=ALU.mult, op1=ALU.max).then_inc(f_al, 1)

                def w(ins):
                    ins.then_inc(f_w, 1)

                def before_scores(gy, py):
                    heads = end_row.rearrange("p (h k) -> p h k", k=JR)
                    w(ve.tensor_copy(c_old[:, :].unsqueeze(2), into_f.rearrange("p (h k) -> p h k", k=JR)[:, :, J:JR]))
                    w(ve.tensor_reduce(ends[:, 1:2], penT[:, py, 0:T], AX.X, ALU.min))
                    ve.wait_ge(f_w, w_done("old", gy))
                    w(ve.tensor_scalar(heads[:, :, 0:1], c_old[:, :].unsqueeze(2), part_from[0:1, bass.ds(gy, 1)],
                                       None, ALU.add))

                def running_maxima(gy, py):
                    ve.wait_ge(f_C1, gy + 1)
                    w(ve.tensor_tensor_scan(run_f[:, :], penT[:, py, 0:T], small[:, 0:T], BREAK, ALU.add, ALU.max))
                    w(ve.tensor_tensor_scan(run_b[:, ::-1], penT[:, py, T:0:-1], small[:, 0:T][:, ::-1], BREAK,
                                            ALU.add, ALU.max))
                    ve.wait_ge(f_w, w_done("bwd", gy))
                    w(ve.tensor_tensor(ends[:, 0:1], run_b[:, 0:1], penT[:, py, 0:1], ALU.add))

                def maxima_over_tiles(gy):
                    ve.wait_ge(f_copied, 3 * gy + 2)
                    w(ve.tensor_tensor_scan(into_f, any_new[:, 0:K], end_row, BREAK, ALU.add, ALU.max))
                    ve.wait_ge(f_copied, 3 * gy + 3)
                    w(ve.tensor_tensor_scan(into_b[:, 0:K][:, ::-1], any_new[:, K:0:-1], head_row[:, ::-1], BREAK,
                                            ALU.add, ALU.max))
                    ve.wait_ge(f_w, w_done("across_b", gy))
                    w(ve.tensor_tensor(c_dif[:, :].unsqueeze(2), end_row.rearrange("p (h k) -> p h k", k=JR)[:, :, 0:1],
                                       into_b[:, 0:K].rearrange("p (h k) -> p h k", k=JR)[:, :, 0:1], ALU.max))
                    ve.wait_ge(f_w, w_done("first", gy))
                    w(ve.tensor_tensor(c_dif[:, :], c_old[:, :], c_dif[:, :], ALU.subtract))
                    ve.wait_ge(f_w, w_done("dif", gy))
                    w(ve.tensor_scalar(c_dif[:, :], c_dif[:, :], 0.0, None, ALU.min))

                def node_maxima(gy, py):
                    ve.wait_ge(f_C3, gy + 1)
                    w(ve.tensor_copy(into[:, :], small[:, 126:128]))
                    ve.wait_ge(f_w, w_done("into", gy))
                    w(ve.tensor_tensor_scan(run_f[:, :], penT[:, py, 0:T], small[:, 0:T], into[:, 0:1],
                                            ALU.add, ALU.max))
                    w(ve.tensor_tensor_scan(run_b[:, ::-1], penT[:, py, T:0:-1], small[:, 0:T][:, ::-1],
                                            into[:, 1:2], ALU.add, ALU.max))
                    ve.wait_ge(f_w, w_done("again_b", gy))
                    w(ve.tensor_tensor(run_f[:, :], run_f[:, :], run_b[:, :], ALU.max))

                def shift(gy):
                    ve.wait_ge(f_C4, gy + 1)
                    w(ve.tensor_tensor(dsh[:, :].rearrange("p (j h) -> p j h", h=H), by_tile,
                                       small[0:T, 0:K].rearrange("p (h k) -> p k h", h=H)[:, 0:J, :],
                                       ALU.subtract))

                def messages(gy, py, piece):
                    ve.wait_ge(f_exp, gy + 1)
                    rows = Gr[:, py, VT * piece:VT * (piece + 1), 0:HD].rearrange("p j (h b) -> p j h b", h=H)
                    ve.tensor_tensor(rows[:, :, :, 0:DH], rows[:, :, :, 0:DH],
                                     rows[:, :, :, DH:HB].broadcast_to([T, VT, H, DH]), ALU.mult).then_inc(f_v, 1)

                def carried(gy):
                    ve.wait_ge(f_fac, gy + 1)
                    ve.tensor_scalar(c_fs[:, :], c_fac[:, :], straddle[0:1, bass.ds(gy, 1)], None,
                                     ALU.mult).then_inc(f_fs, 1)
                    ve.wait_ge(f_fs, gy + 1)
                    ve.wait_ge(f_craw, gy + 3)
                    ve.wait_ge(f_agg, VN * gy + 2 * VN)
                    ve.tensor_tensor(crow[:, :].rearrange("p (h b) -> p h b", h=H),
                                     c_raw[:, 0:HD].rearrange("p (h b) -> p h b", h=H),
                                     c_fs[:, :].unsqueeze(2).broadcast_to([1, H, HB]), ALU.mult).then_inc(f_crow, 1)

                def step(gx, px, kx, gy, py, ky, last=False):
                    if gx is not None:
                        onehot(gx, px, 0)
                    if gy is not None:
                        scores(gy, py, ky)
                        before_scores(gy, py)
                    if gx is not None:
                        onehot(gx, px, 1)
                    if gy is not None:
                        running_maxima(gy, py)
                    for j in range(J):
                        if gx is not None:
                            product(gx, px, j)
                            if j:
                                add_up(gx, px, j - 1)
                        if gy is not None and j == 1:
                            maxima_over_tiles(gy)
                        if gx is not None and j in (0, 3, 6):
                            onehot(gx, px, j // 3 + 2)
                        if gy is not None and j == 2:
                            node_maxima(gy, py)
                        if gy is not None and j == 4:
                            shift(gy)
                        if gy is not None and j in MESSAGES_AT[:VV]:
                            messages(gy, py, MESSAGES_AT.index(j))
                        if gy is not None and j == 11:
                            carried(gy)
                    if gx is not None:
                        add_up(gx, px, J - 1)

                ve.wait_ge(f_hot, START)
                ve.wait_ge(f_natd, NAT_STEPS + 2)
                step(0, 0, 0, None, None, None)
                with ve.Fori(0, G // 2 - 1) as i:
                    step(2 * i + 1, 1, i, 2 * i, 0, i)
                    step(2 * i + 2, 0, i + 1, 2 * i + 1, 1, i)
                step(G - 1, 1, G // 2 - 1, G - 2, 0, G // 2 - 1, last=True)
                step(None, None, None, G - 1, 1, G // 2 - 1)

            steps = 0

            def did(ins, s=f_natd):
                nonlocal steps
                ins.then_inc(s, 1)
                steps += 1
                ve.wait_ge(s, steps)

            ve.wait_ge(s_initst, 16)
            ve.wait_ge(f_pad, 16)
            ve.wait_ge(f_nat[0], 16)
            ve.wait_ge(f_nat[1], 16)
            did(ve.memset(nat_f[:, 0:1], -1.0))
            did(ve.memset(nat_f[:, GE + 1:GE + 2], -1.0))
            did(ve.tensor_copy(nat_f[:, 1:GE + 1], nat_dst[:, :].bitcast(I32)))
            did(ve.tensor_copy(nat_nextf[:, :], nat_next[:, :]))
            did(ve.tensor_tensor(nat_dst[:, 0:GE - 1], nat_f[:, 2:GE + 1], nat_f[:, 1:GE], ALU.subtract))
            did(ve.tensor_reduce(nat_gap[:, 0:1], nat_dst[:, 0:GE - 1], AX.X, ALU.min))
            did(ve.tensor_tensor(nat_gap[:, 1:2], nat_nextf[:, :], nat_f[:, GE:GE + 1], ALU.subtract))
            did(ve.tensor_tensor(nat_str[:, :], nat_nextf[:, :], nat_f[:, GE:GE + 1], ALU.is_equal))
            did(ve.tensor_tensor(nat_loc[:, :], nat_f[:, GE:GE + 1], nat_f[:, 1:2], ALU.subtract))
            did(ve.tensor_scalar(nat_gap[:, 2:3], nat_loc[:, :], -1.0, float(W - 1), ALU.mult, ALU.add))
            did(ve.tensor_reduce(nat_ok[:, :], nat_gap[:, 0:3], AX.X, ALU.min))
            did(ve.tensor_scalar(nat_dst[:, :], nat_f[:, 1:GE + 1], nat_f[:, 1:2], None, ALU.subtract))
            did(ve.tensor_tensor(nat_new[:, :], nat_f[:, 1:GE + 1], nat_f[:, 0:GE], ALU.not_equal))
            did(ve.memset(nat_new[:, 0:1], 0.0))
            ve.wait_ge(f_nat[2], 16)
            did(ve.tensor_copy(nat_src[:, :], nat_src[:, :].bitcast(I32)))
            assert steps == NAT_STEPS
            ve.wait_ge(f_rows, 1)
            ve.tensor_reduce(ok[:, 0:1], bank[6][0:1, 0:G], AX.X, ALU.min).then_inc(f_natd, 1)
            ve.wait_ge(f_natd, NAT_STEPS + 1)
            ve.tensor_scalar(ok_i[:, :], ok[:, 0:1], 0.0, None, ALU.is_ge).then_inc(f_ok, 1)
            ve.tensor_copy(base_i[:, :], bank[6][0:1, 128:128 + G]).then_inc(f_ok, 1)
            ve.tensor_copy(straddle[:, 1:G + 1], bank[6][0:1, 256:256 + G]).then_inc(f_ok, 1)
            ve.wait_ge(f_ok, 3)
            ve.tensor_scalar(part_from[:, :], straddle[:, :], 1.0, -BREAK, ALU.subtract,
                             ALU.mult).then_inc(f_natd, 1)
            ve.tensor_scalar(last_hot[:, :], bank[6][:, 384:384 + G], iota_p[:, :], None,
                             ALU.is_equal).then_inc(f_ok, 1)
            for n in COLUMNS_VEC:
                ve.wait_ge(f_turn, n + 1)
                kind, dest, _, scale = column_batches[n]
                ve.tensor_scalar(dest, bank[n % 4][0:T, 0:G * dest.shape[1]].rearrange("p (j g) -> p j g", g=G),
                                 scale, None, ALU.mult).then_inc(f_colv, 1)
            ve.wait_ge(f_cola, COLA)
            ve.wait_ge(f_colv, COLV)

            ve.wait_ge(f_ok, 4)
            grouped = ve.value_load(ok_i[0:1, 0:1], min_val=0, max_val=1)
            with ve.If(grouped == 1):
                in_groups()
            with ve.Else():
                any_order()

            def weight_sums(part, par, i):
                ve.wait_ge(s_st[par], 16 * i + 16)
                sums = st[:, par, :, 0:HD].rearrange("p j (h b) -> p j h b", h=H)
                ve.tensor_scalar(den[:, par, :, :].unsqueeze(3), sums[:, :, :, DH:HB], 1e-10, None,
                                 ALU.max).then_inc(s_den, 1)
                ve.wait_ge(s_den, part + 1)
                ve.reciprocal(rden[:, par, :, :], den[:, par, :, :]).then_inc(s_rden, 1)

            def add_part(part, par):
                ve.wait_ge(s_agg, part + 3)
                tiles = X[:, bass.ds(PER_LOAD * part, PER_LOAD), :]
                ve.tensor_tensor(tiles, tiles, agg[:, par, :, :], ALU.add).then_inc(s_x1, 1)
                ve.wait_ge(s_x1, part + 3)
                part_stats(part, LOADS + part)

            weight_sums(0, 0, 0)
            with ve.Fori(0, LOADS // 2 - 1) as i:
                weight_sums(2 * i + 1, 1, i)
                add_part(2 * i, 0)
                weight_sums(2 * i + 2, 0, i + 1)
                add_part(2 * i + 1, 1)
            weight_sums(LOADS - 1, 1, LOADS // 2 - 1)
            add_part(LOADS - 2, 0)
            add_part(LOADS - 1, 1)
            rsqrt_all(1)
            with ve.Fori(0, NT // 2) as i:
                for par in range(2):
                    t = 2 * i + par
                    ve.wait_ge(s_yT, t + 1)
                    normalise(xn[:, par, :], t).then_inc(s_yr, 1)
            ve.wait_ge(s_ysum, 1)
            ve.tensor_copy(ysum[:, :], bank[7][:, 0:KC]).then_inc(s_ysum, 1)

            steps = 0

            def done(ins):
                nonlocal steps
                ins.then_inc(s_r, 1)
                steps += 1
                ve.wait_ge(s_r, steps)

            def softmax(a, top_, shifted_, e, total, rtotal, w, turn_):
                done(ve.tensor_reduce(top_[:, :], a[:, :], AX.X, ALU.max))
                ve.tensor_scalar(shifted_[:, :], a[:, :], top_[:, :], None, ALU.subtract).then_inc(s_ra, 1)
                ve.wait_ge(s_ra, turn_)
                done(ve.tensor_reduce(total[:, :], e[:, :], AX.X, ALU.add))
                done(ve.reciprocal(rtotal[:, :], total[:, :]))
                done(ve.tensor_scalar(w[:, :], e[:, :], rtotal[:, :], None, ALU.mult))

            ve.wait_ge(s_rp, 1)
            done(ve.scalar_tensor_tensor(out=r["tmp"][:, :], in0=bank[2][0:1, 0:X8], scalar=1.0 / N, in1=br[:, :],
                                         op0=ALU.mult, op1=ALU.add))
            softmax(r["tmp"], rs["max"], r["logits"], r["exp"], rs["sum"], rs["rsum"], r["w"], 2)
            done(ve.tensor_scalar(r["load"][:, :], r["w"][:, :], float(N), None, ALU.mult))
            done(ve.reciprocal(r["cap"][:, :], r["load"][:, :]))
            done(ve.tensor_scalar(r["cap"][:, :], r["cap"][:, :], CAPACITY, 1.0, ALU.mult, ALU.min))
            done(ve.tensor_tensor(r["load"][:, :], r["w"][:, :], r["cap"][:, :], ALU.mult))
            softmax(r["load"], rs["max2"], r["tmp"], r["exp2"], rs["sum2"], rs["rsum2"], r["w2"], 4)
            w_i = r["w2"][:, :].unsqueeze(2).broadcast_to([1, X8, X8])
            w_j = r["w2"][:, :].unsqueeze(1).broadcast_to([1, X8, X8])
            done(ve.tensor_tensor(pair[:, :, :], w_j, w_i, ALU.is_equal))
            done(ve.tensor_tensor(pair[:, :, :], pair[:, :, :], tri8[:, :, :], ALU.mult))
            done(ve.tensor_tensor(pair2[:, :, :], w_j, w_i, ALU.is_gt))
            done(ve.tensor_tensor(pair[:, :, :], pair[:, :, :], pair2[:, :, :], ALU.add))
            done(ve.tensor_reduce(r["rank"][:, :], pair[:, :, :], AX.X, ALU.add))
            for n in range(TOP):
                done(ve.tensor_scalar(r["first"][:, :], r["rank"][:, :], float(n), None, ALU.is_equal))
                done(ve.tensor_tensor(r["second"][:, :], r["first"][:, :], r["num"][:, :], ALU.mult))
                done(ve.tensor_reduce(topi[:, n:n + 1], r["second"][:, :], AX.X, ALU.add))
                done(ve.tensor_tensor(r["second"][:, :], r["first"][:, :], r["w2"][:, :], ALU.mult))
                done(ve.tensor_reduce(top[:, n:n + 1], r["second"][:, :], AX.X, ALU.add))
            ve.tensor_copy(topi_i[:, :], topi[:, :]).then_inc(s_topi, 1)
            ve.tensor_tensor(rs["diff"][:, :], top[:, 1:2], top[:, 0:1], ALU.subtract).then_inc(s_ra, 1)
            ve.wait_ge(s_ra, 6)
            done(ve.tensor_scalar(rs["e1"][:, :], rs["e"][:, :], 1.0, None, ALU.add))
            done(ve.reciprocal(topw[:, 0:1], rs["e1"][:, :]))
            ve.tensor_tensor(topw[:, 1:2], topw[:, 0:1], rs["e"][:, :], ALU.mult).then_inc(s_w2s, 1)
            ve.wait_ge(s_rp, 2)
            ve.tensor_copy(topwB[:, :], bank[3][:, 0:TOP]).then_inc(s_w2s, 1)
            ve.wait_ge(s_w2s, 2)
            ve.wait_ge(s_wx, 8 * 16)
            for n in range(TOP):
                ve.tensor_scalar(W2[:, n, :, :], W2[:, n, :, :], topwB[:, n:n + 1], None, ALU.mult).then_inc(s_w2s, 1)
                ve.tensor_scalar(b2[:, n, :], b2[:, n, :], topw[:, n:n + 1], None, ALU.mult).then_inc(s_w2s, 1)
            ve.wait_ge(s_w2s, 6)
            ve.tensor_tensor(bias_row[:, :], b2[:, 0, :], b2[:, 1, :], ALU.add).then_inc(s_w2s, 1)
            ve.wait_ge(s_rp, 3)
            ve.tensor_copy(biasB[:, :], bank[7][0:T, 0:D]).then_inc(s_w2s, 1)
            ve.wait_ge(s_w2s, 8)

            def outputs(c, cp, first=False):
                for half in range(2):
                    normalise(yrow[:, half, :], 2 * c + half).then_inc(s_yrow, 1)
                for half in range(2):
                    ve.wait_ge(s_yrow, 4 * c + half + 1)
                    ve.tensor_tensor(yrow[:, half, :], yrow[:, half, :], biasB[:, :], ALU.add).then_inc(s_yrow, 1)
                for half in range(2):
                    t = 2 * c + half
                    ve.wait_ge(s_l2, t + 5)
                    ve.wait_ge(s_yrow, 4 * c + half + 3)
                    ve.tensor_tensor(z[:, half, :], yrow[:, half, :], bank[4 + 2 * cp + half][0:T, 0:D],
                                     ALU.add).then_inc(s_z, 1)
                    ve.wait_ge(s_z, t + 5)
                    ve.sem_inc(s_passed, 1)
                    ve.bn_stats(stats[:, half, :], z[:, half, :]).then_inc(s_zst, 1)
                    ve.wait_ge(s_zst, t + 1)
                    ve.sem_inc(s_passed, 1)
                    ve.bn_aggr(zmv[:, half, :], stats[:, half, :]).then_inc(s_zmv, 1)
                ve.wait_ge(s_zmv, 2 * c + 2)
                ve.tensor_scalar(zsd[:, :], zmv[:, :, 1:2].rearrange("p t a -> p (t a)"), EPS, None,
                                 ALU.add).then_inc(s_zvar, 1)
                ve.wait_ge(s_zsd, c + 1)
                ve.reciprocal(zr[:, :], zsd[:, :]).then_inc(s_zr, 1)
                ve.wait_ge(s_zr, c + 1)
                for half in range(2):
                    t = 2 * c + half
                    if not first:
                        ve.wait_ge(s_out[half], 16 * c)
                    ve.tensor_scalar(res[:, half, :], z[:, half, :], zmv[:, half, 0:1], zr[:, half:half + 1],
                                     ALU.subtract, ALU.mult).then_inc(s_n1, 1)
                    ve.wait_ge(s_n1, t + 1)
                    ve.tensor_tensor(res[:, half, :], res[:, half, :], gamma[:, :], ALU.mult).then_inc(s_n2, 1)
                    ve.wait_ge(s_n2, t + 1)
                    ve.tensor_tensor(res[:, half, :], res[:, half, :], beta[:, :], ALU.add).then_inc(s_n3, 1)
                    ve.wait_ge(s_n3, t + 1)
                    ve.tensor_tensor(res[:, half, :], res[:, half, :],
                                     X[:, bass.ds(t, 1), :].rearrange("p a f -> p (a f)"), ALU.add).then_inc(s_res, 1)

            outputs(0, 0, first=True)
            with ve.Fori(0, NCH // 2) as i:
                for cp in range(2):
                    outputs(2 * i + cp + 1, 1 - cp)


_INS = ["x", "src", "dst", "edge_attr_3", "L0_gnn_W", "L0_gnn_a_src", "L0_gnn_a_dst", "L0_gnn_edge_W",
        "L0_gnn_edge_b", "L0_gnn_bias", "L0_mix_W_qkv", "L0_mix_W_out", "L0_mix_b_out", "L0_ffn_Wr",
        "L0_ffn_br", "L0_ffn_W1", "L0_ffn_b1", "L0_ffn_W2", "L0_ffn_b2", "L0_ffn_gamma", "L0_ffn_beta"]


def kernel(**inputs):
    import numpy as _np
    import concourse.bacc as _bacc
    from concourse.bass_utils import run_bass_kernel_spmd as _run

    nc = _bacc.Bacc("TRN2", target_bir_lowering=False, num_devices=1)
    arrays, args = {}, []
    for name in _INS:
        a = _np.ascontiguousarray(inputs[name])
        arrays[f"in_{name}"] = a
        args.append(nc.dram_tensor(f"in_{name}", a.shape, mybir.dt.from_np(a.dtype), kind="ExternalInput").ap())
    out = nc.dram_tensor("out_0", (N, D), F32, kind="ExternalOutput").ap()
    gps_block(nc, *args, out)
    r = _run(nc, [arrays], core_ids=[0])
    return r.results[0]["out_0"]
```
